# Optimizing a Trainium2 kernel written in Bass

```python
import numpy as np
import jax
import jax.numpy as jnp

def _softmax(x, axis=-1):
    return jax.nn.softmax(x, axis=axis)

def _gelu(x):
    return jax.nn.gelu(x, approximate=True)

def _silu(x):
    return jax.nn.silu(x)

def _sigmoid(x):
    return jax.nn.sigmoid(x)

def _layernorm(x, axis=-1, eps=1e-05):
    m = jnp.mean(x, axis=axis, keepdims=True)
    v = jnp.var(x, axis=axis, keepdims=True)
    return (x - m) / jnp.sqrt(v + eps)

def _scatter_add(tgt, idx, src, axis=0):
    return tgt.at[idx].add(src)

def _segment_sum(src, seg, n):
    return jax.ops.segment_sum(src, seg, n)
kernel_name = 'mk_seq_postln_d2_jaxref_r8_7f6232'

def setup_inputs(seed: int=0):
    np.random.seed(seed)
    _w = jnp.asarray

    def _L0_attn_setup():
        import jax, jax.numpy as jnp
        import numpy as np
        D_MODEL = 512
        NUM_HEADS = 32
        NUM_KV_HEADS = 8
        HEAD_DIM = D_MODEL // NUM_HEADS
        GROUP = NUM_HEADS // NUM_KV_HEADS
        NEG = -1000000000.0
        key = jax.random.key(seed)
        ks = jax.random.split(key, 9)
        B, S = (2, 256)
        s = 0.02
        x = jax.random.normal(ks[0], (B, S, D_MODEL), dtype=jnp.float32)
        Wq = jax.random.normal(ks[1], (D_MODEL, D_MODEL), dtype=jnp.float32) * s
        bq = jax.random.normal(ks[2], (D_MODEL,), dtype=jnp.float32) * s
        Wk = jax.random.normal(ks[3], (D_MODEL, NUM_KV_HEADS * HEAD_DIM), dtype=jnp.float32) * s
        bk = jax.random.normal(ks[4], (NUM_KV_HEADS * HEAD_DIM,), dtype=jnp.float32) * s
        Wv = jax.random.normal(ks[5], (D_MODEL, NUM_KV_HEADS * HEAD_DIM), dtype=jnp.float32) * s
        bv = jax.random.normal(ks[6], (NUM_KV_HEADS * HEAD_DIM,), dtype=jnp.float32) * s
        Wo = jax.random.normal(ks[7], (D_MODEL, D_MODEL), dtype=jnp.float32) * s
        bo = jax.random.normal(ks[8], (D_MODEL,), dtype=jnp.float32) * s
        return {'x': x, 'Wq': Wq, 'bq': bq, 'Wk': Wk, 'bk': bk, 'Wv': Wv, 'bv': bv, 'Wo': Wo, 'bo': bo}
    _L0_attn_in = _L0_attn_setup()

    def _L0_ffn_setup():
        import jax, jax.numpy as jnp
        import numpy as np
        BLOCK = 32

        def _dequantize(q_scales, q_vals):
            OUT, n_blocks = q_scales.shape
            codes = q_vals.astype(jnp.float32) - 128.0
            w = q_scales[:, :, None] * codes
            return w.reshape(OUT, n_blocks * BLOCK)
        key = jax.random.key(seed)
        k1, k2, k3, k4 = jax.random.split(key, 4)
        B, S, IN, OUT = (2, 512, 512, 512)
        n_blocks = IN // BLOCK
        x = jax.random.normal(k1, (B, S, IN), dtype=jnp.float32)
        q_scales = jax.random.uniform(k2, (OUT, n_blocks), dtype=jnp.float32) * 0.05
        q_vals = jax.random.randint(k3, (OUT, n_blocks, BLOCK), 0, 32, dtype=jnp.int32)
        bias = jax.random.normal(k4, (OUT,), dtype=jnp.float32)
        return {'x': x, 'q_scales': q_scales, 'q_vals': q_vals, 'bias': bias}
    _L0_ffn_in = _L0_ffn_setup()

    def _L1_attn_setup():
        import jax, jax.numpy as jnp
        import numpy as np
        import math
        NH, NKV, D = (32, 8, 128)

        def _alibi_slopes(n):
            cp2 = 2 ** math.floor(math.log2(n))
            base = 2.0 ** (-8.0 / cp2)
            slopes = base ** np.arange(1, cp2 + 1, dtype=np.float32)
            if cp2 != n:
                extra_base = 2.0 ** (-4.0 / cp2)
                extra = extra_base ** np.arange(1, 1 + 2 * (n - cp2), 2, dtype=np.float32)
                slopes = np.concatenate([slopes, extra])
            return slopes.astype(np.float32)
        key = jax.random.key(seed)
        k1, k2, k3 = jax.random.split(key, 3)
        B, S, H = (4, 128, 512)
        qkv_out = NH * D + 2 * NKV * D
        return {'hidden_states': jax.random.normal(k1, (B, S, H), jnp.float32) * 0.02, 'w_qkv': jax.random.normal(k2, (H, qkv_out), jnp.float32) * 0.02, 'w_o': jax.random.normal(k3, (NH * D, H), jnp.float32) * 0.02}
    _L1_attn_in = _L1_attn_setup()

    def _L1_ffn_setup():
        import jax, jax.numpy as jnp
        import numpy as np
        UNITS = 512
        INPUT_SIZE = 512
        COMPRESSED = INPUT_SIZE * UNITS // 8
        key = jax.random.key(seed)
        k1, k2 = jax.random.split(key)
        x = jax.random.normal(k1, (2, 512, INPUT_SIZE), dtype=jnp.float32)
        kernel = jax.random.randint(k2, (COMPRESSED,), -1, 2, dtype=jnp.int32).astype(jnp.int8)
        return {'x': x, 'kernel': kernel}
    _L1_ffn_in = _L1_ffn_setup()
    _d = {'L0_attn_x': _L0_attn_in['x'], 'L0_attn_Wq': _L0_attn_in['Wq'], 'L0_attn_bq': _L0_attn_in['bq'], 'L0_attn_Wk': _L0_attn_in['Wk'], 'L0_attn_bk': _L0_attn_in['bk'], 'L0_attn_Wv': _L0_attn_in['Wv'], 'L0_attn_bv': _L0_attn_in['bv'], 'L0_attn_Wo': _L0_attn_in['Wo'], 'L0_attn_bo': _L0_attn_in['bo'], 'L0_ffn_q_scales': _L0_ffn_in['q_scales'], 'L0_ffn_q_vals': _L0_ffn_in['q_vals'], 'L0_ffn_bias': _L0_ffn_in['bias'], 'L1_attn_w_qkv': _L1_attn_in['w_qkv'], 'L1_attn_w_o': _L1_attn_in['w_o'], 'L1_ffn_kernel': _L1_ffn_in['kernel']}
    _x0 = _d['L0_attn_x']
    _d['L0_attn_x'] = jax.random.normal(jax.random.fold_in(jax.random.key(seed), 1), (4, 256, 512), dtype=_x0.dtype)
    del _x0
    return _d

def reference(L0_attn_x, L0_attn_Wq, L0_attn_bq, L0_attn_Wk, L0_attn_bk, L0_attn_Wv, L0_attn_bv, L0_attn_Wo, L0_attn_bo, L0_ffn_q_scales, L0_ffn_q_vals, L0_ffn_bias, L1_attn_w_qkv, L1_attn_w_o, L1_ffn_kernel):

    def _L0_attn_ref(x, Wq, bq, Wk, bk, Wv, bv, Wo, bo):
        import jax, jax.numpy as jnp
        import numpy as np
        D_MODEL = 512
        NUM_HEADS = 32
        NUM_KV_HEADS = 8
        HEAD_DIM = D_MODEL // NUM_HEADS
        GROUP = NUM_HEADS // NUM_KV_HEADS
        NEG = -1000000000.0
        B, S, _ = x.shape
        q = (x @ Wq + bq).reshape(B, S, NUM_HEADS, HEAD_DIM).transpose(0, 2, 1, 3)
        k = (x @ Wk + bk).reshape(B, S, NUM_KV_HEADS, HEAD_DIM).transpose(0, 2, 1, 3)
        v = (x @ Wv + bv).reshape(B, S, NUM_KV_HEADS, HEAD_DIM).transpose(0, 2, 1, 3)
        k = jnp.repeat(k, GROUP, axis=1)
        v = jnp.repeat(v, GROUP, axis=1)
        scores = jnp.einsum('bhqd,bhkd->bhqk', q, k) / jnp.sqrt(jnp.asarray(HEAD_DIM, dtype=jnp.float32))
        causal = jnp.tril(jnp.ones((S, S), dtype=bool))
        scores = jnp.where(causal, scores, NEG)
        p = jax.nn.softmax(scores, axis=-1)
        out = jnp.einsum('bhqk,bhkd->bhqd', p, v)
        out = out.transpose(0, 2, 1, 3).reshape(B, S, D_MODEL)
        return out @ Wo + bo

    def _L0_ffn_ref(x, q_scales, q_vals, bias):
        import jax, jax.numpy as jnp
        import numpy as np
        BLOCK = 32

        def _dequantize(q_scales, q_vals):
            OUT, n_blocks = q_scales.shape
            codes = q_vals.astype(jnp.float32) - 128.0
            w = q_scales[:, :, None] * codes
            return w.reshape(OUT, n_blocks * BLOCK)
        W = _dequantize(q_scales, q_vals)
        out = jnp.einsum('bsi,oi->bso', x, W) + bias
        return out

    def _L1_attn_ref(hidden_states, w_qkv, w_o):
        import jax, jax.numpy as jnp
        import numpy as np
        import math
        NH, NKV, D = (32, 8, 128)

        def _alibi_slopes(n):
            cp2 = 2 ** math.floor(math.log2(n))
            base = 2.0 ** (-8.0 / cp2)
            slopes = base ** np.arange(1, cp2 + 1, dtype=np.float32)
            if cp2 != n:
                extra_base = 2.0 ** (-4.0 / cp2)
                extra = extra_base ** np.arange(1, 1 + 2 * (n - cp2), 2, dtype=np.float32)
                slopes = np.concatenate([slopes, extra])
            return slopes.astype(np.float32)
        B, S, H = hidden_states.shape
        G = NH // NKV
        scale = D ** (-0.5)
        qkv = hidden_states @ w_qkv
        q = qkv[..., :NH * D].reshape(B, S, NKV, G, D)
        k = qkv[..., NH * D:NH * D + NKV * D].reshape(B, S, NKV, D)
        v = qkv[..., NH * D + NKV * D:].reshape(B, S, NKV, D)
        scores = jnp.einsum('bqhgd,bkhd->bhgqk', q, k) * scale
        slopes = jnp.asarray(_alibi_slopes(NH)).reshape(NKV, G)
        pos = jnp.arange(S)
        rel = pos[:, None] - pos[None, :]
        sqrt_dist = jnp.sqrt(jnp.maximum(rel, 0).astype(jnp.float32))
        bias = -slopes[:, :, None, None] * sqrt_dist
        bias = jnp.where(rel[None, None] >= 0, bias, -jnp.inf)
        attn = jax.nn.softmax(scores + bias[None], axis=-1)
        out = jnp.einsum('bhgqk,bkhd->bqhgd', attn, v).reshape(B, S, NH * D)
        return out @ w_o

    def _L1_ffn_ref(x, kernel):
        import jax, jax.numpy as jnp
        import numpy as np
        UNITS = 512
        INPUT_SIZE = 512
        COMPRESSED = INPUT_SIZE * UNITS // 8
        w = jnp.broadcast_to(kernel[None, :], (8, COMPRESSED))
        w = w.astype(jnp.float32).reshape(INPUT_SIZE, UNITS)
        return x @ w
    x = L0_attn_x
    x = _layernorm(x + _L0_attn_ref(x, L0_attn_Wq, L0_attn_bq, L0_attn_Wk, L0_attn_bk, L0_attn_Wv, L0_attn_bv, L0_attn_Wo, L0_attn_bo), axis=-1)
    x = _layernorm(x + _L0_ffn_ref(x, L0_ffn_q_scales, L0_ffn_q_vals, L0_ffn_bias), axis=-1)
    x = _layernorm(x + _L1_attn_ref(x, L1_attn_w_qkv, L1_attn_w_o), axis=-1)
    x = _layernorm(x + _L1_ffn_ref(x, L1_ffn_kernel), axis=-1)
    return x

_drawn_inputs = setup_inputs


def setup_inputs(seed=0):
    import zlib

    import numpy as np

    out = dict(_drawn_inputs(seed))
    spreads = {}
    factors = {'L0_attn_Wq': 8.0,
     'L0_attn_bq': 8.0,
     'L0_attn_Wk': 8.0,
     'L0_attn_bk': 8.0,
     'L0_attn_bv': 4.306}
    for name, (base, spread) in spreads.items():
        noise = np.random.default_rng([zlib.crc32(name.encode()), seed]).standard_normal(out[name].shape)
        drawn = base * np.exp(spread * noise) if base else spread * noise
        out[name] = jnp.asarray(drawn.astype(out[name].dtype))
    for name, factor in factors.items():
        out[name] = (out[name] * factor).astype(out[name].dtype)
    return out
```

```python
from contextlib import ExitStack

import concourse.bass as bass
from concourse import mybir

F32 = mybir.dt.float32
F32R = mybir.dt.float32r
I32 = mybir.dt.int32
I8 = mybir.dt.int8
ALU = mybir.AluOpType
ACT = mybir.ActivationFunctionType
AX = mybir.AxisListType

P = 128
B, S, DM = 4, 256, 512
TOK = B * S
TILES = TOK // P
KC = DM // P
HALF = TOK // 2
NKV, GRP = 8, 4
HD0 = 16
HD1 = 128
EPS = 1e-5
SCALE0 = 0.25
SCALE1 = float(HD1) ** -0.5
QCOLS = NKV * GRP * HD1
KVC = NKV * HD1
SP0 = GRP * P
SPC = SP0 + GRP * S
FLOOR = -3.0e38


def hold(eng, semaphore, count):
    eng.wait_ge(semaphore, count)
    eng.nop(nofuse=True)


class Ring:

    def __init__(self, banks, full, free):
        self.banks, self.full, self.free = banks, full, free

    def bank(self, n):
        return self.banks[n % len(self.banks)]

    def wait_free(self, eng, n, loop=0):
        turn = n // len(self.banks)
        if turn or not at_start(loop):
            eng.wait_ge(self.free[n % len(self.banks)], turn + loop)

    def wait_full(self, eng, n, loop=0):
        eng.wait_ge(self.full[n % len(self.banks)], n // len(self.banks) + 1 + loop)

    def wait_done(self, eng, uses):
        for b in range(len(self.banks)):
            eng.wait_ge(self.free[b], (uses - b + len(self.banks) - 1) // len(self.banks))

    def filled(self, ins, n):
        ins.then_inc(self.full[n % len(self.banks)], 1)

    def freed(self, ins, n):
        ins.then_inc(self.free[n % len(self.banks)], 1)


def steps(rows_):
    use = norm = 0
    uses, norms, out = {}, {}, []
    for what, t, takes in rows_:
        mine = number = None
        if what in USES:
            mine = uses[what, t] = use
            use += 1
        if what.startswith("norm"):
            number = norms[what[-1], t] = norm
            norm += 1
        if what.startswith("scale"):
            number = norms[what[-1], t]
        out.append((what, t, mine, number, uses.get((takes, t))))
    return out, use


USES = ("proj", "turn1", "linear", "turn2", "turn", "codes")


def pipeline(slots, order):
    return [(what, s - lag, takes) for s in slots for what, lag, takes in order if 0 <= s - lag < TILES]


POST, POST_USES = steps(pipeline(range(-1, TILES + 5), [
    ("proj", 0, None), ("attn", -1, None), ("turn1", 2, None), ("linear", 3, "turn1"), ("turn2", 5, None),
    ("norm1", 0, "proj"), ("norm2", 3, "linear"), ("scale1", 0, None), ("scale2", 3, None)]))
TAIL, TAIL_USES = steps(pipeline(range(TILES + 2), [
    ("turn", 1, None), ("codes", 1, "turn"), ("norm3", 0, None), ("norm4", 2, "codes"),
    ("scale3", 0, None), ("scale4", 2, None)]))
NORMS = 2 * TILES


def scaled(plan, base=0):
    return {(what, t): base + n + 1 for n, (what, t) in
            enumerate([(w, t) for w, t, _, _, _ in plan if w.startswith("scale")])}


SCALED = {**scaled(POST), **scaled(TAIL, NORMS)}


def at_start(n):
    return isinstance(n, int) and n == 0


def two_layers(nc, x_in, wq0, bq0, wk0, bk0, wv0, bv0, wo0, bo0, q_scales, q_vals, ffn_bias,
               w_qkv, w_o, codes, ident_in, mask_in, dist_in, slopes_in, out):
    root = ExitStack()
    with root:
        def sb(name, shape, dt=F32, scope=root):
            return scope.enter_context(nc.sbuf_tensor(name, shape, dt))

        def sem(name):
            return root.enter_context(nc.semaphore(name))

        X = sb("X", [P, TILES, DM])
        XTh = sb("XTh", [P, KC, TOK], F32R)
        XTl = sb("XTl", [P, KC, TOK], F32R)
        attn = XTh[:].bitcast(F32)
        ident = sb("ident", [P, P])
        mask = sb("mask", [P, 3 * P])
        dist = sb("dist", [P, 3 * P])
        slopes = sb("slopes", [P, NKV * GRP])
        stats = sb("stats", [P, 4, 6])
        moments = sb("moments", [P, 4, 2])
        std = sb("std", [P, 4])
        rstd = sb("rstd", [P, 4])
        eps = sb("eps", [P, 1])
        rowmax = sb("rowmax", [P, 2, 2 * GRP])
        negmax = sb("negmax", [P, 2, 2 * GRP])
        rowsum = sb("rowsum", [P, 2, 2 * GRP])
        rowrec = sb("rowrec", [P, 2, 2 * GRP])
        bo_b = sb("bo_b", [P, DM])
        fb_b = sb("fb_b", [P, DM])
        bq_t = sb("bq_t", [P, KC])
        bq_s = sb("bq_s", [P, KC])
        bk_t = sb("bk_t", [P, 1])
        bv_t = sb("bv_t", [P, 1])
        keep = ExitStack()
        WFh = sb("WFh", [P, KC, DM], F32R, keep)
        WFl = sb("WFl", [P, KC, DM], F32R, keep)
        early = ExitStack()
        Qh = sb("Qh", [P, KC, TOK], F32R, early)
        Ql = sb("Ql", [P, KC, TOK], F32R, early)
        Kh = sb("Kh", [P, TOK], F32R, early)
        Kl = sb("Kl", [P, TOK], F32R, early)
        Vf = sb("Vf", [P, TILES, P], F32, early)
        QS = sb("QS", [P, GRP, TOK], F32R, early)
        KS = sb("KS", [P, TOK], F32R, early)
        proj = ExitStack()
        W0raw = sb("W0raw", [P, KC, 6 * P], F32, proj)
        W0h = sb("W0h", [P, KC, 6 * P], F32R, proj)
        W0l = sb("W0l", [P, KC, 6 * P], F32R, proj)
        QKf = sb("QKf", [P, 2, HALF], F32, proj)
        VTf = sb("VTf", [P, TOK], F32, proj)
        qv = sb("qv", [P, KC, DM], I32, proj)
        qw = sb("qw", [P, KC, DM], F32, proj)
        qs = sb("qs", [P, KC, 16], F32, proj)
        proj.close()
        att = ExitStack()
        Sb0 = [sb(f"Sb0_{i}", [P, SPC], F32, att) for i in range(2)]
        PT0 = sb("PT0", [P, 3, 4 * P], F32, att)
        Of = sb("Of", [HD0, GRP, TOK], F32, att)
        VS = sb("VS", [P, 2, TILES, HD0], F32, att)
        Wo0raw = sb("Wo0raw", [P, KC, DM], F32, att)
        Wo0h = sb("Wo0h", [P, KC, DM], F32R, att)
        Wo0l = sb("Wo0l", [P, KC, DM], F32R, att)
        att.close()
        early.close()
        post = ExitStack()
        Y = sb("Y", [P, 2, DM], F32, post)
        Z = sb("Z", [P, TILES, DM], F32, post)
        ATh = sb("ATh", [P, 2, KC, P], F32R, post)
        ATl = sb("ATl", [P, 2, KC, P], F32R, post)
        X1h = sb("X1h", [P, 2, KC, P], F32R, post)
        X1l = sb("X1l", [P, 2, KC, P], F32R, post)
        post.close()
        keep.close()
        QT = sb("QT", [P, GRP, TOK])
        KT = sb("KT", [P, TOK])
        VT = sb("VT", [P, TOK])
        Sb1 = [sb(f"Sb1_{i}", [P, SPC]) for i in range(2)]
        PTh1 = sb("PTh1", [P, 3, 4 * P], F32R)
        PTl1 = sb("PTl1", [P, 3, 4 * P], F32R)
        OTh = sb("OTh", [P, 2, GRP, P], F32R)
        OTl = sb("OTl", [P, 2, GRP, P], F32R)
        W1raw = sb("W1raw", [P, KC, 6 * P])
        W1h = sb("W1h", [P, KC, 6 * P], F32R)
        W1l = sb("W1l", [P, KC, 6 * P], F32R)
        Woraw = sb("Woraw", [P, GRP, DM])
        Vh = sb("Vh", [P, TILES, P], F32R)
        Vl = sb("Vl", [P, TILES, P], F32R)
        tab = sb("tab", [P, GRP, 3 * P])
        Woh = sb("Woh", [P, GRP, DM], F32R)
        Wol = sb("Wol", [P, GRP, DM], F32R)
        codes_i = sb("codes_i", [64, DM // 4], I32)
        codes_f = sb("codes_f", [64, DM], F32R)
        fold = sb("fold", [P, 2, 64])
        FTh = sb("FTh", [64, 2, P], F32R)
        FTl = sb("FTl", [64, 2, P], F32R)

        banks = [root.enter_context(nc.psum_tensor(f"bank{i}", [P, 512], F32)) for i in range(8)]

        def ring(name, ids):
            return Ring([banks[i] for i in ids], [sem(f"{name}_full{i}") for i in ids],
                        [sem(f"{name}_free{i}") for i in ids])

        ringA = ring("proj0", [0, 1, 2, 3])
        ringO0 = ring("pv0", [5, 6])
        ringC = ring("post", [0, 1, 2, 3])
        ringL = ring("l1", [5, 6, 7])
        ringF = ring("tail", [0, 1, 2, 3])

        x_loaded = [sem(f"x_loaded{i}") for i in range(4)]
        w0_loaded = sem("w0_loaded")
        ident_loaded = sem("ident_loaded")
        consts_loaded = sem("consts_loaded")
        biases_loaded = sem("biases_loaded")
        q_loaded = sem("q_loaded")
        wo0_loaded = sem("wo0_loaded")
        post_loaded = sem("post_loaded")
        w1_loaded = sem("w1_loaded")
        wo1_loaded = sem("wo1_loaded")
        codes_loaded = sem("codes_loaded")
        stored = sem("stored")
        w0h_ready = sem("w0h_ready")
        w0l_ready = sem("w0l_ready")
        xh_ready = sem("xh_ready")
        xl_ready = sem("xl_ready")
        bqs_ready = sem("bqs_ready")
        qk_biased = sem("qk_biased")
        qkh_ready = sem("qkh_ready")
        qkl_ready = sem("qkl_ready")
        vt_ready = sem("vt_ready")
        vf_ready = sem("vf_ready")
        deq_step = sem("deq_step")
        wfh_ready = sem("wfh_ready")
        wfl_ready = sem("wfl_ready")
        eps_ready = sem("eps_ready")
        qs_loaded = [sem("qs_loaded0"), sem("qs_loaded1")]
        vs_ready = sem("vs_ready")
        out_moved = sem("out_moved")
        pt0_act = sem("pt0_act")
        pt0_dve = sem("pt0_dve")
        rec_ready = sem("rec_ready")
        scale_step = sem("scale_step")
        wo0h_ready = sem("wo0h_ready")
        wo0_ready = sem("wo0_ready")

        def softmax_sems(name):
            return {k: sem(f"{name}_{k}") for k in
                    ("scores_ready", "scores_read", "max_ready", "negmax_ready", "exp_done", "rec_ready",
                     "norm_done", "pt_full", "pth_ready", "ptl_ready")}
        A0, A1 = softmax_sems("a0"), softmax_sems("a1")
        ath_ready = sem("ath_ready")
        atl_ready = sem("atl_ready")
        y_ready = sem("y_ready")
        ln_dve = sem("ln_dve")
        std_ready = sem("std_ready")
        xn_ready = sem("xn_ready")
        x1h_ready = sem("x1h_ready")
        x1l_ready = sem("x1l_ready")
        x2h_ready = sem("x2h_ready")
        x2l_ready = sem("x2l_ready")
        bias_added = sem("bias_added")
        z_ready = sem("z_ready")
        w1_split = sem("w1_split")
        w1_step = sem("w1_step")
        wo1_split = sem("wo1_split")
        wo1_step = sem("wo1_step")
        tab_ready = sem("tab_ready")
        kt_ready = sem("kt_ready")
        vt1_ready = sem("vt1_ready")
        vh_ready = sem("vh_ready")
        vl_ready = sem("vl_ready")
        qt_ready = sem("qt_ready")
        oth_ready = sem("oth_ready")
        otl_ready = sem("otl_ready")
        x_added = sem("x_added")
        codes_ready = sem("codes_ready")
        fold_ready = sem("fold_ready")
        fh_ready = sem("fh_ready")
        fl_ready = sem("fl_ready")

        x_v = x_in.rearrange("b (t p) d -> p (b t) d", p=P)
        out_v = out.rearrange("b (t p) d -> p (b t) d", p=P)

        def rows(w):
            return w.rearrange("(c p) n -> p c n", p=P)

        wqkv_v = rows(w_qkv)
        wo_v = w_o.rearrange("(h p) n -> p h n", p=P)

        def sb_q0(t):
            return t[:, 0:SP0].rearrange("p (h k) -> p h k", h=GRP)

        def sb_q1(t):
            return t[:, SP0:SPC].rearrange("p (h k) -> p h k", h=GRP)

        def score_slices(h):
            return [(0, h * P, h * P, P), (1 + h // 2, (h % 2) * S, SP0 + h * S, S)]

        def bank_slices(bank):
            qt = 0 if bank == 0 else 1
            heads = range(GRP) if bank == 0 else range(2 * bank - 2, 2 * bank)
            return heads, qt, slice(qt * GRP + heads[0], qt * GRP + heads[-1] + 1)

        def softmax_max(v, A, n, k, buf, table_of, scale, only=range(3)):
            i = k % 2
            for bank in only:
                hold(v, A["scores_ready"], 3 * (n + k) + bank + 1)
                heads, qt, cols = bank_slices(bank)
                for h in heads:
                    _, c0, s0, w = score_slices(h)[qt]
                    last = nc.vector.tensor_tensor_reduce(
                        out=buf[i][:, s0:s0 + w], in0=banks[bank][:, c0:c0 + w], in1=table_of(h, qt), scale=1.0,
                        scalar=FLOOR, op0=ALU.add, op1=ALU.max,
                        accum_out=rowmax[:, i, qt * GRP + h:qt * GRP + h + 1])
                last.then_inc(A["scores_read"], 1)
                v.wait_ge(A["scores_read"], 3 * (n + k) + bank + 1)
                nc.vector.tensor_scalar(negmax[:, i, cols], rowmax[:, i, cols], -scale, None,
                                        ALU.mult).then_inc(A["negmax_ready"], 1)

        def softmax_exp(act, A, n, k, bank, buf, scale):
            i = k % 2
            act.wait_ge(A["negmax_ready"], 3 * (n + k) + bank + 1)
            heads, qt, _ = bank_slices(bank)
            for h in heads:
                _, _, s0, w = score_slices(h)[qt]
                j = qt * GRP + h
                last = nc.scalar.activation(buf[i][:, s0:s0 + w], buf[i][:, s0:s0 + w], ACT.Exp,
                                            bias=negmax[:, i, j:j + 1], scale=scale,
                                            accum_out=rowsum[:, i, j:j + 1])
            last.then_inc(A["exp_done"], 1)

        def softmax_rec(v, A, n, k, bank):
            i = k % 2
            _, _, cols = bank_slices(bank)
            v.wait_ge(A["exp_done"], 3 * (n + k) + bank + 1)
            nc.vector.reciprocal(rowrec[:, i, cols], rowsum[:, i, cols]).then_inc(A["rec_ready"], 1)

        def softmax_norm(g, A, n, k, buf):
            i = k % 2
            for bank in range(3):
                hold(g, A["rec_ready"], 3 * (n + k) + bank + 1)
                heads, qt, cols = bank_slices(bank)
                w = P if qt == 0 else S
                view = (sb_q1 if qt else sb_q0)(buf[i])[:, heads[0]:heads[-1] + 1, :]
                r = rowrec[:, i, cols].unsqueeze(2).broadcast_to([P, len(heads), w])
                nc.gpsimd.tensor_tensor(view, view, r, ALU.mult).then_inc(A["norm_done"], 1)

        def transpose_probs(pe, A, n, k, part, buf):
            if part < 2:
                pe.wait_ge(A["norm_done"], 3 * (n + k) + (3 if part else 1))
            j = 3 * k + part
            if A is A0 and part == 2:
                pe.wait_ge(pt0_act, n + k + 1)
            elif not at_start(n) or k or part == 2:
                if A is A0:
                    pe.wait_ge(pt0_dve, 2 * (n + k) + part - 1)
                else:
                    pe.wait_ge(A["ptl_ready"], 3 * n + j - 1)
            for h in range(GRP):
                _, _, s0, _ = score_slices(h)[0 if part == 0 else 1]
                s0 += P * (part == 2)
                last = nc.tensor.transpose(banks[3 + j % 2][:, h * P:(h + 1) * P],
                                           buf[k % 2][:, s0:s0 + P], ident[:])
            last.then_inc(A["pt_full"], 1)

        def split_hi(act, A, n, k, part, PTh):
            j = 3 * k + part
            act.wait_ge(A["pt_full"], 3 * n + j + 1)
            nc.scalar.activation(PTh[:, part, :], banks[3 + j % 2][:], ACT.Copy).then_inc(A["pth_ready"], 1)

        def split_lo(v, A, n, k, part, PTh, PTl):
            j = 3 * k + part
            v.wait_ge(A["pth_ready"], 3 * n + j + 1)
            nc.vector.tensor_tensor(PTl[:, part, :], banks[3 + j % 2][:], PTh[:, part, :].bitcast(F32),
                                    ALU.subtract).then_inc(A["ptl_ready"], 1)

        block = root.enter_context(nc.Block())

        UX, UK, UV, UQ, UVT, UW, UA_END = 0, 8, 10, 12, 20, 22, 26
        GP = NKV // 2
        UNITS = 2 * B
        RV, RK, RVT, RQ, RP = 0, 2, 4, 6, 14
        RPV = [[RP, RP + 1]] + [[RP + 4 * b - 1, RP + 4 * b + 1] for b in range(1, B)]
        ROP = [[RP + 4 * b + 2, RP + 4 * b + 4] for b in range(B - 1)] + [[RP + 4 * B - 2, RP + 4 * B - 1]]
        RL = 30
        TURNS = RL // 3

        @block.sync
        def _(sp):
            for i in range(4):
                sp.dma_start(X[:, 2 * i:2 * i + 2, :], x_v[:, 2 * i:2 * i + 2, :]).then_inc(x_loaded[i], 16)
                if i == 0:
                    sp.dma_start(ident[:], ident_in).then_inc(ident_loaded, 16)
                    sp.dma_start(W0raw[:, :, 4 * P:5 * P], rows(wk0)).then_inc(w0_loaded, 16)
                    sp.dma_start(W0raw[:, :, 5 * P:6 * P], rows(wv0)).then_inc(w0_loaded, 16)
                    sp.dma_start(W0raw[:, :, 0:4 * P], rows(wq0)).then_inc(w0_loaded, 16)
            sp.dma_start(bq_t[:], bq0.rearrange("(c p) -> p c", p=P), allow_slow_non_contiguous=True).then_inc(biases_loaded, 16)
            sp.dma_start(bk_t[:], bk0.rearrange("(p a) -> p a", a=1), allow_slow_non_contiguous=True).then_inc(biases_loaded, 16)
            sp.dma_start(bv_t[:], bv0.rearrange("(p a) -> p a", a=1), allow_slow_non_contiguous=True).then_inc(biases_loaded, 16)
            sp.dma_start(qv[:], q_vals.rearrange("(c p) b k -> p c (b k)", p=P)).then_inc(q_loaded, 16)
            sp.dma_start(qs[:], q_scales.rearrange("(c p) b -> p c b", p=P)).then_inc(q_loaded, 16)
            sp.dma_start(bo_b[:], bo0.rearrange("(a n) -> a n", a=1).partition_broadcast(P)
                         .rearrange("p a n -> p (a n)")).then_inc(post_loaded, 16)
            sp.dma_start(fb_b[:], ffn_bias.rearrange("(a n) -> a n", a=1).partition_broadcast(P)
                         .rearrange("p a n -> p (a n)")).then_inc(post_loaded, 16)
            sp.dma_start(mask[:], mask_in).then_inc(consts_loaded, 16)
            sp.dma_start(dist[:], dist_in).then_inc(consts_loaded, 16)
            sp.dma_start(slopes[:], slopes_in).then_inc(consts_loaded, 16)

            def stack(pair, par, prefetch=True):
                base, src = 64 * par, 64 * par
                for h in range(GRP):
                    for r, q in enumerate((Qh, Qh, Ql, Ql)):
                        sp.dma_start(QS[base + 16 * r:base + 16 * (r + 1), h, :].bitcast(F32),
                                     q[src + 16 * h:src + 16 * (h + 1), bass.ds(pair, 1), :]
                                     .rearrange("p a t -> p (a t)").bitcast(F32)).then_inc(qs_loaded[par], 16)

            def stack_k(g, par):
                base = 64 * par
                for r, k in enumerate((Kh, Kl, Kh, Kl)):
                    sp.dma_start(KS[base + 16 * r:base + 16 * (r + 1), :].bitcast(F32),
                                 k[16 * g:16 * (g + 1), :].bitcast(F32)).then_inc(qs_loaded[par], 16)

            for par in range(2):
                sp.wait_ge(qkl_ready, 4)
                stack(0, par)
                stack_k(par, par)

            def move_out(pair, par):
                for h in range(GRP):
                    d0 = 64 * par + 16 * h
                    sp.dma_start(attn[d0:d0 + 16, pair, :], Of[:, h, :]).then_inc(out_moved, 16)

            for pair in range(GP):
                for par in range(2):
                    n = UNITS * pair + B * par
                    if pair + 1 < GP:
                        sp.wait_ge(A0["scores_read"], 3 * (n + B))
                        if pair == 0:
                            sp.wait_ge(qkl_ready, 10)
                        stack(pair + 1, par)
                        stack_k(2 * (pair + 1) + par, par)
                    if pair == 0 and par == 0:
                        sp.wait_ge(vf_ready, 2)
                        sp.wait_ge(wfl_ready, KC)
                        sp.dma_start(Wo0raw[:], rows(wo0)).then_inc(wo0_loaded, 16)
                    for bank in range(2):
                        sp.wait_ge(ringO0.free[bank], n + B)
                    move_out(pair, par)
            def load_w1(g):
                sp.dma_start(W1raw[:, :, 0:4 * P], wqkv_v[:, :, bass.ds(g * 4 * P, 4 * P)]).then_inc(w1_loaded, 16)
                sp.dma_start(W1raw[:, :, 4 * P:5 * P],
                             wqkv_v[:, :, bass.ds(g * P + QCOLS, P)]).then_inc(w1_loaded, 16)
                sp.dma_start(W1raw[:, :, 5 * P:6 * P],
                             wqkv_v[:, :, bass.ds(g * P + QCOLS + KVC, P)]).then_inc(w1_loaded, 16)

            load_w1(0)
            ringC.wait_done(sp, POST_USES)
            sp.dma_start(codes_i[:], codes.rearrange("(r n) -> r n", n=DM // 4)).then_inc(codes_loaded, 16)

            sp.dma_start(Woraw[:], wo_v[:, 0:GRP, :]).then_inc(wo1_loaded, 16)
            sp.wait_ge(w1_split, 1)
            load_w1(1)
            with sp.Fori(1, NKV - 1) as g:
                sp.wait_ge(wo1_split, g)
                sp.dma_start(Woraw[:], wo_v[:, bass.ds(g * GRP, GRP), :]).then_inc(wo1_loaded, 16)
                sp.wait_ge(w1_split, g + 1)
                load_w1(g + 1)
            sp.wait_ge(wo1_split, NKV - 1)
            sp.dma_start(Woraw[:], wo_v[:, (NKV - 1) * GRP:NKV * GRP, :]).then_inc(wo1_loaded, 16)

            for t in range(TILES):
                sp.wait_ge(xn_ready, SCALED["scale4", t])
                sp.dma_start(out_v[:, t, :], X[:, t, :]).then_inc(stored, 16)
            sp.wait_ge(stored, 16 * TILES)

        @block.gpsimd
        def _(pool):
            nc.gpsimd.memset(eps[:], EPS).then_inc(eps_ready, 1)

            def stage_v(pair, par):
                nc.gpsimd.tensor_copy(VS[:, par], Vf[:, :, bass.ds((pair * 2 + par) * HD0, HD0)])\
                  .then_inc(vs_ready, 1)

            hold(pool, vf_ready, 2)
            pool.wait_ge(post_loaded, 32)
            hold(pool, wfl_ready, KC)
            stage_v(0, 0)
            stage_v(0, 1)

            def attention_pair(pair, last):
                n = UNITS * pair
                for k in range(UNITS):
                    softmax_norm(pool, A0, n, k, Sb0)
                    if at_start(pair):
                        nc.gpsimd.tensor_tensor(X[:, k, :], X[:, k, :], bo_b[:], ALU.add).then_inc(bias_added, 1)
                    if last and k < KC:
                        if k == 0:
                            pool.wait_ge(wo0_loaded, 16)
                        nc.gpsimd.tensor_copy(Wo0h[:, k, :], Wo0raw[:, k, :]).then_inc(wo0h_ready, 1)
                        pool.wait_ge(wo0h_ready, k + 1)
                        nc.gpsimd.tensor_tensor(Wo0l[:, k, :], Wo0raw[:, k, :], Wo0h[:, k, :].bitcast(F32),
                                                ALU.subtract).then_inc(wo0_ready, 1)
                    if k % B == 0 and k and not last:
                        hold(pool, ringO0.free[1], n + k)
                        stage_v(pair + 1, k // B - 1)
                if not last:
                    hold(pool, ringO0.free[1], n + UNITS)
                    stage_v(pair + 1, 1)

            attention_pair(0, False)
            with pool.Fori(1, GP - 1) as pair:
                attention_pair(pair, False)
            attention_pair(GP - 1, True)

            def split_w1(g, c0, c1, first, count):
                if first:
                    hold(pool, w1_loaded, (g + 1) * 48)
                nc.gpsimd.tensor_copy(W1h[:, c0:c1, :], W1raw[:, c0:c1, :]).then_inc(w1_step, 1)
                hold(pool, w1_step, g * 4 + count)
                last = nc.gpsimd.tensor_tensor(W1l[:, c0:c1, :], W1raw[:, c0:c1, :],
                                               W1h[:, c0:c1, :].bitcast(F32), ALU.subtract)
                if c1 == KC:
                    last.then_inc(w1_split, 1)

            chunk = 0
            for what, t, use, i, before in POST:
                if what == "scale1":
                    pool.wait_ge(xn_ready, SCALED[what, t])
                    nc.gpsimd.tensor_tensor(Z[:, t, :], X[:, t, :], fb_b[:], ALU.add).then_inc(z_ready, 1)
                    if chunk < KC:
                        split_w1(0, chunk, chunk + 1, chunk == 0, chunk + 1)
                        chunk += 1

            def group(g, last):
                n = B * g
                hold(pool, wo1_loaded, (g + 1) * 16)
                if not at_start(g):
                    hold(pool, x_added, g * 2 * B)
                nc.gpsimd.tensor_copy(Woh[:], Woraw[:]).then_inc(wo1_step, 1)
                hold(pool, wo1_step, g + 1)
                nc.gpsimd.tensor_tensor(Wol[:], Woraw[:], Woh[:].bitcast(F32), ALU.subtract).then_inc(wo1_split, 1)
                def split_chunks(*chunks):
                    if not last:
                        for c in chunks:
                            split_w1(g + 1, c, c + 1, c == 0, c + 1)

                softmax_norm(pool, A1, n, 0, Sb1)
                softmax_norm(pool, A1, n, 1, Sb1)
                if not last:
                    hold(pool, qt_ready, 8 * g + 8)
                split_chunks(0)
                softmax_norm(pool, A1, n, 2, Sb1)
                split_chunks(1, 2)
                softmax_norm(pool, A1, n, 3, Sb1)
                split_chunks(3)

            ringC.wait_done(pool, POST_USES)
            group(0, False)
            with pool.Fori(1, NKV - 1) as g:
                group(g, False)
            group(NKV - 1, True)
            hold(pool, codes_loaded, 16)
            nc.gpsimd.tensor_copy(codes_f[:], codes_i[:].bitcast(I8)).then_inc(codes_ready, 1)

        @block.scalar
        def _(act):
            act.wait_ge(w0_loaded, 48)
            for c in range(KC):
                nc.scalar.activation(W0h[:, c, :], W0raw[:, c, :], ACT.Copy).then_inc(w0h_ready, 1)
            for t in range(TILES):
                ringA.wait_full(act, UX + t)
                nc.scalar.activation(XTh[:, :, t * P:(t + 1) * P],
                                     ringA.bank(UX + t)[:].rearrange("p (c t) -> p c t", c=KC),
                                     ACT.Copy).then_inc(xh_ready, 1)
            act.wait_ge(biases_loaded, 48)

            def biased(use, j, bias, scale):
                ringA.wait_full(act, use)
                if j >= 2:
                    act.wait_ge(qkl_ready, j - 1)
                ringA.freed(nc.scalar.activation(QKf[:, j % 2, :], ringA.bank(use)[:], ACT.Identity,
                                                 bias=bias, scale=scale), use)

            for j in range(2):
                biased(UK + j, j, bk_t[:, 0:1], 1.0)
            for j in range(2):
                ringA.wait_full(act, UV + j)
                ringA.freed(nc.scalar.activation(VTf[:, j * HALF:(j + 1) * HALF], ringA.bank(UV + j)[:],
                                                 ACT.Identity, bias=bv_t[:, 0:1]), UV + j)
            act.wait_ge(bqs_ready, 1)
            for j in range(8):
                biased(UQ + j, 2 + j, bq_s[:, j // 2:j // 2 + 1], SCALE0)
            for c in range(KC):
                ringA.wait_full(act, UW + c)
                nc.scalar.activation(WFh[:, :, c * P:(c + 1) * P],
                                     ringA.bank(UW + c)[:].rearrange("p (c t) -> p c t", c=KC),
                                     ACT.Copy).then_inc(wfh_ready, 1)

            def outs0(n, k, qt):
                b, u = k % B, 2 * k + qt
                if b == 0 and (k or not at_start(n)):
                    act.wait_ge(out_moved, (n + k) * (GRP * 16 // B))
                ringO0.wait_full(act, u, n)
                ringO0.freed(nc.scalar.activation(
                    Of[:, :, b * S + qt * P:b * S + (qt + 1) * P],
                    ringO0.bank(u)[0:HD0, :].rearrange("p (h q) -> p h q", h=GRP), ACT.Copy), u)

            def attention_pair(pair, last):
                n = UNITS * pair
                for k in range(UNITS):
                    ahead = k + 2 < UNITS or not last
                    act.wait_ge(A0["pt_full"], 3 * (n + k) + 1)
                    nc.scalar.activation(PT0[:, 0, :], banks[3 + 3 * k % 2][:], ACT.Copy).then_inc(pt0_act, 1)
                    if ahead:
                        softmax_exp(act, A0, n, k + 2, 0, Sb0, 1.0)
                    outs0(n, k, 0)
                    if ahead:
                        softmax_exp(act, A0, n, k + 2, 1, Sb0, 1.0)
                        softmax_exp(act, A0, n, k + 2, 2, Sb0, 1.0)

            for k in range(2):
                for bank in range(3):
                    softmax_exp(act, A0, 0, k, bank, Sb0, 1.0)
            attention_pair(0, False)
            with act.Fori(1, GP - 1) as pair:
                attention_pair(pair, False)
            attention_pair(GP - 1, True)

            act.wait_ge(eps_ready, 1)

            def std_of(i):
                act.wait_ge(ln_dve, 2 * i + 2)
                nc.scalar.activation(std[:, i % 4:i % 4 + 1], moments[:, i % 4, 1:2], ACT.Sqrt,
                                     bias=eps[:, 0:1]).then_inc(std_ready, 1)

            def hi_of(use, dst, done):
                ringC.wait_full(act, use)
                nc.scalar.activation(dst, ringC.bank(use)[:].rearrange("p (c t) -> p c t", c=KC),
                                     ACT.Copy).then_inc(done, 1)

            proj_use = {t: use for what, t, use, _, _ in POST if what == "proj"}
            act.wait_ge(out_moved, 16 * GRP * NKV)
            for what, t, use, i, before in POST:
                if what == "attn":
                    if t >= 2:
                        ringC.wait_full(act, proj_use[t - 2])
                    nc.scalar.activation(ATh[:, t % 2], attn[:, :, t * P:(t + 1) * P], ACT.Copy)\
                      .then_inc(ath_ready, 1)
                elif what in ("norm1", "norm2"):
                    std_of(i)
                elif what == "turn1":
                    hi_of(use, X1h[:, t % 2], x1h_ready)
                elif what == "turn2":
                    hi_of(use, XTh[:, :, t * P:(t + 1) * P], x2h_ready)

            def table(g):
                for h in range(GRP):
                    last = nc.scalar.activation(tab[:, h, :], dist[:], ACT.Copy,
                                                scale=slopes[:, bass.ds(g * GRP + h, 1)])
                last.then_inc(tab_ready, 1)

            def q_out1(g, j):
                use = RQ + j
                ringL.wait_full(act, use, g * TURNS)
                h, half = j % GRP, j // GRP
                nc.scalar.activation(QT[:, h, half * HALF:(half + 1) * HALF], ringL.bank(use)[:],
                                     ACT.Copy).then_inc(qt_ready, 1)

            def group(g, last):
                n = B * g
                for j in range(2):
                    ringL.wait_full(act, RVT + j, g * TURNS)
                    nc.scalar.activation(Vh[:, 4 * j:4 * j + 4, :],
                                         ringL.bank(RVT + j)[:].rearrange("p (t d) -> p t d", t=4),
                                         ACT.Copy).then_inc(vh_ready, 1)
                def exps(b, bank):
                    softmax_exp(act, A1, n, b, bank, Sb1, SCALE1)

                def out_hi(b, qt):
                    use = RPV[b][qt]
                    ringL.wait_full(act, use, g * TURNS)
                    nc.scalar.activation(OTh[:, qt], ringL.bank(use)[:].rearrange("p (h q) -> p h q", h=GRP),
                                         ACT.Copy).then_inc(oth_ready, 1)

                for j in range(5):
                    q_out1(g, j)
                for bank in range(3):
                    exps(0, bank)
                q_out1(g, 5)
                q_out1(g, 6)
                for bank in range(3):
                    exps(1, bank)
                split_hi(act, A1, n, 0, 0, PTh1)
                split_hi(act, A1, n, 0, 1, PTh1)
                q_out1(g, 7)
                split_hi(act, A1, n, 0, 2, PTh1)
                out_hi(0, 0)
                exps(2, 0)
                exps(2, 1)
                out_hi(0, 1)
                exps(2, 2)
                for b in range(1, B):
                    for part in range(3):
                        split_hi(act, A1, n, b, part, PTh1)
                    out_hi(b, 0)
                    out_hi(b, 1)
                    if b == 1:
                        for bank in range(3):
                            exps(3, bank)
                if not last:
                    act.wait_ge(A1["scores_read"], 3 * (n + B))
                    table(g + 1)

            ringC.wait_done(act, POST_USES)
            table(0)
            group(0, False)
            with act.Fori(1, NKV - 1) as g:
                group(g, False)
            group(NKV - 1, True)

            for what, t, use, i, before in TAIL:
                if what in ("norm3", "norm4"):
                    std_of(NORMS + i)
                elif what == "turn":
                    ringF.wait_full(act, use)
                    nc.scalar.activation(FTh[:, t % 2, :], ringF.bank(use)[0:64, 0:P], ACT.Copy)\
                      .then_inc(fh_ready, 1)

        @block.vector
        def _(v):
            v.wait_ge(biases_loaded, 48)
            nc.vector.tensor_scalar(bq_s[:], bq_t[:], SCALE0, None, ALU.mult).then_inc(bqs_ready, 1)
            for c in range(KC):
                v.wait_ge(w0h_ready, c + 1)
                nc.vector.tensor_tensor(W0l[:, c, :], W0raw[:, c, :], W0h[:, c, :].bitcast(F32),
                                        ALU.subtract).then_inc(w0l_ready, 1)
            for t in range(TILES):
                v.wait_ge(xh_ready, t + 1)
                ins = nc.vector.tensor_tensor(XTl[:, :, t * P:(t + 1) * P],
                                              ringA.bank(UX + t)[:].rearrange("p (c t) -> p c t", c=KC),
                                              XTh[:, :, t * P:(t + 1) * P].bitcast(F32), ALU.subtract)
                ringA.freed(ins, UX + t)
            v.wait_ge(q_loaded, 32)
            nc.vector.tensor_scalar(qw[:], qv[:], -128.0, None, ALU.add).then_inc(deq_step, 1)
            v.wait_ge(deq_step, 1)
            for c in range(KC):
                w = qw[:, c, :].rearrange("p (b k) -> p b k", k=32)
                nc.vector.tensor_tensor(w, w, qs[:, c, :].unsqueeze(2).broadcast_to([P, 16, 32]),
                                        ALU.mult).then_inc(deq_step, 1)

            def split_qk(j):
                hi, lo = (Kh, Kl) if j < 2 else (Qh[:, (j - 2) // 2], Ql[:, (j - 2) // 2])
                cols = slice((j % 2) * HALF, (j % 2 + 1) * HALF)
                use = UK + j if j < 2 else UQ + j - 2
                v.wait_ge(ringA.free[use % 4], use // 4 + 1)
                nc.vector.tensor_copy(hi[:, cols], QKf[:, j % 2, :]).then_inc(qkh_ready, 1)
                v.wait_ge(qkh_ready, j + 1)
                nc.vector.tensor_tensor(lo[:, cols], QKf[:, j % 2, :], hi[:, cols].bitcast(F32),
                                        ALU.subtract).then_inc(qkl_ready, 1)

            for j in range(10):
                split_qk(j)
            for j in range(2):
                ringA.wait_full(v, UVT + j)
                nc.vector.tensor_copy(Vf[:, 4 * j:4 * j + 4, :],
                                      ringA.bank(UVT + j)[:].rearrange("p (t d) -> p t d", t=4))\
                  .then_inc(vf_ready, 1)
            for c in range(KC):
                v.wait_ge(wfh_ready, c + 1)
                nc.vector.tensor_tensor(WFl[:, :, c * P:(c + 1) * P],
                                        ringA.bank(UW + c)[:].rearrange("p (c t) -> p c t", c=KC),
                                        WFh[:, :, c * P:(c + 1) * P].bitcast(F32), ALU.subtract)\
                  .then_inc(wfl_ready, 1)

            def mask_of(h, qt):
                return mask[:, 0:P] if qt == 0 else mask[:, P:3 * P]

            def attention_pair(pair, last):
                n = UNITS * pair
                for k in range(UNITS):
                    ahead = k + 2 < UNITS or not last
                    if ahead:
                        hold(v, A0["pt_full"], 3 * (n + k) + 1)
                        softmax_max(v, A0, n, k + 2, Sb0, mask_of, 1.0, [0])
                    for part in (1, 2):
                        v.wait_ge(A0["pt_full"], 3 * (n + k) + part + 1)
                        nc.vector.tensor_copy(PT0[:, part, :], banks[3 + (3 * k + part) % 2][:])\
                          .then_inc(pt0_dve, 1)
                        if part == 1 and (k + 1 < UNITS or not last):
                            for bank in range(3):
                                softmax_rec(v, A0, n, k + 1, bank)
                    if ahead:
                        softmax_max(v, A0, n, k + 2, Sb0, mask_of, 1.0, [1, 2])
                    b, u = k % B, 2 * k + 1
                    if b == 0 and (k or not at_start(n)):
                        v.wait_ge(out_moved, (n + k) * (GRP * 16 // B))
                    ringO0.wait_full(v, u, n)
                    ringO0.freed(nc.vector.tensor_copy(
                        Of[:, :, b * S + P:(b + 1) * S],
                        ringO0.bank(u)[0:HD0, :].rearrange("p (h q) -> p h q", h=GRP)), u)

            v.wait_ge(consts_loaded, 48)
            softmax_max(v, A0, 0, 0, Sb0, mask_of, 1.0)
            softmax_max(v, A0, 0, 1, Sb0, mask_of, 1.0)
            for bank in range(3):
                softmax_rec(v, A0, 0, 0, bank)
            attention_pair(0, False)
            with v.Fori(1, GP - 1) as pair:
                attention_pair(pair, False)
            attention_pair(GP - 1, True)

            def norm(i, t, y):
                k = i % 4
                nc.vector.bn_stats(stats[:, k, :], y).then_inc(ln_dve, 1)
                v.wait_ge(ln_dve, 2 * i + 1)
                nc.vector.bn_aggr(moments[:, k, :], stats[:, k, :]).then_inc(ln_dve, 1)

            def normalize(what, i, t, y):
                k, done = i % 4, SCALED[what, t]
                v.wait_ge(std_ready, i + 1)
                nc.vector.reciprocal(rstd[:, k:k + 1], std[:, k:k + 1]).then_inc(rec_ready, 1)
                v.wait_ge(rec_ready, done)
                nc.vector.tensor_scalar(X[:, t, :], y, moments[:, k, 0:1], rstd[:, k:k + 1],
                                        ALU.subtract, ALU.mult).then_inc(xn_ready, 1)

            for what, t, use, i, before in POST:
                if what == "attn":
                    v.wait_ge(ath_ready, t + 1)
                    nc.vector.tensor_tensor(ATl[:, t % 2], attn[:, :, t * P:(t + 1) * P], ATh[:, t % 2].bitcast(F32),
                                            ALU.subtract).then_inc(atl_ready, 1)
                elif what in ("norm1", "norm2"):
                    y = Y[:, i % 2, :]
                    if what == "norm1":
                        v.wait_ge(bias_added, t + 1)
                    else:
                        v.wait_ge(z_ready, t + 1)
                    ringC.wait_full(v, before)
                    ringC.freed(nc.vector.tensor_tensor(y, ringC.bank(before)[:],
                                                        (X if what == "norm1" else Z)[:, t, :], ALU.add), before)
                    v.wait_ge(ringC.free[before % 4], before // 4 + 1)
                    norm(i, t, y)
                elif what in ("scale1", "scale2"):
                    normalize(what, i, t, Y[:, i % 2, :])
                elif what == "turn1":
                    v.wait_ge(x1h_ready, t + 1)
                    ringC.freed(nc.vector.tensor_tensor(
                        X1l[:, t % 2], ringC.bank(use)[:].rearrange("p (c t) -> p c t", c=KC),
                        X1h[:, t % 2].bitcast(F32), ALU.subtract), use)
                elif what == "turn2":
                    v.wait_ge(x2h_ready, t + 1)
                    ringC.freed(nc.vector.tensor_tensor(
                        XTl[:, :, t * P:(t + 1) * P], ringC.bank(use)[:].rearrange("p (c t) -> p c t", c=KC),
                        XTh[:, :, t * P:(t + 1) * P].bitcast(F32), ALU.subtract), use)

            def tab_of(h, qt):
                return tab[:, h, 0:P] if qt == 0 else tab[:, h, P:3 * P]

            def add_out(g, b, qt):
                use = ROP[b][qt]
                ringL.wait_full(v, use, g * TURNS)
                t = 2 * b + qt
                nc.vector.tensor_tensor(X[:, t, :], ringL.bank(use)[:], X[:, t, :], ALU.add).then_inc(x_added, 1)

            def out_lo(g, b, qt):
                use = RPV[b][qt]
                v.wait_ge(oth_ready, 2 * (B * g + b) + qt + 1)
                nc.vector.tensor_tensor(
                    OTl[:, qt], ringL.bank(use)[:].rearrange("p (h q) -> p h q", h=GRP),
                    OTh[:, qt].bitcast(F32), ALU.subtract).then_inc(otl_ready, 1)

            def group(g, last):
                n = B * g

                def maxes(b):
                    softmax_max(v, A1, n, b, Sb1, tab_of, SCALE1)

                def recs(b):
                    for bank in range(3):
                        softmax_rec(v, A1, n, b, bank)

                for use, dst, done in ((RV, VT, vt1_ready), (RK, KT, kt_ready)):
                    for j in range(2):
                        ringL.wait_full(v, use + j, g * TURNS)
                        nc.vector.tensor_copy(dst[:, j * HALF:(j + 1) * HALF], ringL.bank(use + j)[:])\
                          .then_inc(done, 1)
                for j in range(2):
                    v.wait_ge(vh_ready, 2 * g + j + 1)
                    nc.vector.tensor_tensor(
                        Vl[:, 4 * j:4 * j + 4, :], ringL.bank(RVT + j)[:].rearrange("p (t d) -> p t d", t=4),
                        Vh[:, 4 * j:4 * j + 4, :].bitcast(F32), ALU.subtract).then_inc(vl_ready, 1)
                v.wait_ge(tab_ready, g + 1)
                maxes(0)
                recs(0)
                maxes(1)
                recs(1)
                split_lo(v, A1, n, 0, 0, PTh1, PTl1)
                split_lo(v, A1, n, 0, 1, PTh1, PTl1)
                split_lo(v, A1, n, 0, 2, PTh1, PTl1)
                maxes(2)
                out_lo(g, 0, 0)
                softmax_rec(v, A1, n, 2, 0)
                softmax_rec(v, A1, n, 2, 1)
                out_lo(g, 0, 1)
                softmax_rec(v, A1, n, 2, 2)
                for b in range(1, B):
                    split_lo(v, A1, n, b, 0, PTh1, PTl1)
                    split_lo(v, A1, n, b, 1, PTh1, PTl1)
                    add_out(g, b - 1, 0)
                    split_lo(v, A1, n, b, 2, PTh1, PTl1)
                    out_lo(g, b, 0)
                    add_out(g, b - 1, 1)
                    out_lo(g, b, 1)
                    if b == 1:
                        maxes(3)
                        recs(3)
                add_out(g, B - 1, 0)
                add_out(g, B - 1, 1)

            group(0, False)
            with v.Fori(1, NKV - 1) as g:
                group(g, False)
            group(NKV - 1, True)

            v.wait_ge(x_added, 2 * B * NKV)
            for what, t, use, i, before in TAIL:
                if what == "norm3":
                    norm(NORMS + i, t, X[:, t, :])
                elif what == "scale3":
                    normalize(what, NORMS + i, t, X[:, t, :])
                    v.wait_ge(xn_ready, SCALED[what, t])
                    nc.vector.tensor_reduce(fold[:, t % 2, :], X[:, t, :].rearrange("p (a r) -> p r a", r=64),
                                            AX.X, ALU.add).then_inc(fold_ready, 1)
                elif what == "turn":
                    v.wait_ge(fh_ready, t + 1)
                    ringF.freed(nc.vector.tensor_tensor(
                        FTl[:, t % 2, :], ringF.bank(use)[0:64, 0:P], FTh[:, t % 2, :].bitcast(F32),
                        ALU.subtract), use)
                elif what == "norm4":
                    ringF.wait_full(v, before)
                    ringF.freed(nc.vector.tensor_tensor(X[:, t, :], ringF.bank(before)[:], X[:, t, :], ALU.add),
                                before)
                    v.wait_ge(ringF.free[before % 4], before // 4 + 1)
                    norm(NORMS + i, t, X[:, t, :])
                elif what == "scale4":
                    normalize(what, NORMS + i, t, X[:, t, :])

        @block.tensor
        def _(pe):
            def three(out_ap, lh, ll, rh, rl, first, last):
                nc.tensor.matmul(out_ap, lh, rh, start=first, stop=False)
                nc.tensor.matmul(out_ap, lh, rl, start=False, stop=False)
                return nc.tensor.matmul(out_ap, ll, rh, start=False, stop=last)

            pe.wait_ge(ident_loaded, 16)
            for t in range(TILES):
                pe.wait_ge(x_loaded[t // 2], 16)
                ringA.wait_free(pe, UX + t)
                for c in range(KC):
                    last = nc.tensor.transpose(ringA.bank(UX + t)[:, c * P:(c + 1) * P],
                                               X[:, t, c * P:(c + 1) * P], ident[:])
                ringA.filled(last, UX + t)

            def project0(use, m, half):
                ringA.wait_free(pe, use)
                cols = slice(half * HALF, (half + 1) * HALF)
                for c in range(KC):
                    last = three(ringA.bank(use)[:], W0h[:, c, m * P:(m + 1) * P], W0l[:, c, m * P:(m + 1) * P],
                                 XTh[:, c, cols], XTl[:, c, cols], c == 0, c == KC - 1)
                ringA.filled(last, use)

            pe.wait_ge(w0l_ready, KC)
            for b in range(4):
                pe.wait_ge(ringA.free[b], 2)
            for half in range(2):
                project0(UK + half, 4, half)
            for half in range(2):
                project0(UV + half, 5, half)
            for m in range(4):
                for half in range(2):
                    project0(UQ + 2 * m + half, m, half)
            for j in range(2):
                ringA.wait_free(pe, UVT + j)
                pe.wait_ge(ringA.free[(UV + j) % 4], (UV + j) // 4 + 1)
                for t in range(4):
                    last = nc.tensor.transpose(ringA.bank(UVT + j)[:, t * P:(t + 1) * P],
                                               VTf[:, (4 * j + t) * P:(4 * j + t + 1) * P], ident[:])
                ringA.filled(last, UVT + j)
            pe.wait_ge(deq_step, 1 + KC)
            for c in range(KC):
                if c < 2:
                    ringA.wait_free(pe, UW + c)
                else:
                    pe.wait_ge(vf_ready, c - 1)
                for i in range(KC):
                    last = nc.tensor.transpose(ringA.bank(UW + c)[:, i * P:(i + 1) * P],
                                               qw[:, c, i * P:(i + 1) * P], ident[:])
                ringA.filled(last, UW + c)

            def scores0(n, k, pair):
                b, par = k % B, (k // B) % 2
                rows_ = slice(64 * par, 64 * par + 64)
                if b == 0:
                    pe.wait_ge(qs_loaded[par], (pair + 1) * 16 * 20)
                for bank in range(3):
                    if not at_start(n) or k:
                        pe.wait_ge(A0["scores_read"], 3 * (n + k) + bank - 2)
                    heads = range(GRP) if bank == 0 else range(2 * bank - 2, 2 * bank)
                    for h in heads:
                        qt = 0 if bank == 0 else 1
                        _, c0, _, w = score_slices(h)[qt]
                        last = nc.tensor.matmul(banks[bank][:, c0:c0 + w],
                                                QS[rows_, h, b * S + qt * P:b * S + (qt + 1) * P],
                                                KS[rows_, b * S:b * S + w], start=True, stop=True)
                    last.then_inc(A0["scores_ready"], 1)

            def values0(n, k, pair, qt):
                b, par = k % B, k // B
                if b == 0 and qt == 0:
                    pe.wait_ge(vs_ready, 2 * pair + par + 1)
                u = 2 * k + qt
                ringO0.wait_free(pe, u, n)
                if qt == 0:
                    pe.wait_ge(pt0_act, n + k + 1)
                else:
                    pe.wait_ge(pt0_dve, 2 * (n + k) + 2)
                parts = [(0, 0)] if qt == 0 else [(1, 0), (2, 1)]
                for j, (part, kt) in enumerate(parts):
                    last = nc.tensor.matmul(ringO0.bank(u)[0:HD0, :], VS[:, par, 2 * b + kt, :],
                                            PT0[:, part, :], start=(j == 0), stop=(j == len(parts) - 1))
                ringO0.filled(last, u)

            def attention_pair(pair, last):
                n = UNITS * pair
                for k in range(UNITS):
                    if k + 2 < UNITS or not last:
                        scores0(n, k + 2, pair + (k + 2) // UNITS)
                    transpose_probs(pe, A0, n, k, 0, Sb0)
                    transpose_probs(pe, A0, n, k, 1, Sb0)
                    values0(n, k, pair, 0)
                    transpose_probs(pe, A0, n, k, 2, Sb0)
                    values0(n, k, pair, 1)

            pe.wait_ge(wfl_ready, KC)
            scores0(0, 0, 0)
            scores0(0, 1, 0)
            attention_pair(0, False)
            with pe.Fori(1, GP - 1) as pair:
                attention_pair(pair, False)
            attention_pair(GP - 1, True)

            pe.wait_ge(wo0_ready, KC)
            for what, t, i, _, before in POST:
                if what == "proj":
                    pe.wait_ge(atl_ready, t + 1)
                    ringC.wait_free(pe, i)
                    for c in range(KC):
                        last = three(ringC.bank(i)[:], ATh[:, t % 2, c, :], ATl[:, t % 2, c, :],
                                     Wo0h[:, c, :], Wo0l[:, c, :], c == 0, c == KC - 1)
                    ringC.filled(last, i)
                elif what == "linear":
                    pe.wait_ge(ringC.free[before % 4], before // 4 + 1)
                    ringC.wait_free(pe, i)
                    for c in range(KC):
                        last = three(ringC.bank(i)[:], X1h[:, t % 2, c, :], X1l[:, t % 2, c, :],
                                     WFh[:, c, :], WFl[:, c, :], c == 0, c == KC - 1)
                    ringC.filled(last, i)
                elif what in ("turn1", "turn2"):
                    pe.wait_ge(xn_ready, SCALED["scale" + what[-1], t])
                    ringC.wait_free(pe, i)
                    for c in range(KC):
                        last = nc.tensor.transpose(ringC.bank(i)[:, c * P:(c + 1) * P],
                                                   X[:, t, c * P:(c + 1) * P], ident[:])
                    ringC.filled(last, i)

            def lwait(g, use):
                prev = use - len(ringL.banks)
                if prev < 0 and at_start(g):
                    return
                if prev < 0:
                    pe.wait_ge(*((otl_ready, 2 * B * g) if prev == -3 else (x_added, 2 * B * g + prev + 1)))
                elif prev < RK:
                    pe.wait_ge(vt1_ready, 2 * g + prev - RV + 1)
                elif prev < RVT:
                    pe.wait_ge(kt_ready, 2 * g + prev - RK + 1)
                elif prev < RQ:
                    pe.wait_ge(vl_ready, 2 * g + prev - RVT + 1)
                elif prev < RP:
                    pe.wait_ge(qt_ready, 8 * g + prev - RQ + 1)
                else:
                    for b in range(B):
                        for qt in range(2):
                            if prev == RPV[b][qt]:
                                pe.wait_ge(otl_ready, 2 * (B * g + b) + qt + 1)
                            if prev == ROP[b][qt]:
                                pe.wait_ge(x_added, 2 * (B * g + b) + qt + 1)

            def project1(g, use, m, half):
                lwait(g, use)
                cols = slice(half * HALF, (half + 1) * HALF)
                for c in range(KC):
                    last = three(ringL.bank(use)[:], W1h[:, c, m * P:(m + 1) * P], W1l[:, c, m * P:(m + 1) * P],
                                 XTh[:, c, cols], XTl[:, c, cols], c == 0, c == KC - 1)
                ringL.filled(last, use)

            def scores1(g, b):
                n = B * g
                for bank in range(3):
                    if not at_start(n) or b:
                        pe.wait_ge(A1["scores_read"], 3 * (n + b) + bank - 2)
                    heads = range(GRP) if bank == 0 else range(2 * bank - 2, 2 * bank)
                    for h in heads:
                        qt = 0 if bank == 0 else 1
                        _, c0, _, w = score_slices(h)[qt]
                        last = nc.tensor.matmul(banks[bank][:, c0:c0 + w],
                                                QT[:, h, b * S + qt * P:b * S + (qt + 1) * P],
                                                KT[:, b * S:b * S + w], start=True, stop=True)
                    last.then_inc(A1["scores_ready"], 1)

            def values1(g, b, qt):
                n = B * g
                use = RPV[b][qt]
                lwait(g, use)
                pe.wait_ge(A1["ptl_ready"], 3 * (n + b) + (1 if qt == 0 else 3))
                parts = [(0, 0)] if qt == 0 else [(1, 0), (2, 1)]
                for j, (part, kt) in enumerate(parts):
                    last = three(ringL.bank(use)[:], Vh[:, 2 * b + kt, :], Vl[:, 2 * b + kt, :],
                                 PTh1[:, part, :], PTl1[:, part, :], j == 0, j == len(parts) - 1)
                ringL.filled(last, use)

            def output1(g, b, qt):
                use = ROP[b][qt]
                lwait(g, use)
                if b == 0 and qt == 0:
                    pe.wait_ge(wo1_split, g + 1)
                pe.wait_ge(otl_ready, 2 * (B * g + b) + qt + 1)
                for h in range(GRP):
                    last = three(ringL.bank(use)[:], OTh[:, qt, h, :], OTl[:, qt, h, :],
                                 Woh[:, h, :], Wol[:, h, :], h == 0, h == GRP - 1)
                ringL.filled(last, use)

            def group(g, last):
                n = B * g
                pe.wait_ge(w1_split, g + 1)
                for half in range(2):
                    project1(g, RV + half, 5, half)
                for half in range(2):
                    project1(g, RK + half, 4, half)
                for j in range(2):
                    lwait(g, RVT + j)
                    pe.wait_ge(vt1_ready, 2 * g + j + 1)
                    for t in range(4):
                        ins = nc.tensor.transpose(ringL.bank(RVT + j)[:, t * P:(t + 1) * P],
                                                  VT[:, (4 * j + t) * P:(4 * j + t + 1) * P], ident[:])
                    ringL.filled(ins, RVT + j)
                for j in range(5):
                    project1(g, RQ + j, j % GRP, j // GRP)
                pe.wait_ge(qt_ready, 8 * g + 4)
                scores1(g, 0)
                project1(g, RQ + 5, 1, 1)
                project1(g, RQ + 6, 2, 1)
                scores1(g, 1)
                transpose_probs(pe, A1, n, 0, 0, Sb1)
                transpose_probs(pe, A1, n, 0, 1, Sb1)
                project1(g, RQ + 7, 3, 1)
                transpose_probs(pe, A1, n, 0, 2, Sb1)
                values1(g, 0, 0)
                pe.wait_ge(qt_ready, 8 * g + 8)
                scores1(g, 2)
                values1(g, 0, 1)
                for b in range(1, B):
                    transpose_probs(pe, A1, n, b, 0, Sb1)
                    transpose_probs(pe, A1, n, b, 1, Sb1)
                    output1(g, b - 1, 0)
                    transpose_probs(pe, A1, n, b, 2, Sb1)
                    values1(g, b, 0)
                    output1(g, b - 1, 1)
                    values1(g, b, 1)
                    if b == 1:
                        scores1(g, 3)
                output1(g, B - 1, 0)
                output1(g, B - 1, 1)

            ringC.wait_done(pe, POST_USES)
            group(0, False)
            with pe.Fori(1, NKV - 1) as g:
                group(g, False)
            group(NKV - 1, True)

            pe.wait_ge(codes_ready, 1)
            for what, t, i, _, before in TAIL:
                if what == "turn":
                    pe.wait_ge(fold_ready, t + 1)
                    ringF.wait_free(pe, i)
                    ringF.filled(nc.tensor.transpose(ringF.bank(i)[0:64, 0:P], fold[:, t % 2, :], ident[:]), i)
                elif what == "codes":
                    pe.wait_ge(ringF.free[before % 4], before // 4 + 1)
                    ringF.wait_free(pe, i)
                    nc.tensor.matmul(ringF.bank(i)[:], FTh[:, t % 2, :], codes_f[:], start=True, stop=False)
                    last = nc.tensor.matmul(ringF.bank(i)[:], FTl[:, t % 2, :], codes_f[:], start=False, stop=True)
                    ringF.filled(last, i)


_INS = ["L0_attn_x", "L0_attn_Wq", "L0_attn_bq", "L0_attn_Wk", "L0_attn_bk", "L0_attn_Wv", "L0_attn_bv",
        "L0_attn_Wo", "L0_attn_bo", "L0_ffn_q_scales", "L0_ffn_q_vals", "L0_ffn_bias", "L1_attn_w_qkv",
        "L1_attn_w_o", "L1_ffn_kernel"]


def kernel(**inputs):
    import numpy as _np
    import concourse.bacc as _bacc
    from concourse import mybir as _mybir
    from concourse.bass_utils import run_bass_kernel_spmd as _run

    nc = _bacc.Bacc("TRN2", target_bir_lowering=False, num_devices=1)
    arrays, args = {}, []

    def feed(name, a):
        arrays[name] = a
        args.append(nc.dram_tensor(name, a.shape, _mybir.dt.from_np(a.dtype), kind="ExternalInput").ap())

    for name in _INS:
        a = _np.ascontiguousarray(inputs[name])
        feed(f"in_{name}_dram", a.view(_np.int32) if a.dtype == _np.int8 else a)
    q = _np.arange(P)[:, None]
    rel = _np.concatenate([q - _np.arange(P)[None, :], q + P - _np.arange(S)[None, :]], axis=1)
    feed("identity", _np.eye(P, dtype=_np.float32))
    feed("mask_const", _np.where(rel >= 0, 0.0, -1e30).astype(_np.float32))
    feed("dist_const", _np.where(rel >= 0, -_np.sqrt(_np.maximum(rel, 0)) / SCALE1, -1e30).astype(_np.float32))
    slopes = (2.0 ** (-8.0 / (NKV * GRP))) ** _np.arange(1, NKV * GRP + 1, dtype=_np.float32)
    feed("slopes_const", _np.ascontiguousarray(_np.broadcast_to(slopes.astype(_np.float32), (P, NKV * GRP))))
    args.append(nc.dram_tensor("out_0_dram", (B, S, DM), _mybir.dt.float32, kind="ExternalOutput").ap())
    two_layers(nc, *args)
    r = _run(nc, [arrays], core_ids=[0])
    return r.results[0]["out_0_dram"]
```

```python
from contextlib import ExitStack

import concourse.bass as bass
from concourse import mybir

F32 = mybir.dt.float32
F32R = mybir.dt.float32r
I32 = mybir.dt.int32
I8 = mybir.dt.int8
ALU = mybir.AluOpType
ACT = mybir.ActivationFunctionType
AX = mybir.AxisListType

P = 128
B, S, DM = 4, 256, 512
TOK = B * S
TILES = TOK // P
KC = DM // P
HALF = TOK // 2
NKV, GRP = 8, 4
HD0 = 16
HD1 = 128
EPS = 1e-5
SCALE0 = 0.25
SCALE1 = float(HD1) ** -0.5
QCOLS = NKV * GRP * HD1
KVC = NKV * HD1
SP0 = GRP * P
SPC = SP0 + GRP * S
FLOOR = -3.0e38


def hold(eng, semaphore, count):
    eng.wait_ge(semaphore, count)
    eng.nop(nofuse=True)


class Ring:

    def __init__(self, banks, full, free):
        self.banks, self.full, self.free = banks, full, free

    def bank(self, n):
        return self.banks[n % len(self.banks)]

    def wait_free(self, eng, n, loop=0):
        turn = n // len(self.banks)
        if turn or not at_start(loop):
            eng.wait_ge(self.free[n % len(self.banks)], turn + loop)

    def wait_full(self, eng, n, loop=0):
        eng.wait_ge(self.full[n % len(self.banks)], n // len(self.banks) + 1 + loop)

    def wait_read(self, eng, n):
        eng.wait_ge(self.free[n % len(self.banks)], n // len(self.banks) + 1)

    def wait_done(self, eng, uses):
        for b in range(len(self.banks)):
            eng.wait_ge(self.free[b], (uses - b + len(self.banks) - 1) // len(self.banks))

    def filled(self, ins, n):
        ins.then_inc(self.full[n % len(self.banks)], 1)

    def freed(self, ins, n):
        ins.then_inc(self.free[n % len(self.banks)], 1)


def steps(rows_):
    use = norm = 0
    uses, norms, out = {}, {}, []
    for what, t, takes in rows_:
        mine = number = None
        if what in USES:
            mine = uses[what, t] = use
            use += 1
        if what.startswith("norm"):
            number = norms[what[-1], t] = norm
            norm += 1
        if what.startswith("scale"):
            number = norms[what[-1], t]
        out.append((what, t, mine, number, uses.get((takes, t))))
    return out, use


USES = ("proj", "turn1", "linear", "turn2", "turn", "codes")


def pipeline(slots, order):
    return [(what, s - lag, takes) for s in slots for what, lag, takes in order if 0 <= s - lag < TILES]


POST, POST_USES = steps(pipeline(range(-1, TILES + 4), [
    ("turn1", 2, None), ("norm2", 3, "linear"), ("scale1", 1, None), ("turn2", 4, None), ("proj", 0, None),
    ("attn", -1, None), ("scale2", 3, None), ("linear", 2, "turn1"), ("norm1", 0, "proj")]))
TAIL_ORDER = [("scale3", 1, None), ("scale4", 4, None), ("norm3", 0, None), ("codes", 3, "turn"),
              ("turn", 2, None), ("norm4", 3, "codes")]
TAIL_SLOTS = TILES + 4
TAIL, TAIL_USES = steps(pipeline(range(TAIL_SLOTS), TAIL_ORDER))


def tail_steps(slots):
    lag = {what: n for what, n, _ in TAIL_ORDER}
    return [step for step in TAIL if step[1] + lag[step[0]] in slots]


NORMS = 2 * TILES


def scaled(plan, base=0):
    return {(what, t): base + n + 1 for n, (what, t) in
            enumerate([(w, t) for w, t, _, _, _ in plan if w.startswith("scale")])}


NAMES = [("scale" + what[-1], t) for what, t, _, _, _ in POST if what.startswith("norm")]
SCALED = {**scaled(POST), **scaled(TAIL, NORMS)}


def at_start(n):
    return isinstance(n, int) and n == 0


def two_layers(nc, x_in, wq0, bq0, wk0, bk0, wv0, bv0, wo0, bo0, q_scales, q_vals, ffn_bias,
               w_qkv, w_o, codes, ident_in, mask_in, dist_in, slopes_in, out):
    root = ExitStack()
    with root:
        def sb(name, shape, dt=F32, scope=root):
            return scope.enter_context(nc.sbuf_tensor(name, shape, dt))

        def sem(name):
            return root.enter_context(nc.semaphore(name))

        X = sb("X", [P, TILES, DM])
        XTh = sb("XTh", [P, KC, TOK], F32R)
        XTl = sb("XTl", [P, KC, TOK], F32R)
        attn = XTh[:].bitcast(F32)
        ident = sb("ident", [P, P])
        mask = sb("mask", [P, 3 * P])
        dist = sb("dist", [P, 3 * P])
        slopes = sb("slopes", [P, NKV * GRP])
        stats = sb("stats", [P, 4, 6])
        moments = sb("moments", [P, 4, 2])
        std = sb("std", [P, 4])
        rstd = sb("rstd", [P, 4])
        shift = sb("shift", [P, 4])
        eps = sb("eps", [P, 1])
        rowmax = sb("rowmax", [P, 2, 2 * GRP])
        negmax = sb("negmax", [P, 2, 2 * GRP])
        rowsum = sb("rowsum", [P, 2, 2 * GRP])
        rowrec = sb("rowrec", [P, 2, 2 * GRP])
        bo_b = sb("bo_b", [P, DM])
        fb_b = sb("fb_b", [P, DM])
        bq_t = sb("bq_t", [P, KC])
        bq_s = sb("bq_s", [P, KC])
        bk_t = sb("bk_t", [P, 1])
        bv_t = sb("bv_t", [P, 1])
        keep = ExitStack()
        WFh = sb("WFh", [P, KC, DM], F32R, keep)
        WFl = sb("WFl", [P, KC, DM], F32R, keep)
        early = ExitStack()
        Qh = sb("Qh", [P, KC, TOK], F32R, early)
        Ql = sb("Ql", [P, KC, TOK], F32R, early)
        Kh = sb("Kh", [P, TOK], F32R, early)
        Kl = sb("Kl", [P, TOK], F32R, early)
        Vf = sb("Vf", [P, TILES, P], F32, early)
        QS = sb("QS", [P, GRP, TOK], F32R, early)
        KS = sb("KS", [P, TOK], F32R, early)
        proj = ExitStack()
        W0raw = sb("W0raw", [P, KC, 6 * P], F32, proj)
        W0h = sb("W0h", [P, KC, 6 * P], F32R, proj)
        W0l = sb("W0l", [P, KC, 6 * P], F32R, proj)
        QKf = sb("QKf", [P, 2, HALF], F32, proj)
        VTf = sb("VTf", [P, TOK], F32, proj)
        qv = sb("qv", [P, KC, DM], I32, proj)
        qw = sb("qw", [P, KC, DM], F32, proj)
        qs = sb("qs", [P, KC, 16], F32, proj)
        proj.close()
        att = ExitStack()
        Sb0 = [sb(f"Sb0_{i}", [P, SPC], F32, att) for i in range(2)]
        PT0 = sb("PT0", [P, 3, 4 * P], F32, att)
        Of = sb("Of", [HD0, GRP, TOK], F32, att)
        VS = sb("VS", [P, 2, TILES, HD0], F32, att)
        Wo0raw = sb("Wo0raw", [P, KC, DM], F32, att)
        Wo0h = sb("Wo0h", [P, KC, DM], F32R, att)
        Wo0l = sb("Wo0l", [P, KC, DM], F32R, att)
        att.close()
        early.close()
        post = ExitStack()
        Y = sb("Y", [P, 2, DM], F32, post)
        Z = sb("Z", [P, TILES, DM], F32, post)
        ATh = sb("ATh", [P, 2, KC, P], F32R, post)
        ATl = sb("ATl", [P, 2, KC, P], F32R, post)
        X1h = sb("X1h", [P, 2, KC, P], F32R, post)
        X1l = sb("X1l", [P, 2, KC, P], F32R, post)
        post.close()
        keep.close()
        QT = sb("QT", [P, GRP, TOK])
        KT = sb("KT", [P, TOK])
        VT = sb("VT", [P, TOK])
        Sb1 = [sb(f"Sb1_{i}", [P, SPC]) for i in range(2)]
        PTh1 = sb("PTh1", [P, 3, 4 * P], F32R)
        PTl1 = sb("PTl1", [P, 3, 4 * P], F32R)
        OTh = sb("OTh", [P, 2, GRP, P], F32R)
        OTl = sb("OTl", [P, 2, GRP, P], F32R)
        W1raw = sb("W1raw", [P, KC, 6 * P])
        W1h = sb("W1h", [P, KC, 6 * P], F32R)
        W1l = sb("W1l", [P, KC, 6 * P], F32R)
        Woraw = sb("Woraw", [P, GRP, DM])
        Vh = sb("Vh", [P, TILES, P], F32R)
        Vl = sb("Vl", [P, TILES, P], F32R)
        tab = sb("tab", [P, GRP, 3 * P])
        Woh = sb("Woh", [P, GRP, DM], F32R)
        Wol = sb("Wol", [P, GRP, DM], F32R)
        codes_i = sb("codes_i", [P, DM // 4], I32)
        codes_f = sb("codes_f", [P, DM], F32R)
        FTh = sb("FTh", [P, 2, P], F32R)
        FTl = sb("FTl", [P, 2, P], F32R)

        banks = [root.enter_context(nc.psum_tensor(f"bank{i}", [P, 512], F32)) for i in range(8)]

        def ring(name, ids):
            return Ring([banks[i] for i in ids], [sem(f"{name}_full{i}") for i in ids],
                        [sem(f"{name}_free{i}") for i in ids])

        ringA = ring("proj0", [0, 1, 2, 3])
        ringO0 = ring("pv0", [5, 6])
        ringC = ring("post", [0, 1, 2, 3])
        ringL = ring("l1", [5, 6, 7])
        ringF = ring("tail", [0, 1, 2])

        x_loaded = [sem(f"x_loaded{i}") for i in range(4)]
        w0_loaded = sem("w0_loaded")
        ident_loaded = sem("ident_loaded")
        consts_loaded = sem("consts_loaded")
        biases_loaded = sem("biases_loaded")
        q_loaded = sem("q_loaded")
        wo0_loaded = sem("wo0_loaded")
        post_loaded = sem("post_loaded")
        w1_loaded = sem("w1_loaded")
        wo1_loaded = sem("wo1_loaded")
        codes_loaded = sem("codes_loaded")
        stored = sem("stored")
        w0h_ready = sem("w0h_ready")
        w0l_ready = sem("w0l_ready")
        xh_ready = sem("xh_ready")
        xl_ready = sem("xl_ready")
        bqs_ready = sem("bqs_ready")
        qk_biased = sem("qk_biased")
        qkh_ready = sem("qkh_ready")
        qkl_ready = sem("qkl_ready")
        vt_ready = sem("vt_ready")
        vf_ready = sem("vf_ready")
        deq_step = sem("deq_step")
        wfh_ready = sem("wfh_ready")
        wfl_ready = sem("wfl_ready")
        eps_ready = sem("eps_ready")
        qs_loaded = [sem("qs_loaded0"), sem("qs_loaded1")]
        vs_ready = sem("vs_ready")
        out_moved = [sem("out_moved0"), sem("out_moved1")]
        pt0_act = sem("pt0_act")
        pt0_dve = sem("pt0_dve")
        rstd_ready = sem("rstd_ready")
        rec_ready = sem("rec_ready")
        scale_step = sem("scale_step")
        wo0h_ready = sem("wo0h_ready")
        wo0_ready = sem("wo0_ready")

        def softmax_sems(name):
            return {k: sem(f"{name}_{k}") for k in
                    ("scores_ready", "scores_read", "max_ready", "negmax_ready", "exp_done", "rec_ready",
                     "norm_done", "pt_full", "pth_ready", "ptl_ready")}
        A0, A1 = softmax_sems("a0"), softmax_sems("a1")
        ath_ready = sem("ath_ready")
        atl_ready = sem("atl_ready")
        y_ready = sem("y_ready")
        ln_dve = sem("ln_dve")
        std_ready = sem("std_ready")
        xn_ready = sem("xn_ready")
        x1h_ready = sem("x1h_ready")
        x1l_ready = sem("x1l_ready")
        x2h_ready = sem("x2h_ready")
        x2l_ready = sem("x2l_ready")
        bias_added = sem("bias_added")
        z_ready = sem("z_ready")
        w1_split = sem("w1_split")
        w1_step = sem("w1_step")
        wo1_split = sem("wo1_split")
        wo1_step = sem("wo1_step")
        tab_ready = sem("tab_ready")
        kt_ready = sem("kt_ready")
        vt1_ready = sem("vt1_ready")
        vh_ready = sem("vh_ready")
        vl_ready = sem("vl_ready")
        qt_ready = sem("qt_ready")
        oth_ready = sem("oth_ready")
        otl_ready = sem("otl_ready")
        x_added = sem("x_added")
        codes_ready = sem("codes_ready")
        fh_ready = sem("fh_ready")
        fl_ready = sem("fl_ready")

        x_v = x_in.rearrange("b (t p) d -> p (b t) d", p=P)
        out_v = out.rearrange("b (t p) d -> p (b t) d", p=P)

        def rows(w):
            return w.rearrange("(c p) n -> p c n", p=P)

        wqkv_v = rows(w_qkv)
        wo_v = w_o.rearrange("(h p) n -> p h n", p=P)

        def sb_q0(t):
            return t[:, 0:SP0].rearrange("p (h k) -> p h k", h=GRP)

        def sb_q1(t):
            return t[:, SP0:SPC].rearrange("p (h k) -> p h k", h=GRP)

        def score_slices(h):
            return [(0, h * P, h * P, P), (1 + h // 2, (h % 2) * S, SP0 + h * S, S)]

        def bank_slices(bank):
            qt = 0 if bank == 0 else 1
            heads = range(GRP) if bank == 0 else range(2 * bank - 2, 2 * bank)
            return heads, qt, slice(qt * GRP + heads[0], qt * GRP + heads[-1] + 1)

        def softmax_max(v, A, n, k, buf, table_of, scale, only=range(3)):
            i = k % 2
            for bank in only:
                hold(v, A["scores_ready"], 3 * (n + k) + bank + 1)
                heads, qt, cols = bank_slices(bank)
                for h in heads:
                    _, c0, s0, w = score_slices(h)[qt]
                    last = nc.vector.tensor_tensor_reduce(
                        out=buf[i][:, s0:s0 + w], in0=banks[bank][:, c0:c0 + w], in1=table_of(h, qt), scale=1.0,
                        scalar=FLOOR, op0=ALU.add, op1=ALU.max,
                        accum_out=rowmax[:, i, qt * GRP + h:qt * GRP + h + 1])
                last.then_inc(A["scores_read"], 1)
                v.wait_ge(A["scores_read"], 3 * (n + k) + bank + 1)
                nc.vector.tensor_scalar(negmax[:, i, cols], rowmax[:, i, cols], -scale, None,
                                        ALU.mult).then_inc(A["negmax_ready"], 1)

        def softmax_exp(act, A, n, k, bank, buf, scale):
            i = k % 2
            act.wait_ge(A["negmax_ready"], 3 * (n + k) + bank + 1)
            heads, qt, _ = bank_slices(bank)
            for h in heads:
                _, _, s0, w = score_slices(h)[qt]
                j = qt * GRP + h
                last = nc.scalar.activation(buf[i][:, s0:s0 + w], buf[i][:, s0:s0 + w], ACT.Exp,
                                            bias=negmax[:, i, j:j + 1], scale=scale,
                                            accum_out=rowsum[:, i, j:j + 1])
            last.then_inc(A["exp_done"], 1)

        def softmax_rec(v, A, n, k, bank):
            i = k % 2
            _, _, cols = bank_slices(bank)
            v.wait_ge(A["exp_done"], 3 * (n + k) + bank + 1)
            nc.vector.reciprocal(rowrec[:, i, cols], rowsum[:, i, cols]).then_inc(A["rec_ready"], 1)

        def softmax_norm(g, A, n, k, buf):
            i = k % 2
            for bank in range(3):
                hold(g, A["rec_ready"], 3 * (n + k) + bank + 1)
                heads, qt, cols = bank_slices(bank)
                w = P if qt == 0 else S
                view = (sb_q1 if qt else sb_q0)(buf[i])[:, heads[0]:heads[-1] + 1, :]
                r = rowrec[:, i, cols].unsqueeze(2).broadcast_to([P, len(heads), w])
                nc.gpsimd.tensor_tensor(view, view, r, ALU.mult).then_inc(A["norm_done"], 1)

        def turn_bank(A, k, part):
            return banks[(3, 4, 7)[part] if A is A0 else 3 + (3 * k + part) % 2]

        def transpose_probs(pe, A, n, k, part, buf):
            if part < 2:
                pe.wait_ge(A["norm_done"], 3 * (n + k) + (3 if part else 1))
            j = 3 * k + part
            if A is A1:
                if not at_start(n) or j >= 2:
                    pe.wait_ge(A["ptl_ready"], 3 * n + j - 1)
            elif not at_start(n) or k:
                if part == 0:
                    pe.wait_ge(pt0_act, n + k)
                else:
                    pe.wait_ge(pt0_dve, 2 * (n + k) + part - 2)
            for h in range(GRP):
                _, _, s0, _ = score_slices(h)[0 if part == 0 else 1]
                s0 += P * (part == 2)
                last = nc.tensor.transpose(turn_bank(A, k, part)[:, h * P:(h + 1) * P],
                                           buf[k % 2][:, s0:s0 + P], ident[:])
            last.then_inc(A["pt_full"], 1)

        def split_hi(act, A, n, k, part, PTh):
            j = 3 * k + part
            act.wait_ge(A["pt_full"], 3 * n + j + 1)
            nc.scalar.activation(PTh[:, part, :], turn_bank(A, k, part)[:], ACT.Copy).then_inc(A["pth_ready"], 1)

        def split_lo(v, A, n, k, part, PTh, PTl):
            j = 3 * k + part
            v.wait_ge(A["pth_ready"], 3 * n + j + 1)
            nc.vector.tensor_tensor(PTl[:, part, :], turn_bank(A, k, part)[:], PTh[:, part, :].bitcast(F32),
                                    ALU.subtract).then_inc(A["ptl_ready"], 1)

        def wait_moved(eng, n, k):
            b = k % B
            if b % 2 == 0 and (k >= B or not at_start(n)):
                eng.wait_ge(out_moved[b // 2], (n + k - b) * (GRP * 16 // B))

        def read_out(eng, n, k, qt, copy):
            b, use = k % B, 2 * k + qt
            ringO0.wait_full(eng, use, n)
            ringO0.freed(copy(Of[:, :, b * S + qt * P:b * S + (qt + 1) * P],
                              ringO0.bank(use)[0:HD0, :].rearrange("p (h q) -> p h q", h=GRP)), use)

        block = root.enter_context(nc.Block())

        UX, UK, UV, UQ, UVT, UW, UA_END = 0, 8, 10, 12, 20, 22, 26
        GP = NKV // 2
        UNITS = 2 * B
        RVK, RVT, RQ, RP = 0, 4, 6, 14
        RPV = [[RP, RP + 1]] + [[RP + 4 * b - 1, RP + 4 * b + 1] for b in range(1, B)]
        ROP = [[RP + 4 * b + 2, RP + 4 * b + 4] for b in range(B - 1)] + [[RP + 4 * B - 2, RP + 4 * B - 1]]
        RL = 30
        TURNS = RL // 3

        @block.sync
        def _(sp):
            for i in range(4):
                sp.dma_start(X[:, 2 * i:2 * i + 2, :], x_v[:, 2 * i:2 * i + 2, :]).then_inc(x_loaded[i], 16)
                if i == 0:
                    sp.dma_start(ident[:], ident_in).then_inc(ident_loaded, 16)
                    sp.dma_start(W0raw[:, :, 4 * P:5 * P], rows(wk0)).then_inc(w0_loaded, 16)
                    sp.dma_start(W0raw[:, :, 5 * P:6 * P], rows(wv0)).then_inc(w0_loaded, 16)
                    sp.dma_start(W0raw[:, :, 0:4 * P], rows(wq0)).then_inc(w0_loaded, 16)
            sp.dma_start(bq_t[:], bq0.rearrange("(c p) -> p c", p=P), allow_slow_non_contiguous=True).then_inc(biases_loaded, 16)
            sp.dma_start(bk_t[:], bk0.rearrange("(p a) -> p a", a=1), allow_slow_non_contiguous=True).then_inc(biases_loaded, 16)
            sp.dma_start(bv_t[:], bv0.rearrange("(p a) -> p a", a=1), allow_slow_non_contiguous=True).then_inc(biases_loaded, 16)
            sp.dma_start(qv[:], q_vals.rearrange("(c p) b k -> p c (b k)", p=P)).then_inc(q_loaded, 16)
            sp.dma_start(qs[:], q_scales.rearrange("(c p) b -> p c b", p=P)).then_inc(q_loaded, 16)
            sp.dma_start(bo_b[:], bo0.rearrange("(a n) -> a n", a=1).partition_broadcast(P)
                         .rearrange("p a n -> p (a n)")).then_inc(post_loaded, 16)
            sp.dma_start(fb_b[:], ffn_bias.rearrange("(a n) -> a n", a=1).partition_broadcast(P)
                         .rearrange("p a n -> p (a n)")).then_inc(post_loaded, 16)
            sp.dma_start(mask[:], mask_in).then_inc(consts_loaded, 16)
            sp.dma_start(dist[:], dist_in).then_inc(consts_loaded, 16)
            sp.dma_start(slopes[:], slopes_in).then_inc(consts_loaded, 16)

            def stack(pair, par, prefetch=True):
                base, src = 64 * par, 64 * par
                for h in range(GRP):
                    for r, q in enumerate((Qh, Qh, Ql, Ql)):
                        sp.dma_start(QS[base + 16 * r:base + 16 * (r + 1), h, :].bitcast(F32),
                                     q[src + 16 * h:src + 16 * (h + 1), bass.ds(pair, 1), :]
                                     .rearrange("p a t -> p (a t)").bitcast(F32)).then_inc(qs_loaded[par], 16)

            def stack_k(g, par):
                base = 64 * par
                for r, k in enumerate((Kh, Kl, Kh, Kl)):
                    sp.dma_start(KS[base + 16 * r:base + 16 * (r + 1), :].bitcast(F32),
                                 k[16 * g:16 * (g + 1), :].bitcast(F32)).then_inc(qs_loaded[par], 16)

            for par in range(2):
                sp.wait_ge(qkl_ready, 4)
                stack(0, par)
                stack_k(par, par)

            def move_out(pair, par, half):
                cols = slice(half * HALF, (half + 1) * HALF)
                for h in range(GRP):
                    d0 = 64 * par + 16 * h
                    sp.dma_start(attn[d0:d0 + 16, pair, cols], Of[:, h, cols]).then_inc(out_moved[half], 16)

            for pair in range(GP):
                for par in range(2):
                    n = UNITS * pair + B * par
                    if pair + 1 < GP:
                        sp.wait_ge(A0["scores_read"], 3 * (n + B))
                        if pair == 0:
                            sp.wait_ge(qkl_ready, 10)
                        stack(pair + 1, par)
                        stack_k(2 * (pair + 1) + par, par)
                    if pair == 0 and par == 0:
                        sp.wait_ge(vf_ready, 2)
                        sp.wait_ge(wfl_ready, KC)
                        sp.dma_start(Wo0raw[:], rows(wo0)).then_inc(wo0_loaded, 16)
                    for half in range(2):
                        for bank in range(2):
                            sp.wait_ge(ringO0.free[bank], n + (half + 1) * B // 2)
                        move_out(pair, par, half)
            def load_w1(g):
                sp.dma_start(W1raw[:, :, 0:4 * P], wqkv_v[:, :, bass.ds(g * 4 * P, 4 * P)]).then_inc(w1_loaded, 16)
                sp.dma_start(W1raw[:, :, 4 * P:5 * P],
                             wqkv_v[:, :, bass.ds(g * P + QCOLS, P)]).then_inc(w1_loaded, 16)
                sp.dma_start(W1raw[:, :, 5 * P:6 * P],
                             wqkv_v[:, :, bass.ds(g * P + QCOLS + KVC, P)]).then_inc(w1_loaded, 16)

            load_w1(0)
            ringC.wait_done(sp, POST_USES)
            for half in range(2):
                sp.dma_start(codes_i[half * 64:(half + 1) * 64, :],
                             codes.rearrange("(r n) -> r n", n=DM // 4)).then_inc(codes_loaded, 16)

            sp.dma_start(Woraw[:], wo_v[:, 0:GRP, :]).then_inc(wo1_loaded, 16)
            sp.wait_ge(w1_split, 1)
            load_w1(1)
            with sp.Fori(1, NKV - 1) as g:
                sp.wait_ge(wo1_split, g)
                sp.dma_start(Woraw[:], wo_v[:, bass.ds(g * GRP, GRP), :]).then_inc(wo1_loaded, 16)
                sp.wait_ge(w1_split, g + 1)
                load_w1(g + 1)
            sp.wait_ge(wo1_split, NKV - 1)
            sp.dma_start(Woraw[:], wo_v[:, (NKV - 1) * GRP:NKV * GRP, :]).then_inc(wo1_loaded, 16)

            for t in range(TILES):
                sp.wait_ge(xn_ready, SCALED["scale4", t])
                sp.dma_start(out_v[:, t, :], X[:, t, :]).then_inc(stored, 16)
            sp.wait_ge(stored, 16 * TILES)

        @block.gpsimd
        def _(pool):
            nc.gpsimd.memset(eps[:], EPS).then_inc(eps_ready, 1)

            def stage_v(pair, par):
                nc.gpsimd.tensor_copy(VS[:, par], Vf[:, :, bass.ds((pair * 2 + par) * HD0, HD0)])\
                  .then_inc(vs_ready, 1)

            hold(pool, vf_ready, 2)
            pool.wait_ge(post_loaded, 32)
            hold(pool, wfl_ready, KC)
            stage_v(0, 0)
            stage_v(0, 1)

            def attention_pair(pair, last):
                n = UNITS * pair
                for k in range(UNITS):
                    softmax_norm(pool, A0, n, k, Sb0)
                    if at_start(pair):
                        nc.gpsimd.tensor_tensor(X[:, k, :], X[:, k, :], bo_b[:], ALU.add).then_inc(bias_added, 1)
                    if last and k < KC:
                        if k == 0:
                            pool.wait_ge(wo0_loaded, 16)
                        nc.gpsimd.tensor_copy(Wo0h[:, k, :], Wo0raw[:, k, :]).then_inc(wo0h_ready, 1)
                        pool.wait_ge(wo0h_ready, k + 1)
                        nc.gpsimd.tensor_tensor(Wo0l[:, k, :], Wo0raw[:, k, :], Wo0h[:, k, :].bitcast(F32),
                                                ALU.subtract).then_inc(wo0_ready, 1)
                    if k % B == 0 and (k and not last or not k and not at_start(pair)):
                        hold(pool, ringO0.free[1], n + k)
                        stage_v(*((pair + 1, 0) if k else (pair, 1)))

            attention_pair(0, False)
            with pool.Fori(1, GP - 1) as pair:
                attention_pair(pair, False)
            attention_pair(GP - 1, True)

            def split_w1(g, c0, c1, first, count):
                if first:
                    hold(pool, w1_loaded, (g + 1) * 48)
                nc.gpsimd.tensor_copy(W1h[:, c0:c1, :], W1raw[:, c0:c1, :]).then_inc(w1_step, 1)
                hold(pool, w1_step, g * 4 + count)
                last = nc.gpsimd.tensor_tensor(W1l[:, c0:c1, :], W1raw[:, c0:c1, :],
                                               W1h[:, c0:c1, :].bitcast(F32), ALU.subtract)
                if c1 == KC:
                    last.then_inc(w1_split, 1)

            chunk = 0
            for what, t, use, i, before in POST:
                if what == "scale1":
                    pool.wait_ge(xn_ready, SCALED[what, t])
                    nc.gpsimd.tensor_tensor(Z[:, t, :], X[:, t, :], fb_b[:], ALU.add).then_inc(z_ready, 1)
                    if chunk < KC:
                        split_w1(0, chunk, chunk + 1, chunk == 0, chunk + 1)
                        chunk += 1

            def group(g, last):
                n = B * g
                hold(pool, wo1_loaded, (g + 1) * 16)
                if not at_start(g):
                    hold(pool, x_added, g * 2 * B)
                nc.gpsimd.tensor_copy(Woh[:], Woraw[:]).then_inc(wo1_step, 1)
                hold(pool, wo1_step, g + 1)
                nc.gpsimd.tensor_tensor(Wol[:], Woraw[:], Woh[:].bitcast(F32), ALU.subtract).then_inc(wo1_split, 1)
                if last:
                    hold(pool, codes_loaded, 32)
                    nc.gpsimd.tensor_copy(codes_f[:], codes_i[:].bitcast(I8)).then_inc(codes_ready, 1)

                def split_chunks(*chunks):
                    if not last:
                        for c in chunks:
                            split_w1(g + 1, c, c + 1, c == 0, c + 1)

                softmax_norm(pool, A1, n, 0, Sb1)
                softmax_norm(pool, A1, n, 1, Sb1)
                if not last:
                    hold(pool, qt_ready, 8 * g + 8)
                split_chunks(0)
                softmax_norm(pool, A1, n, 2, Sb1)
                split_chunks(1, 2)
                softmax_norm(pool, A1, n, 3, Sb1)
                split_chunks(3)

            ringC.wait_done(pool, POST_USES)
            group(0, False)
            with pool.Fori(1, NKV - 1) as g:
                group(g, False)
            group(NKV - 1, True)

        @block.scalar
        def _(act):
            act.wait_ge(w0_loaded, 48)
            for c in range(KC):
                nc.scalar.activation(W0h[:, c, :], W0raw[:, c, :], ACT.Copy).then_inc(w0h_ready, 1)
            for t in range(TILES):
                ringA.wait_full(act, UX + t)
                nc.scalar.activation(XTh[:, :, t * P:(t + 1) * P],
                                     ringA.bank(UX + t)[:].rearrange("p (c t) -> p c t", c=KC),
                                     ACT.Copy).then_inc(xh_ready, 1)
            act.wait_ge(biases_loaded, 48)

            def biased(use, j, bias, scale):
                ringA.wait_full(act, use)
                if j >= 2:
                    act.wait_ge(qkl_ready, j - 1)
                ringA.freed(nc.scalar.activation(QKf[:, j % 2, :], ringA.bank(use)[:], ACT.Identity,
                                                 bias=bias, scale=scale), use)

            for j in range(2):
                biased(UK + j, j, bk_t[:, 0:1], 1.0)
            for j in range(2):
                ringA.wait_full(act, UV + j)
                ringA.freed(nc.scalar.activation(VTf[:, j * HALF:(j + 1) * HALF], ringA.bank(UV + j)[:],
                                                 ACT.Identity, bias=bv_t[:, 0:1]), UV + j)
            act.wait_ge(bqs_ready, 1)
            for j in range(8):
                biased(UQ + j, 2 + j, bq_s[:, j // 2:j // 2 + 1], SCALE0)
            for c in range(KC):
                ringA.wait_full(act, UW + c)
                nc.scalar.activation(WFh[:, :, c * P:(c + 1) * P],
                                     ringA.bank(UW + c)[:].rearrange("p (c t) -> p c t", c=KC),
                                     ACT.Copy).then_inc(wfh_ready, 1)

            def attention_pair(pair, last):
                n = UNITS * pair
                for k in range(UNITS):
                    act.wait_ge(A0["pt_full"], 3 * (n + k) + 1)
                    nc.scalar.activation(PT0[:, 0, :], turn_bank(A0, k, 0)[:], ACT.Copy).then_inc(pt0_act, 1)
                    if k + 1 < UNITS or not last:
                        softmax_exp(act, A0, n, k + 1, 1, Sb0, 1.0)
                        softmax_exp(act, A0, n, k + 1, 2, Sb0, 1.0)
                    if k + 2 < UNITS or not last:
                        softmax_exp(act, A0, n, k + 2, 0, Sb0, 1.0)
                    wait_moved(act, n, k)
                    read_out(act, n, k, 0, lambda dst, src: nc.scalar.activation(dst, src, ACT.Copy))

            for k, bank in ((0, 0), (0, 1), (0, 2), (1, 0)):
                softmax_exp(act, A0, 0, k, bank, Sb0, 1.0)
            attention_pair(0, False)
            with act.Fori(1, GP - 1) as pair:
                attention_pair(pair, False)
            attention_pair(GP - 1, True)

            act.wait_ge(eps_ready, 1)

            def std_of(i):
                act.wait_ge(ln_dve, 2 * i + 2)
                nc.scalar.activation(std[:, i % 4:i % 4 + 1], moments[:, i % 4, 1:2], ACT.Sqrt,
                                     bias=eps[:, 0:1]).then_inc(std_ready, 1)

            def scale_of(what, i, t, y):
                act.wait_ge(rec_ready, SCALED[what, t])
                nc.scalar.activation(X[:, t, :], y, ACT.Identity, bias=shift[:, i % 4:i % 4 + 1],
                                     scale=rstd[:, i % 4:i % 4 + 1]).then_inc(xn_ready, 1)

            def hi_of(use, dst, done):
                ringC.wait_full(act, use)
                nc.scalar.activation(dst, ringC.bank(use)[:].rearrange("p (c t) -> p c t", c=KC),
                                     ACT.Copy).then_inc(done, 1)

            proj_use = {t: use for what, t, use, _, _ in POST if what == "proj"}
            for what, t, use, i, before in POST:
                if what == "attn":
                    if t % (TILES // 2) == 0:
                        act.wait_ge(out_moved[t // (TILES // 2)], 16 * GRP * NKV)
                    if t >= 2:
                        ringC.wait_full(act, proj_use[t - 2])
                    nc.scalar.activation(ATh[:, t % 2], attn[:, :, t * P:(t + 1) * P], ACT.Copy)\
                      .then_inc(ath_ready, 1)
                elif what in ("norm1", "norm2"):
                    std_of(i)
                elif what in ("scale1", "scale2"):
                    scale_of(what, i, t, Y[:, i % 2, :])
                elif what == "turn1":
                    hi_of(use, X1h[:, t % 2], x1h_ready)
                elif what == "turn2":
                    hi_of(use, XTh[:, :, t * P:(t + 1) * P], x2h_ready)

            def table(g):
                for h in range(GRP):
                    last = nc.scalar.activation(tab[:, h, :], dist[:], ACT.Copy,
                                                scale=slopes[:, bass.ds(g * GRP + h, 1)])
                last.then_inc(tab_ready, 1)

            def q_out1(g, j):
                use = RQ + j
                ringL.wait_full(act, use, g * TURNS)
                h, half = j % GRP, j // GRP
                nc.scalar.activation(QT[:, h, half * HALF:(half + 1) * HALF], ringL.bank(use)[:],
                                     ACT.Copy).then_inc(qt_ready, 1)

            def group(g, last):
                n = B * g
                for j in range(2):
                    ringL.wait_full(act, RVT + j, g * TURNS)
                    nc.scalar.activation(Vh[:, 4 * j:4 * j + 4, :],
                                         ringL.bank(RVT + j)[:].rearrange("p (t d) -> p t d", t=4),
                                         ACT.Copy).then_inc(vh_ready, 1)
                def exps(b, bank):
                    softmax_exp(act, A1, n, b, bank, Sb1, SCALE1)

                def out_hi(b, qt):
                    use = RPV[b][qt]
                    ringL.wait_full(act, use, g * TURNS)
                    nc.scalar.activation(OTh[:, qt], ringL.bank(use)[:].rearrange("p (h q) -> p h q", h=GRP),
                                         ACT.Copy).then_inc(oth_ready, 1)

                for j in range(5):
                    q_out1(g, j)
                for bank in range(3):
                    exps(0, bank)
                q_out1(g, 5)
                q_out1(g, 6)
                for bank in range(3):
                    exps(1, bank)
                split_hi(act, A1, n, 0, 0, PTh1)
                split_hi(act, A1, n, 0, 1, PTh1)
                q_out1(g, 7)
                split_hi(act, A1, n, 0, 2, PTh1)
                out_hi(0, 0)
                exps(2, 0)
                exps(2, 1)
                out_hi(0, 1)
                exps(2, 2)
                for b in range(1, B):
                    split_hi(act, A1, n, b, 0, PTh1)
                    split_hi(act, A1, n, b, 1, PTh1)
                    if last and b >= 2:
                        tail(2 * b - 3)
                    split_hi(act, A1, n, b, 2, PTh1)
                    out_hi(b, 0)
                    if last and b >= 2:
                        tail(2 * b - 2)
                    out_hi(b, 1)
                    if b == 1:
                        for bank in range(3):
                            exps(3, bank)
                        if last:
                            tail(0)
                if last:
                    tail(*range(5, TAIL_SLOTS))
                else:
                    act.wait_ge(A1["scores_read"], 3 * (n + B))
                    table(g + 1)

            def tail(*slots):
                for what, t, use, i, before in tail_steps(slots):
                    if what in ("norm3", "norm4"):
                        std_of(NORMS + i)
                    elif what in ("scale3", "scale4"):
                        scale_of(what, NORMS + i, t, X[:, t, :])
                    elif what == "turn":
                        ringF.wait_full(act, use)
                        nc.scalar.activation(FTh[:, t % 2, :], ringF.bank(use)[:, 0:P], ACT.Copy)\
                          .then_inc(fh_ready, 1)

            ringC.wait_done(act, POST_USES)
            table(0)
            group(0, False)
            with act.Fori(1, NKV - 1) as g:
                group(g, False)
            group(NKV - 1, True)

        @block.vector
        def _(v):
            v.wait_ge(biases_loaded, 48)
            nc.vector.tensor_scalar(bq_s[:], bq_t[:], SCALE0, None, ALU.mult).then_inc(bqs_ready, 1)
            for c in range(KC):
                v.wait_ge(w0h_ready, c + 1)
                nc.vector.tensor_tensor(W0l[:, c, :], W0raw[:, c, :], W0h[:, c, :].bitcast(F32),
                                        ALU.subtract).then_inc(w0l_ready, 1)
            for t in range(TILES):
                v.wait_ge(xh_ready, t + 1)
                ins = nc.vector.tensor_tensor(XTl[:, :, t * P:(t + 1) * P],
                                              ringA.bank(UX + t)[:].rearrange("p (c t) -> p c t", c=KC),
                                              XTh[:, :, t * P:(t + 1) * P].bitcast(F32), ALU.subtract)
                ringA.freed(ins, UX + t)
            v.wait_ge(q_loaded, 32)
            nc.vector.tensor_scalar(qw[:], qv[:], -128.0, None, ALU.add).then_inc(deq_step, 1)
            v.wait_ge(deq_step, 1)
            for c in range(KC):
                w = qw[:, c, :].rearrange("p (b k) -> p b k", k=32)
                nc.vector.tensor_tensor(w, w, qs[:, c, :].unsqueeze(2).broadcast_to([P, 16, 32]),
                                        ALU.mult).then_inc(deq_step, 1)

            def split_qk(j):
                hi, lo = (Kh, Kl) if j < 2 else (Qh[:, (j - 2) // 2], Ql[:, (j - 2) // 2])
                cols = slice((j % 2) * HALF, (j % 2 + 1) * HALF)
                use = UK + j if j < 2 else UQ + j - 2
                v.wait_ge(ringA.free[use % 4], use // 4 + 1)
                nc.vector.tensor_copy(hi[:, cols], QKf[:, j % 2, :]).then_inc(qkh_ready, 1)
                v.wait_ge(qkh_ready, j + 1)
                nc.vector.tensor_tensor(lo[:, cols], QKf[:, j % 2, :], hi[:, cols].bitcast(F32),
                                        ALU.subtract).then_inc(qkl_ready, 1)

            for j in range(10):
                split_qk(j)
            for j in range(2):
                ringA.wait_full(v, UVT + j)
                nc.vector.tensor_copy(Vf[:, 4 * j:4 * j + 4, :],
                                      ringA.bank(UVT + j)[:].rearrange("p (t d) -> p t d", t=4))\
                  .then_inc(vf_ready, 1)
            for c in range(KC):
                v.wait_ge(wfh_ready, c + 1)
                nc.vector.tensor_tensor(WFl[:, :, c * P:(c + 1) * P],
                                        ringA.bank(UW + c)[:].rearrange("p (c t) -> p c t", c=KC),
                                        WFh[:, :, c * P:(c + 1) * P].bitcast(F32), ALU.subtract)\
                  .then_inc(wfl_ready, 1)

            def mask_of(h, qt):
                return mask[:, 0:P] if qt == 0 else mask[:, P:3 * P]

            def attention_pair(pair, last):
                n = UNITS * pair
                for k in range(UNITS):
                    ahead = k + 2 < UNITS or not last
                    if k + 1 < UNITS or not last:
                        softmax_rec(v, A0, n, k + 1, 0)
                    if k or not at_start(n):
                        outs0(n, k - 1)
                    if ahead:
                        hold(v, A0["pt_full"], 3 * (n + k) + 1)
                        softmax_max(v, A0, n, k + 2, Sb0, mask_of, 1.0, [0])
                    for part in (1, 2):
                        v.wait_ge(A0["pt_full"], 3 * (n + k) + part + 1)
                        nc.vector.tensor_copy(PT0[:, part, :], turn_bank(A0, k, part)[:])\
                          .then_inc(pt0_dve, 1)
                    if k + 1 < UNITS or not last:
                        softmax_rec(v, A0, n, k + 1, 1)
                        softmax_rec(v, A0, n, k + 1, 2)
                    if ahead:
                        softmax_max(v, A0, n, k + 2, Sb0, mask_of, 1.0, [1, 2])

            def outs0(n, k):
                wait_moved(v, n, k)
                read_out(v, n, k, 1, lambda dst, src: nc.vector.tensor_copy(dst, src))

            v.wait_ge(consts_loaded, 48)
            softmax_max(v, A0, 0, 0, Sb0, mask_of, 1.0)
            softmax_max(v, A0, 0, 1, Sb0, mask_of, 1.0)
            for bank in range(3):
                softmax_rec(v, A0, 0, 0, bank)
            attention_pair(0, False)
            with v.Fori(1, GP - 1) as pair:
                attention_pair(pair, False)
            attention_pair(GP - 1, True)
            outs0(UNITS * (GP - 1), UNITS - 1)

            def norm(i, t, y):
                k = i % 4
                nc.vector.bn_stats(stats[:, k, :], y).then_inc(ln_dve, 1)
                v.wait_ge(ln_dve, 2 * i + 1)
                nc.vector.bn_aggr(moments[:, k, :], stats[:, k, :]).then_inc(ln_dve, 1)

            def normalize(what, i, t):
                k, done = i % 4, SCALED[what, t]
                v.wait_ge(std_ready, i + 1)
                nc.vector.reciprocal(rstd[:, k:k + 1], std[:, k:k + 1]).then_inc(rstd_ready, 1)
                v.wait_ge(rstd_ready, done)
                nc.vector.scalar_tensor_tensor(shift[:, k:k + 1], moments[:, k, 0:1], -1.0, rstd[:, k:k + 1],
                                               ALU.mult, ALU.mult).then_inc(rec_ready, 1)

            for what, t, use, i, before in POST:
                if what == "attn":
                    v.wait_ge(ath_ready, t + 1)
                    nc.vector.tensor_tensor(ATl[:, t % 2], attn[:, :, t * P:(t + 1) * P], ATh[:, t % 2].bitcast(F32),
                                            ALU.subtract).then_inc(atl_ready, 1)
                elif what in ("norm1", "norm2"):
                    y = Y[:, i % 2, :]
                    if what == "norm1":
                        v.wait_ge(bias_added, t + 1)
                    else:
                        v.wait_ge(z_ready, t + 1)
                    if i >= 2:
                        v.wait_ge(xn_ready, SCALED[NAMES[i - 2]])
                    ringC.wait_full(v, before)
                    ringC.freed(nc.vector.tensor_tensor(y, ringC.bank(before)[:],
                                                        (X if what == "norm1" else Z)[:, t, :], ALU.add), before)
                    ringC.wait_read(v, before)
                    norm(i, t, y)
                elif what in ("scale1", "scale2"):
                    normalize(what, i, t)
                elif what == "turn1":
                    v.wait_ge(x1h_ready, t + 1)
                    ringC.freed(nc.vector.tensor_tensor(
                        X1l[:, t % 2], ringC.bank(use)[:].rearrange("p (c t) -> p c t", c=KC),
                        X1h[:, t % 2].bitcast(F32), ALU.subtract), use)
                elif what == "turn2":
                    v.wait_ge(x2h_ready, t + 1)
                    ringC.freed(nc.vector.tensor_tensor(
                        XTl[:, :, t * P:(t + 1) * P], ringC.bank(use)[:].rearrange("p (c t) -> p c t", c=KC),
                        XTh[:, :, t * P:(t + 1) * P].bitcast(F32), ALU.subtract), use)

            def tab_of(h, qt):
                return tab[:, h, 0:P] if qt == 0 else tab[:, h, P:3 * P]

            def add_out(g, b, qt):
                use = ROP[b][qt]
                ringL.wait_full(v, use, g * TURNS)
                t = 2 * b + qt
                nc.vector.tensor_tensor(X[:, t, :], ringL.bank(use)[:], X[:, t, :], ALU.add).then_inc(x_added, 1)

            def out_lo(g, b, qt):
                use = RPV[b][qt]
                v.wait_ge(oth_ready, 2 * (B * g + b) + qt + 1)
                nc.vector.tensor_tensor(
                    OTl[:, qt], ringL.bank(use)[:].rearrange("p (h q) -> p h q", h=GRP),
                    OTh[:, qt].bitcast(F32), ALU.subtract).then_inc(otl_ready, 1)

            def group(g, last):
                n = B * g

                def maxes(b):
                    softmax_max(v, A1, n, b, Sb1, tab_of, SCALE1)

                def recs(b):
                    for bank in range(3):
                        softmax_rec(v, A1, n, b, bank)

                for j in range(2):
                    for vk, (dst, done) in enumerate(((VT, vt1_ready), (KT, kt_ready))):
                        use = RVK + 2 * j + vk
                        ringL.wait_full(v, use, g * TURNS)
                        nc.vector.tensor_copy(dst[:, j * HALF:(j + 1) * HALF], ringL.bank(use)[:]).then_inc(done, 1)
                for j in range(2):
                    v.wait_ge(vh_ready, 2 * g + j + 1)
                    nc.vector.tensor_tensor(
                        Vl[:, 4 * j:4 * j + 4, :], ringL.bank(RVT + j)[:].rearrange("p (t d) -> p t d", t=4),
                        Vh[:, 4 * j:4 * j + 4, :].bitcast(F32), ALU.subtract).then_inc(vl_ready, 1)
                v.wait_ge(tab_ready, g + 1)
                maxes(0)
                recs(0)
                maxes(1)
                recs(1)
                split_lo(v, A1, n, 0, 0, PTh1, PTl1)
                split_lo(v, A1, n, 0, 1, PTh1, PTl1)
                split_lo(v, A1, n, 0, 2, PTh1, PTl1)
                maxes(2)
                out_lo(g, 0, 0)
                softmax_rec(v, A1, n, 2, 0)
                softmax_rec(v, A1, n, 2, 1)
                out_lo(g, 0, 1)
                softmax_rec(v, A1, n, 2, 2)
                for b in range(1, B):
                    split_lo(v, A1, n, b, 0, PTh1, PTl1)
                    split_lo(v, A1, n, b, 1, PTh1, PTl1)
                    if last and b >= 2:
                        tail(2 * b - 3)
                    add_out(g, b - 1, 0)
                    split_lo(v, A1, n, b, 2, PTh1, PTl1)
                    out_lo(g, b, 0)
                    if last and b >= 2:
                        tail(2 * b - 2)
                    add_out(g, b - 1, 1)
                    out_lo(g, b, 1)
                    if b == 1:
                        maxes(3)
                        recs(3)
                        if last:
                            tail(0)
                if last:
                    tail(5)
                add_out(g, B - 1, 0)
                if last:
                    tail(6)
                add_out(g, B - 1, 1)
                if last:
                    tail(*range(7, TAIL_SLOTS))

            def tail(*slots):
                for what, t, use, i, before in tail_steps(slots):
                    if what == "norm3":
                        v.wait_ge(x_added, 2 * B * (NKV - 1) + t + 1)
                        norm(NORMS + i, t, X[:, t, :])
                    elif what in ("scale3", "scale4"):
                        normalize(what, NORMS + i, t)
                    elif what == "turn":
                        v.wait_ge(fh_ready, t + 1)
                        ringF.freed(nc.vector.tensor_tensor(
                            FTl[:, t % 2, :], ringF.bank(use)[:, 0:P], FTh[:, t % 2, :].bitcast(F32),
                            ALU.subtract), use)
                    elif what == "norm4":
                        ringF.wait_full(v, before)
                        v.wait_ge(xn_ready, SCALED["scale3", t])
                        ringF.freed(nc.vector.tensor_tensor(X[:, t, :], ringF.bank(before)[:], X[:, t, :], ALU.add),
                                    before)
                        ringF.wait_read(v, before)
                        norm(NORMS + i, t, X[:, t, :])

            group(0, False)
            with v.Fori(1, NKV - 1) as g:
                group(g, False)
            group(NKV - 1, True)

        @block.tensor
        def _(pe):
            def three(out_ap, lh, ll, rh, rl, first, last):
                nc.tensor.matmul(out_ap, lh, rh, start=first, stop=False)
                nc.tensor.matmul(out_ap, lh, rl, start=False, stop=False)
                return nc.tensor.matmul(out_ap, ll, rh, start=False, stop=last)

            pe.wait_ge(ident_loaded, 16)
            for t in range(TILES):
                pe.wait_ge(x_loaded[t // 2], 16)
                ringA.wait_free(pe, UX + t)
                for c in range(KC):
                    last = nc.tensor.transpose(ringA.bank(UX + t)[:, c * P:(c + 1) * P],
                                               X[:, t, c * P:(c + 1) * P], ident[:])
                ringA.filled(last, UX + t)

            def project0(use, m, half):
                ringA.wait_free(pe, use)
                cols = slice(half * HALF, (half + 1) * HALF)
                for c in range(KC):
                    last = three(ringA.bank(use)[:], W0h[:, c, m * P:(m + 1) * P], W0l[:, c, m * P:(m + 1) * P],
                                 XTh[:, c, cols], XTl[:, c, cols], c == 0, c == KC - 1)
                ringA.filled(last, use)

            pe.wait_ge(w0l_ready, KC)
            for b in range(4):
                pe.wait_ge(ringA.free[b], 2)
            for half in range(2):
                project0(UK + half, 4, half)
            for half in range(2):
                project0(UV + half, 5, half)
            for m in range(4):
                for half in range(2):
                    project0(UQ + 2 * m + half, m, half)
            for j in range(2):
                ringA.wait_free(pe, UVT + j)
                pe.wait_ge(ringA.free[(UV + j) % 4], (UV + j) // 4 + 1)
                for t in range(4):
                    last = nc.tensor.transpose(ringA.bank(UVT + j)[:, t * P:(t + 1) * P],
                                               VTf[:, (4 * j + t) * P:(4 * j + t + 1) * P], ident[:])
                ringA.filled(last, UVT + j)
            pe.wait_ge(deq_step, 1 + KC)
            for c in range(KC):
                if c < 2:
                    ringA.wait_free(pe, UW + c)
                else:
                    pe.wait_ge(vf_ready, c - 1)
                for i in range(KC):
                    last = nc.tensor.transpose(ringA.bank(UW + c)[:, i * P:(i + 1) * P],
                                               qw[:, c, i * P:(i + 1) * P], ident[:])
                ringA.filled(last, UW + c)

            def scores0(n, k, pair):
                b, par = k % B, (k // B) % 2
                rows_ = slice(64 * par, 64 * par + 64)
                if b == 0:
                    pe.wait_ge(qs_loaded[par], (pair + 1) * 16 * 20)
                for bank in range(3):
                    if not at_start(n) or k:
                        pe.wait_ge(A0["scores_read"], 3 * (n + k) + bank - 2)
                    heads = range(GRP) if bank == 0 else range(2 * bank - 2, 2 * bank)
                    for h in heads:
                        qt = 0 if bank == 0 else 1
                        _, c0, _, w = score_slices(h)[qt]
                        last = nc.tensor.matmul(banks[bank][:, c0:c0 + w],
                                                QS[rows_, h, b * S + qt * P:b * S + (qt + 1) * P],
                                                KS[rows_, b * S:b * S + w], start=True, stop=True)
                    last.then_inc(A0["scores_ready"], 1)

            def values0(n, k, pair, qt):
                b, par = k % B, (k // B) % 2
                if b == 0 and qt == 0:
                    pe.wait_ge(vs_ready, 2 * pair + par + 1)
                u = 2 * k + qt
                ringO0.wait_free(pe, u, n)
                if qt == 0:
                    pe.wait_ge(pt0_act, n + k + 1)
                else:
                    pe.wait_ge(pt0_dve, 2 * (n + k) + 2)
                parts = [(0, 0)] if qt == 0 else [(1, 0), (2, 1)]
                for j, (part, kt) in enumerate(parts):
                    last = nc.tensor.matmul(ringO0.bank(u)[0:HD0, :], VS[:, par, 2 * b + kt, :],
                                            PT0[:, part, :], start=(j == 0), stop=(j == len(parts) - 1))
                ringO0.filled(last, u)

            def attention_pair(pair, last):
                n = UNITS * pair
                for k in range(UNITS):
                    transpose_probs(pe, A0, n, k, 0, Sb0)
                    if k or not at_start(n):
                        values0(n, k - 1, pair, 1)
                    if k + 2 < UNITS or not last:
                        scores0(n, k + 2, pair + (k + 2) // UNITS)
                    transpose_probs(pe, A0, n, k, 1, Sb0)
                    transpose_probs(pe, A0, n, k, 2, Sb0)
                    values0(n, k, pair, 0)

            pe.wait_ge(wfl_ready, KC)
            scores0(0, 0, 0)
            scores0(0, 1, 0)
            attention_pair(0, False)
            with pe.Fori(1, GP - 1) as pair:
                attention_pair(pair, False)
            attention_pair(GP - 1, True)
            values0(UNITS * (GP - 1), UNITS - 1, GP - 1, 1)

            def lwait(g, use):
                prev = use - len(ringL.banks)
                if prev < 0 and at_start(g):
                    return
                if prev < 0:
                    pe.wait_ge(*((otl_ready, 2 * B * g) if prev == -3 else (x_added, 2 * B * g + prev + 1)))
                elif prev < RVT:
                    pe.wait_ge((vt1_ready, kt_ready)[prev % 2], 2 * g + prev // 2 + 1)
                elif prev < RQ:
                    pe.wait_ge(vl_ready, 2 * g + prev - RVT + 1)
                elif prev < RP:
                    pe.wait_ge(qt_ready, 8 * g + prev - RQ + 1)
                else:
                    for b in range(B):
                        for qt in range(2):
                            if prev == RPV[b][qt]:
                                pe.wait_ge(otl_ready, 2 * (B * g + b) + qt + 1)
                            if prev == ROP[b][qt]:
                                pe.wait_ge(x_added, 2 * (B * g + b) + qt + 1)

            def project1(g, use, m, half):
                lwait(g, use)
                cols = slice(half * HALF, (half + 1) * HALF)
                for c in range(KC):
                    last = three(ringL.bank(use)[:], W1h[:, c, m * P:(m + 1) * P], W1l[:, c, m * P:(m + 1) * P],
                                 XTh[:, c, cols], XTl[:, c, cols], c == 0, c == KC - 1)
                ringL.filled(last, use)

            def project_vk(g, half, which=(0, 1)):
                for vk in which:
                    project1(g, RVK + 2 * half + vk, 5 - vk, half)

            pe.wait_ge(wo0_ready, KC)
            turned = {t: use for what, t, use, _, _ in POST if what == "turn2"}
            for what, t, i, _, before in POST:
                if what == "turn1" and t == TILES - 1:
                    pe.wait_ge(w1_split, 1)
                    for done in range(TILES // 2):
                        ringC.wait_read(pe, turned[done])
                    project_vk(0, 0, [0])
                if what == "turn2" and t == TILES - 2:
                    project_vk(0, 0, [1])
                if what == "proj":
                    pe.wait_ge(atl_ready, t + 1)
                    ringC.wait_free(pe, i)
                    for c in range(KC):
                        last = three(ringC.bank(i)[:], ATh[:, t % 2, c, :], ATl[:, t % 2, c, :],
                                     Wo0h[:, c, :], Wo0l[:, c, :], c == 0, c == KC - 1)
                    ringC.filled(last, i)
                elif what == "linear":
                    ringC.wait_read(pe, before)
                    ringC.wait_free(pe, i)
                    for c in range(KC):
                        last = three(ringC.bank(i)[:], X1h[:, t % 2, c, :], X1l[:, t % 2, c, :],
                                     WFh[:, c, :], WFl[:, c, :], c == 0, c == KC - 1)
                    ringC.filled(last, i)
                elif what in ("turn1", "turn2"):
                    pe.wait_ge(xn_ready, SCALED["scale" + what[-1], t])
                    ringC.wait_free(pe, i)
                    for c in range(KC):
                        last = nc.tensor.transpose(ringC.bank(i)[:, c * P:(c + 1) * P],
                                                   X[:, t, c * P:(c + 1) * P], ident[:])
                    ringC.filled(last, i)

            def scores1(g, b):
                n = B * g
                for bank in range(3):
                    if not at_start(n) or b:
                        pe.wait_ge(A1["scores_read"], 3 * (n + b) + bank - 2)
                    heads = range(GRP) if bank == 0 else range(2 * bank - 2, 2 * bank)
                    for h in heads:
                        qt = 0 if bank == 0 else 1
                        _, c0, _, w = score_slices(h)[qt]
                        last = nc.tensor.matmul(banks[bank][:, c0:c0 + w],
                                                QT[:, h, b * S + qt * P:b * S + (qt + 1) * P],
                                                KT[:, b * S:b * S + w], start=True, stop=True)
                    last.then_inc(A1["scores_ready"], 1)

            def values1(g, b, qt):
                n = B * g
                use = RPV[b][qt]
                lwait(g, use)
                pe.wait_ge(A1["ptl_ready"], 3 * (n + b) + (1 if qt == 0 else 3))
                parts = [(0, 0)] if qt == 0 else [(1, 0), (2, 1)]
                for j, (part, kt) in enumerate(parts):
                    last = three(ringL.bank(use)[:], Vh[:, 2 * b + kt, :], Vl[:, 2 * b + kt, :],
                                 PTh1[:, part, :], PTl1[:, part, :], j == 0, j == len(parts) - 1)
                ringL.filled(last, use)

            def output1(g, b, qt):
                use = ROP[b][qt]
                lwait(g, use)
                if b == 0 and qt == 0:
                    pe.wait_ge(wo1_split, g + 1)
                pe.wait_ge(otl_ready, 2 * (B * g + b) + qt + 1)
                for h in range(GRP):
                    last = three(ringL.bank(use)[:], OTh[:, qt, h, :], OTl[:, qt, h, :],
                                 Woh[:, h, :], Wol[:, h, :], h == 0, h == GRP - 1)
                ringL.filled(last, use)

            def group(g, last):
                n = B * g
                if at_start(g):
                    project_vk(g, 1)
                else:
                    pe.wait_ge(w1_split, g + 1)
                    project_vk(g, 0)
                    project_vk(g, 1)
                for j in range(2):
                    lwait(g, RVT + j)
                    pe.wait_ge(vt1_ready, 2 * g + j + 1)
                    for t in range(4):
                        ins = nc.tensor.transpose(ringL.bank(RVT + j)[:, t * P:(t + 1) * P],
                                                  VT[:, (4 * j + t) * P:(4 * j + t + 1) * P], ident[:])
                    ringL.filled(ins, RVT + j)
                for j in range(5):
                    project1(g, RQ + j, j % GRP, j // GRP)
                pe.wait_ge(qt_ready, 8 * g + 4)
                scores1(g, 0)
                project1(g, RQ + 5, 1, 1)
                project1(g, RQ + 6, 2, 1)
                scores1(g, 1)
                transpose_probs(pe, A1, n, 0, 0, Sb1)
                transpose_probs(pe, A1, n, 0, 1, Sb1)
                project1(g, RQ + 7, 3, 1)
                transpose_probs(pe, A1, n, 0, 2, Sb1)
                values1(g, 0, 0)
                pe.wait_ge(qt_ready, 8 * g + 8)
                scores1(g, 2)
                values1(g, 0, 1)
                for b in range(1, B):
                    transpose_probs(pe, A1, n, b, 0, Sb1)
                    transpose_probs(pe, A1, n, b, 1, Sb1)
                    if last and b >= 2:
                        tail(2 * b - 3)
                    output1(g, b - 1, 0)
                    transpose_probs(pe, A1, n, b, 2, Sb1)
                    values1(g, b, 0)
                    if last and b >= 2:
                        tail(2 * b - 2)
                    output1(g, b - 1, 1)
                    values1(g, b, 1)
                    if b == 1:
                        scores1(g, 3)
                        if last:
                            tail(0)
                if last:
                    tail(5)
                output1(g, B - 1, 0)
                if last:
                    tail(6)
                output1(g, B - 1, 1)
                if last:
                    tail(*range(7, TAIL_SLOTS))

            def tail(*slots):
                for what, t, i, _, before in tail_steps(slots):
                    if what == "turn":
                        pe.wait_ge(xn_ready, SCALED["scale3", t])
                        pe.wait_ge(A1["scores_read"], 3 * B * NKV)
                        ringF.wait_free(pe, i)
                        for c in range(KC):
                            last_ = nc.tensor.matmul(ringF.bank(i)[:, 0:P], X[:, t, c * P:(c + 1) * P], ident[:],
                                                     start=(c == 0), stop=(c == KC - 1))
                        ringF.filled(last_, i)
                    elif what == "codes":
                        pe.wait_ge(codes_ready, 1)
                        ringF.wait_read(pe, before)
                        ringF.wait_free(pe, i)
                        nc.tensor.matmul(ringF.bank(i)[:], FTh[:, t % 2, :], codes_f[:], start=True, stop=False)
                        ringF.filled(nc.tensor.matmul(ringF.bank(i)[:], FTl[:, t % 2, :], codes_f[:],
                                                      start=False, stop=True), i)

            ringC.wait_done(pe, POST_USES)
            group(0, False)
            with pe.Fori(1, NKV - 1) as g:
                group(g, False)
            group(NKV - 1, True)


_INS = ["L0_attn_x", "L0_attn_Wq", "L0_attn_bq", "L0_attn_Wk", "L0_attn_bk", "L0_attn_Wv", "L0_attn_bv",
        "L0_attn_Wo", "L0_attn_bo", "L0_ffn_q_scales", "L0_ffn_q_vals", "L0_ffn_bias", "L1_attn_w_qkv",
        "L1_attn_w_o", "L1_ffn_kernel"]


def kernel(**inputs):
    import numpy as _np
    import concourse.bacc as _bacc
    from concourse import mybir as _mybir
    from concourse.bass_utils import run_bass_kernel_spmd as _run

    nc = _bacc.Bacc("TRN2", target_bir_lowering=False, num_devices=1)
    arrays, args = {}, []

    def feed(name, a):
        arrays[name] = a
        args.append(nc.dram_tensor(name, a.shape, _mybir.dt.from_np(a.dtype), kind="ExternalInput").ap())

    for name in _INS:
        a = _np.ascontiguousarray(inputs[name])
        feed(f"in_{name}_dram", a.view(_np.int32) if a.dtype == _np.int8 else a)
    q = _np.arange(P)[:, None]
    rel = _np.concatenate([q - _np.arange(P)[None, :], q + P - _np.arange(S)[None, :]], axis=1)
    feed("identity", _np.eye(P, dtype=_np.float32))
    feed("mask_const", _np.where(rel >= 0, 0.0, -1e30).astype(_np.float32))
    feed("dist_const", _np.where(rel >= 0, -_np.sqrt(_np.maximum(rel, 0)) / SCALE1, -1e30).astype(_np.float32))
    slopes = (2.0 ** (-8.0 / (NKV * GRP))) ** _np.arange(1, NKV * GRP + 1, dtype=_np.float32)
    feed("slopes_const", _np.ascontiguousarray(_np.broadcast_to(slopes.astype(_np.float32), (P, NKV * GRP))))
    args.append(nc.dram_tensor("out_0_dram", (B, S, DM), _mybir.dt.float32, kind="ExternalOutput").ap())
    two_layers(nc, *args)
    r = _run(nc, [arrays], core_ids=[0])
    return r.results[0]["out_0_dram"]
```

```python
from contextlib import ExitStack

import concourse.bass as bass
from concourse import mybir

F32 = mybir.dt.float32
F32R = mybir.dt.float32r
I32 = mybir.dt.int32
I8 = mybir.dt.int8
ALU = mybir.AluOpType
ACT = mybir.ActivationFunctionType
AX = mybir.AxisListType

P = 128
B, S, DM = 4, 256, 512
TOK = B * S
TILES = TOK // P
KC = DM // P
HALF = TOK // 2
NKV, GRP = 8, 4
HD0 = 16
HD1 = 128
EPS = 1e-5
SCALE0 = 0.25
SCALE1 = float(HD1) ** -0.5
QCOLS = NKV * GRP * HD1
KVC = NKV * HD1
SP0 = GRP * P
SPC = SP0 + GRP * S
FLOOR = -3.0e38


def hold(eng, semaphore, count):
    eng.wait_ge(semaphore, count)
    eng.nop(nofuse=True)


class Ring:

    def __init__(self, banks, full, free):
        self.banks, self.full, self.free = banks, full, free

    def bank(self, n):
        return self.banks[n % len(self.banks)]

    def wait_free(self, eng, n, loop=0):
        turn = n // len(self.banks)
        if turn or not at_start(loop):
            eng.wait_ge(self.free[n % len(self.banks)], turn + loop)

    def wait_full(self, eng, n, loop=0):
        eng.wait_ge(self.full[n % len(self.banks)], n // len(self.banks) + 1 + loop)

    def wait_read(self, eng, n):
        eng.wait_ge(self.free[n % len(self.banks)], n // len(self.banks) + 1)

    def wait_done(self, eng, uses):
        for b in range(len(self.banks)):
            eng.wait_ge(self.free[b], (uses - b + len(self.banks) - 1) // len(self.banks))

    def filled(self, ins, n):
        ins.then_inc(self.full[n % len(self.banks)], 1)

    def freed(self, ins, n):
        ins.then_inc(self.free[n % len(self.banks)], 1)


USES = ("x", "k", "v", "q", "vt", "wf", "proj", "turn1", "linear", "turn2", "turn", "codes")


def steps(rows_):
    use = norm = 0
    uses, norms, out = {}, {}, []
    for what, t, takes in rows_:
        mine = number = None
        if what in USES:
            mine = uses[what, t] = use
            use += 1
        if what.startswith("norm"):
            number = norms[what[-1], t] = norm
            norm += 1
        if what.startswith("scale"):
            number = norms[what[-1], t]
        out.append((what, t, mine, number, uses.get((takes, t))))
    return out, use


def pipeline(slots, order):
    return [(what, s - lag, takes) for s in slots for what, lag, takes in order if 0 <= s - lag < TILES]


PHASE_A = [*[("x", t, 0) for t in range(TILES // 2)], ("w", 4, 0), ("k", 0, 0), ("w", 0, 0), ("v", 0, 0), ("w", 1, 0),
           ("q", 0, 0), ("w", 2, 0), ("x", 4, 1), ("q", 1, 0), ("w", 3, 0), ("x", 5, 1), ("q", 2, 0), ("x", 6, 1),
           ("x", 7, 1), ("q", 3, 0), ("deq", 0, 0), ("k", 0, 1), ("q", 0, 1), ("q", 1, 1), ("scores", 0, 0),
           ("q", 2, 1), ("q", 3, 1), ("wf", 0, 0), ("scores", 1, 0), ("v", 0, 1),
           ("wf", 1, 0), ("wf", 2, 0), ("wf", 3, 0), ("vt", 0, 0), ("vt", 0, 1)]
A_STEPS = [step for step in PHASE_A if step[0] in USES]
A_USE = {step: use for use, step in enumerate(A_STEPS)}
PIECES = [step for step in PHASE_A if step[0] in "kq"]

POST, POST_USES = steps(pipeline(range(-1, TILES + 4), [
    ("scale1", 1, None), ("norm2", 3, "linear"), ("scale2", 3, None), ("attn", -1, None), ("proj", 0, None),
    ("turn1", 1, None), ("turn2", 4, None), ("linear", 2, "turn1"), ("norm1", 0, "proj")]))
TAIL_ORDER = [("turn", 2, None), ("scale3", 1, None), ("scale4", 4, None), ("norm3", 0, None),
              ("codes", 3, "turn"), ("norm4", 3, "codes")]
TAIL_SLOTS = TILES + 4
TAIL, TAIL_USES = steps(pipeline(range(TAIL_SLOTS), TAIL_ORDER))


def tail_steps(slots):
    lag = {what: n for what, n, _ in TAIL_ORDER}
    return [step for step in TAIL if step[1] + lag[step[0]] in slots]


NORMS = 2 * TILES


def scaled(plan, base=0):
    return {(what, t): base + n + 1 for n, (what, t) in
            enumerate([(w, t) for w, t, _, _, _ in plan if w.startswith("scale")])}


NAMES = [("scale" + what[-1], t) for what, t, _, _, _ in POST if what.startswith("norm")]
SCALED = {**scaled(POST), **scaled(TAIL, NORMS)}


def at_start(n):
    return isinstance(n, int) and n == 0


def two_layers(nc, x_in, wq0, bq0, wk0, bk0, wv0, bv0, wo0, bo0, q_scales, q_vals, ffn_bias,
               w_qkv, w_o, codes, ident_in, mask_in, dist_in, slopes_in, out):
    root = ExitStack()
    with root:
        def sb(name, shape, dt=F32, scope=root):
            return scope.enter_context(nc.sbuf_tensor(name, shape, dt))

        def sem(name):
            return root.enter_context(nc.semaphore(name))

        X = sb("X", [P, TILES, DM])
        XTh = sb("XTh", [P, KC, TOK], F32R)
        XTl = sb("XTl", [P, KC, TOK], F32R)
        attn = XTh[:].bitcast(F32)
        ident = sb("ident", [P, P])
        dist = sb("dist", [P, 3 * P])
        slopes = sb("slopes", [P, NKV * GRP])
        stats = sb("stats", [P, 4, 6])
        moments = sb("moments", [P, 4, 2])
        std = sb("std", [P, 4])
        rstd = sb("rstd", [P, 4])
        shift = sb("shift", [P, 4])
        eps = sb("eps", [P, 1])
        rowmax = sb("rowmax", [P, 2, 2 * GRP])
        negmax = sb("negmax", [P, 2, 2 * GRP])
        rowsum = sb("rowsum", [P, 2, 2 * GRP])
        rowrec = sb("rowrec", [P, 2, 2 * GRP])
        bq_t = sb("bq_t", [P, KC])
        bq_s = sb("bq_s", [P, KC])
        bk_t = sb("bk_t", [P, 1])
        bv_t = sb("bv_t", [P, 1])
        keep = ExitStack()
        WFh = sb("WFh", [P, KC, DM], F32R, keep)
        WFl = sb("WFl", [P, KC, DM], F32R, keep)
        mask = sb("mask", [P, 3 * P], F32, keep)
        bo_b = sb("bo_b", [P, DM], F32, keep)
        fb_b = sb("fb_b", [P, DM], F32, keep)
        early = ExitStack()
        Qh = sb("Qh", [P, KC, TOK], F32R, early)
        Ql = sb("Ql", [P, KC, TOK], F32R, early)
        Kh = sb("Kh", [P, TOK], F32R, early)
        Kl = sb("Kl", [P, TOK], F32R, early)
        Vf = sb("Vf", [P, TILES, P], F32, early)
        QS = sb("QS", [P, GRP, TOK], F32R, early)
        KS = sb("KS", [P, TOK], F32R, early)
        proj = ExitStack()
        W0raw = sb("W0raw", [P, KC, 6 * P], F32, proj)
        W0h = sb("W0h", [P, KC, 6 * P], F32R, proj)
        W0l = sb("W0l", [P, KC, 6 * P], F32R, proj)
        QKf = sb("QKf", [P, 2, HALF], F32, proj)
        VTf = sb("VTf", [P, TOK], F32, proj)
        qv = sb("qv", [P, KC, DM], I32, proj)
        qw = sb("qw", [P, KC, DM], F32, proj)
        qs = sb("qs", [P, KC, 16], F32, proj)
        proj.close()
        att = ExitStack()
        Sb0 = [sb(f"Sb0_{i}", [P, SPC], F32, att) for i in range(2)]
        PT0 = sb("PT0", [P, 3, 4 * P], F32, att)
        Of = sb("Of", [HD0, GRP, TOK], F32, att)
        VS = sb("VS", [P, 2, TILES, HD0], F32, att)
        Wo0raw = sb("Wo0raw", [P, KC, DM], F32, att)
        Wo0h = sb("Wo0h", [P, KC, DM], F32R, att)
        Wo0l = sb("Wo0l", [P, KC, DM], F32R, att)
        att.close()
        early.close()
        post = ExitStack()
        Y = sb("Y", [P, 2, DM], F32, post)
        Z = sb("Z", [P, TILES, DM], F32, post)
        ATh = sb("ATh", [P, 2, KC, P], F32R, post)
        ATl = sb("ATl", [P, 2, KC, P], F32R, post)
        X1h = sb("X1h", [P, 2, KC, P], F32R, post)
        X1l = sb("X1l", [P, 2, KC, P], F32R, post)
        post.close()
        keep.close()
        QA = sb("QA", [P, GRP, HALF])
        QBh = sb("QBh", [P, GRP, HALF], F32R)
        QBl = sb("QBl", [P, GRP, HALF], F32R)
        KA = sb("KA", [P, HALF])
        KBh = sb("KBh", [P, TOK], F32R)
        KBl = sb("KBl", [P, TOK], F32R)
        VT = sb("VT", [P, TOK])
        Sb1 = [sb(f"Sb1_{i}", [P, SPC]) for i in range(2)]
        PTh1 = sb("PTh1", [P, 3, 4 * P], F32R)
        PTl1 = sb("PTl1", [P, 3, 4 * P], F32R)
        OTh = sb("OTh", [P, 2, GRP, P], F32R)
        OTl = sb("OTl", [P, 2, GRP, P], F32R)
        W1raw = sb("W1raw", [P, KC, 6 * P])
        W1h = sb("W1h", [P, KC, 6 * P], F32R)
        W1l = sb("W1l", [P, KC, 6 * P], F32R)
        Woraw = sb("Woraw", [P, GRP, DM])
        Vh = sb("Vh", [P, TILES, P], F32R)
        Vl = sb("Vl", [P, TILES, P], F32R)
        tab = sb("tab", [P, GRP, 3 * P])
        Woh = sb("Woh", [P, GRP, DM], F32R)
        Wol = sb("Wol", [P, GRP, DM], F32R)
        codes_i = sb("codes_i", [P, DM // 4], I32)
        codes_f = sb("codes_f", [P, DM], F32R)
        FTh = sb("FTh", [P, 2, P], F32R)
        FTl = sb("FTl", [P, 2, P], F32R)

        banks = [root.enter_context(nc.psum_tensor(f"bank{i}", [P, 512], F32)) for i in range(8)]

        def ring(name, ids):
            return Ring([banks[i] for i in ids], [sem(f"{name}_full{i}") for i in ids],
                        [sem(f"{name}_free{i}") for i in ids])

        ringA = ring("proj0", [3, 4, 5, 6, 7])
        ringO0 = ring("pv0", [5, 6])
        ringC = ring("post", [0, 1, 2, 3, 4, 7])
        ringL = ring("l1", [5, 6, 7])
        ringF = ring("tail", [0, 1, 2])

        x_loaded = [sem(f"x_loaded{i}") for i in range(4)]
        wkv_loaded = sem("wkv_loaded")
        wq_loaded = sem("wq_loaded")
        ident_loaded = sem("ident_loaded")
        consts_loaded = sem("consts_loaded")
        biases_loaded = sem("biases_loaded")
        bq_loaded = sem("bq_loaded")
        q_loaded = sem("q_loaded")
        wo0_loaded = sem("wo0_loaded")
        post_loaded = sem("post_loaded")
        w1_loaded = sem("w1_loaded")
        wo1_loaded = sem("wo1_loaded")
        codes_loaded = sem("codes_loaded")
        stored = sem("stored")
        w0h_ready = sem("w0h_ready")
        w0l_ready = sem("w0l_ready")
        xh_ready = sem("xh_ready")
        bqs_ready = sem("bqs_ready")
        qkh_ready = sem("qkh_ready")
        qkl_ready = sem("qkl_ready")
        deq_step = sem("deq_step")
        wfh_ready = sem("wfh_ready")
        eps_ready = sem("eps_ready")
        qs_loaded = [[sem(f"qs_loaded{par}_{half}") for half in range(2)] for par in range(2)]
        vs_ready = sem("vs_ready")
        out_moved = [sem("out_moved0"), sem("out_moved1")]
        pt0_act = sem("pt0_act")
        pt0_dve = sem("pt0_dve")
        rstd_ready = sem("rstd_ready")
        rec_ready = sem("rec_ready")
        wo0h_ready = sem("wo0h_ready")
        wo0_ready = sem("wo0_ready")

        def softmax_sems(name):
            return {k: sem(f"{name}_{k}") for k in
                    ("scores_ready", "scores_read", "negmax_ready", "exp_done", "rec_ready", "norm_done", "pt_full")}
        A0, A1 = softmax_sems("a0"), softmax_sems("a1")
        pth_ready = sem("pth_ready")
        ptl_ready = sem("ptl_ready")
        ath_ready = sem("ath_ready")
        atl_ready = sem("atl_ready")
        ln_dve = sem("ln_dve")
        std_ready = sem("std_ready")
        xn_ready = sem("xn_ready")
        x1h_ready = sem("x1h_ready")
        x2h_ready = sem("x2h_ready")
        bias_added = sem("bias_added")
        z_ready = sem("z_ready")
        w1_split = sem("w1_split")
        w1_step = sem("w1_step")
        wo1_split = sem("wo1_split")
        wo1_step = sem("wo1_step")
        tab_ready = sem("tab_ready")
        kt_ready = sem("kt_ready")
        vt1_ready = sem("vt1_ready")
        vh_ready = sem("vh_ready")
        vl_ready = sem("vl_ready")
        kh_ready = sem("kh_ready")
        qt_ready = sem("qt_ready")
        ql_ready = sem("ql_ready")
        oth_ready = sem("oth_ready")
        otl_ready = sem("otl_ready")
        x_added = sem("x_added")
        codes_ready = sem("codes_ready")
        fh_ready = sem("fh_ready")

        x_v = x_in.rearrange("b (t p) d -> p (b t) d", p=P)
        out_v = out.rearrange("b (t p) d -> p (b t) d", p=P)

        def rows(w):
            return w.rearrange("(c p) n -> p c n", p=P)

        wqkv_v = rows(w_qkv)
        wo_v = w_o.rearrange("(h p) n -> p h n", p=P)

        def sb_q0(t):
            return t[:, 0:SP0].rearrange("p (h k) -> p h k", h=GRP)

        def sb_q1(t):
            return t[:, SP0:SPC].rearrange("p (h k) -> p h k", h=GRP)

        def score_slices(h):
            return [(0, h * P, h * P, P), (1 + h // 2, (h % 2) * S, SP0 + h * S, S)]

        def bank_slices(bank):
            qt = 0 if bank == 0 else 1
            heads = range(GRP) if bank == 0 else range(2 * bank - 2, 2 * bank)
            return heads, qt, slice(qt * GRP + heads[0], qt * GRP + heads[-1] + 1)

        def softmax_max(v, A, n, k, buf, table_of, scale, only=range(3)):
            i = k % 2
            for bank in only:
                hold(v, A["scores_ready"], 3 * (n + k) + bank + 1)
                heads, qt, cols = bank_slices(bank)
                for h in heads:
                    _, c0, s0, w = score_slices(h)[qt]
                    last = nc.vector.tensor_tensor_reduce(
                        out=buf[i][:, s0:s0 + w], in0=banks[bank][:, c0:c0 + w], in1=table_of(h, qt), scale=1.0,
                        scalar=FLOOR, op0=ALU.add, op1=ALU.max,
                        accum_out=rowmax[:, i, qt * GRP + h:qt * GRP + h + 1])
                last.then_inc(A["scores_read"], 1)
                v.wait_ge(A["scores_read"], 3 * (n + k) + bank + 1)
                nc.vector.tensor_scalar(negmax[:, i, cols], rowmax[:, i, cols], -scale, None,
                                        ALU.mult).then_inc(A["negmax_ready"], 1)

        def softmax_exp(act, A, n, k, bank, buf, scale):
            i = k % 2
            act.wait_ge(A["negmax_ready"], 3 * (n + k) + bank + 1)
            heads, qt, _ = bank_slices(bank)
            for h in heads:
                _, _, s0, w = score_slices(h)[qt]
                j = qt * GRP + h
                last = nc.scalar.activation(buf[i][:, s0:s0 + w], buf[i][:, s0:s0 + w], ACT.Exp,
                                            bias=negmax[:, i, j:j + 1], scale=scale,
                                            accum_out=rowsum[:, i, j:j + 1])
            last.then_inc(A["exp_done"], 1)

        def softmax_rec(v, A, n, k, bank):
            i = k % 2
            _, _, cols = bank_slices(bank)
            v.wait_ge(A["exp_done"], 3 * (n + k) + bank + 1)
            nc.vector.reciprocal(rowrec[:, i, cols], rowsum[:, i, cols]).then_inc(A["rec_ready"], 1)

        def softmax_norm(g, A, n, k, buf):
            i = k % 2
            for bank in range(3):
                hold(g, A["rec_ready"], 3 * (n + k) + bank + 1)
                heads, qt, cols = bank_slices(bank)
                w = P if qt == 0 else S
                view = (sb_q1 if qt else sb_q0)(buf[i])[:, heads[0]:heads[-1] + 1, :]
                r = rowrec[:, i, cols].unsqueeze(2).broadcast_to([P, len(heads), w])
                nc.gpsimd.tensor_tensor(view, view, r, ALU.mult).then_inc(A["norm_done"], 1)

        def turn_bank(A, k, part):
            return banks[(3, 4, 7)[part] if A is A0 else 3 + (3 * k + part) % 2]

        def transpose_probs(pe, A, n, k, part, buf):
            if part < 2:
                pe.wait_ge(A["norm_done"], 3 * (n + k) + (3 if part else 1))
            j = 3 * k + part
            if A is A1:
                if not at_start(n) or j >= 2:
                    pe.wait_ge(ptl_ready, 3 * n + j - 1)
            elif not at_start(n) or k:
                if part == 0:
                    pe.wait_ge(pt0_act, n + k)
                else:
                    pe.wait_ge(pt0_dve, 2 * (n + k) + part - 2)
            for h in range(GRP):
                _, _, s0, _ = score_slices(h)[0 if part == 0 else 1]
                s0 += P * (part == 2)
                last = nc.tensor.transpose(turn_bank(A, k, part)[:, h * P:(h + 1) * P],
                                           buf[k % 2][:, s0:s0 + P], ident[:])
            last.then_inc(A["pt_full"], 1)

        def split_hi(act, A, n, k, part, PTh):
            j = 3 * k + part
            act.wait_ge(A["pt_full"], 3 * n + j + 1)
            nc.scalar.activation(PTh[:, part, :], turn_bank(A, k, part)[:], ACT.Copy).then_inc(pth_ready, 1)

        def split_lo(v, A, n, k, part, PTh, PTl):
            j = 3 * k + part
            v.wait_ge(pth_ready, 3 * n + j + 1)
            nc.vector.tensor_tensor(PTl[:, part, :], turn_bank(A, k, part)[:], PTh[:, part, :].bitcast(F32),
                                    ALU.subtract).then_inc(ptl_ready, 1)

        def w_raw(i):
            if i == 4:
                return W0raw[:, :, 4 * P:6 * P]
            return W0raw[:, :, 0:4 * P].rearrange("p c (g h d) -> p c g h d", g=NKV, h=GRP)[:, :, :, i, :]

        def w_split(w, i):
            if i == 4:
                return w[:, :, 4 * P:6 * P]
            return w[:, :, i * P:(i + 1) * P].rearrange("p c (g d) -> p c g d", g=NKV)

        def tiles_of(bank, which):
            return bank[:].rearrange("p (b t q) -> p b t q", t=2, q=P)[:, :, which, :]

        def q_half(buf, j):
            half = j // GRP
            return buf[:, j % GRP, half * HALF // 2:(half + 1) * HALF // 2].rearrange("p (b q) -> p b q", q=P)

        def wait_moved(eng, n, k):
            b = k % B
            if b % 2 == 0 and (k >= B or not at_start(n)):
                eng.wait_ge(out_moved[b // 2], (n + k - b) * (16 // B))

        def read_out(eng, n, k, qt, copy):
            b, use = k % B, 2 * k + qt
            ringO0.wait_full(eng, use, n)
            ringO0.freed(copy(Of[:, :, b * S + qt * P:b * S + (qt + 1) * P],
                              ringO0.bank(use)[0:HD0, :].rearrange("p (h q) -> p h q", h=GRP)), use)

        block = root.enter_context(nc.Block())

        GP = NKV // 2
        UNITS = 2 * B
        RVK, RVT, RQ, RP = 0, 4, 6, 14
        RPV = [[RP, RP + 1]] + [[RP + 4 * b - 1, RP + 4 * b + 1] for b in range(1, B)]
        ROP = [[RP + 4 * b + 2, RP + 4 * b + 4] for b in range(B - 1)] + [[RP + 4 * B - 2, RP + 4 * B - 1]]
        RL = 30
        TURNS = RL // 3

        @block.sync
        def _(sp):
            def load_x(i):
                sp.dma_start(X[:, 2 * i:2 * i + 2, :], x_v[:, 2 * i:2 * i + 2, :]).then_inc(x_loaded[i], 16)

            load_x(0)
            sp.dma_start(ident[:], ident_in).then_inc(ident_loaded, 16)
            load_x(1)
            sp.dma_start(W0raw[:, :, 4 * P:5 * P], rows(wk0)).then_inc(wkv_loaded, 16)
            sp.dma_start(W0raw[:, :, 5 * P:6 * P], rows(wv0)).then_inc(wkv_loaded, 16)
            for dst, bias in ((bk_t, bk0), (bv_t, bv0)):
                sp.dma_start(dst[:], bias.rearrange("(p a) -> p a", a=1),
                             allow_slow_non_contiguous=True).then_inc(biases_loaded, 16)
            sp.dma_start(W0raw[:, :, 0:4 * P], rows(wq0)).then_inc(wq_loaded, 16)
            load_x(2)
            for g in range(NKV):
                sp.dma_start(bq_t[16 * g:16 * (g + 1), :], bq0.rearrange("(g h d) -> g d h", g=NKV, h=GRP)[g],
                             allow_slow_non_contiguous=True).then_inc(bq_loaded, 16)
            load_x(3)
            sp.dma_start(qv[:], q_vals.rearrange("(c p) b k -> p c (b k)", p=P)).then_inc(q_loaded, 16)
            sp.dma_start(qs[:], q_scales.rearrange("(c p) b -> p c b", p=P)).then_inc(q_loaded, 16)
            sp.dma_start(bo_b[:], bo0.rearrange("(a n) -> a n", a=1).partition_broadcast(P)
                         .rearrange("p a n -> p (a n)")).then_inc(post_loaded, 16)
            sp.dma_start(fb_b[:], ffn_bias.rearrange("(a n) -> a n", a=1).partition_broadcast(P)
                         .rearrange("p a n -> p (a n)")).then_inc(post_loaded, 16)
            sp.dma_start(mask[:], mask_in).then_inc(consts_loaded, 16)
            sp.dma_start(dist[:], dist_in).then_inc(consts_loaded, 16)
            sp.dma_start(slopes[:], slopes_in).then_inc(consts_loaded, 16)

            def stack(g, half):
                par = g % 2
                cols = slice(half * HALF, (half + 1) * HALF)
                src = slice(HD0 * g, HD0 * (g + 1))
                for r, (q, k) in enumerate(((Qh, Kh), (Qh, Kl), (Ql, Kh), (Ql, Kl))):
                    dst = slice(64 * par + HD0 * r, 64 * par + HD0 * (r + 1))
                    sp.dma_start(KS[dst, cols].bitcast(F32), k[src, cols].bitcast(F32))\
                      .then_inc(qs_loaded[par][half], 16)
                    sp.dma_start(QS[dst, :, cols].bitcast(F32), q[src, :, cols].bitcast(F32))\
                      .then_inc(qs_loaded[par][half], 16)

            for half in range(2):
                sp.wait_ge(qkl_ready, len(PIECES) // 2 * (half + 1))
                for par in range(2):
                    stack(par, half)

            def move_out(g, half):
                cols = slice(half * HALF, (half + 1) * HALF)
                sp.dma_start(attn[HD0 * g:HD0 * (g + 1), :, cols], Of[:, :, cols]).then_inc(out_moved[half], 16)

            for g in range(NKV):
                n = B * g
                if g + 2 < NKV:
                    for half in range(2):
                        sp.wait_ge(A0["scores_read"], 3 * (n + (half + 1) * B // 2))
                        stack(g + 2, half)
                if g == 0:
                    ringA.wait_done(sp, len(A_STEPS))
                    for i in range(NKV):
                        sp.dma_start(Wo0raw[HD0 * i:HD0 * (i + 1)],
                                     wo0.rearrange("(g h d) n -> g d h n", g=NKV, h=GRP)[i]).then_inc(wo0_loaded, 16)
                for half in range(2):
                    for bank in range(2):
                        sp.wait_ge(ringO0.free[bank], n + (half + 1) * B // 2)
                    move_out(g, half)

            def load_w1(g):
                sp.dma_start(W1raw[:, :, 0:4 * P], wqkv_v[:, :, bass.ds(g * 4 * P, 4 * P)]).then_inc(w1_loaded, 16)
                sp.dma_start(W1raw[:, :, 4 * P:5 * P],
                             wqkv_v[:, :, bass.ds(g * P + QCOLS, P)]).then_inc(w1_loaded, 16)
                sp.dma_start(W1raw[:, :, 5 * P:6 * P],
                             wqkv_v[:, :, bass.ds(g * P + QCOLS + KVC, P)]).then_inc(w1_loaded, 16)

            load_w1(0)
            ringC.wait_done(sp, POST_USES)
            for half in range(2):
                sp.dma_start(codes_i[half * 64:(half + 1) * 64, :],
                             codes.rearrange("(r n) -> r n", n=DM // 4)).then_inc(codes_loaded, 16)

            sp.dma_start(Woraw[:], wo_v[:, 0:GRP, :]).then_inc(wo1_loaded, 16)
            sp.wait_ge(w1_split, 1)
            load_w1(1)
            with sp.Fori(1, NKV - 1) as g:
                sp.wait_ge(wo1_split, g)
                sp.dma_start(Woraw[:], wo_v[:, bass.ds(g * GRP, GRP), :]).then_inc(wo1_loaded, 16)
                sp.wait_ge(w1_split, g + 1)
                load_w1(g + 1)
            sp.wait_ge(wo1_split, NKV - 1)
            sp.dma_start(Woraw[:], wo_v[:, (NKV - 1) * GRP:NKV * GRP, :]).then_inc(wo1_loaded, 16)

            for t in range(TILES):
                sp.wait_ge(xn_ready, SCALED["scale4", t])
                sp.dma_start(out_v[:, t, :], X[:, t, :]).then_inc(stored, 16)
            sp.wait_ge(stored, 16 * TILES)

        @block.gpsimd
        def _(pool):
            nc.gpsimd.memset(eps[:], EPS).then_inc(eps_ready, 1)

            def stage_v(pair, par):
                nc.gpsimd.tensor_copy(VS[:, par], Vf[:, :, bass.ds((pair * 2 + par) * HD0, HD0)])\
                  .then_inc(vs_ready, 1)

            def attention_pair(pair, last):
                n = UNITS * pair
                for k in range(UNITS):
                    softmax_norm(pool, A0, n, k, Sb0)
                    if at_start(pair) and k == 0:
                        ringA.wait_done(pool, len(A_STEPS))
                        pool.wait_ge(post_loaded, 32)
                        pool.nop(nofuse=True)
                        stage_v(0, 0)
                        stage_v(0, 1)
                    if at_start(pair) and k:
                        for t in range(k - 1, k if k < UNITS - 1 else TILES):
                            nc.gpsimd.tensor_tensor(X[:, t, :], X[:, t, :], bo_b[:], ALU.add).then_inc(bias_added, 1)
                    if last:
                        c, cols = k // 2, slice(k % 2 * DM // 2, (k % 2 + 1) * DM // 2)
                        if k == 0:
                            pool.wait_ge(wo0_loaded, 16 * NKV)
                        nc.gpsimd.tensor_copy(Wo0h[:, c, cols], Wo0raw[:, c, cols]).then_inc(wo0h_ready, 1)
                        pool.wait_ge(wo0h_ready, k + 1)
                        nc.gpsimd.tensor_tensor(Wo0l[:, c, cols], Wo0raw[:, c, cols], Wo0h[:, c, cols].bitcast(F32),
                                                ALU.subtract).then_inc(wo0_ready, 1)
                    if k % B == 0 and (k and not last or not k and not at_start(pair)):
                        hold(pool, ringO0.free[1], n + k)
                        stage_v(*((pair + 1, 0) if k else (pair, 1)))

            attention_pair(0, False)
            with pool.Fori(1, GP - 1) as pair:
                attention_pair(pair, False)
            attention_pair(GP - 1, True)

            def split_w1(g, c0, c1, first, count):
                if first:
                    hold(pool, w1_loaded, (g + 1) * 48)
                nc.gpsimd.tensor_copy(W1h[:, c0:c1, :], W1raw[:, c0:c1, :]).then_inc(w1_step, 1)
                hold(pool, w1_step, g * 4 + count)
                last = nc.gpsimd.tensor_tensor(W1l[:, c0:c1, :], W1raw[:, c0:c1, :],
                                               W1h[:, c0:c1, :].bitcast(F32), ALU.subtract)
                if c1 == KC:
                    last.then_inc(w1_split, 1)

            for t in range(TILES):
                pool.wait_ge(xn_ready, SCALED["scale1", t])
                nc.gpsimd.tensor_tensor(Z[:, t, :], X[:, t, :], fb_b[:], ALU.add).then_inc(z_ready, 1)
                if t < KC:
                    split_w1(0, t, t + 1, t == 0, t + 1)

            def group(g, last):
                n = B * g
                hold(pool, wo1_loaded, (g + 1) * 16)
                if not at_start(g):
                    hold(pool, x_added, g * 2 * B)
                nc.gpsimd.tensor_copy(Woh[:], Woraw[:]).then_inc(wo1_step, 1)
                hold(pool, wo1_step, g + 1)
                nc.gpsimd.tensor_tensor(Wol[:], Woraw[:], Woh[:].bitcast(F32), ALU.subtract).then_inc(wo1_split, 1)
                if last:
                    hold(pool, codes_loaded, 32)
                    nc.gpsimd.tensor_copy(codes_f[:], codes_i[:].bitcast(I8)).then_inc(codes_ready, 1)

                def split_chunks(*chunks):
                    if not last:
                        for c in chunks:
                            split_w1(g + 1, c, c + 1, c == 0, c + 1)

                softmax_norm(pool, A1, n, 0, Sb1)
                softmax_norm(pool, A1, n, 1, Sb1)
                if not last:
                    hold(pool, qt_ready, 8 * g + 8)
                split_chunks(0)
                softmax_norm(pool, A1, n, 2, Sb1)
                split_chunks(1, 2)
                softmax_norm(pool, A1, n, 3, Sb1)
                split_chunks(3)

            ringC.wait_done(pool, POST_USES)
            group(0, False)
            with pool.Fori(1, NKV - 1) as g:
                group(g, False)
            group(NKV - 1, True)

        @block.scalar
        def _(act):
            def biased(use, j, bias, scale):
                if j >= 2:
                    act.wait_ge(qkl_ready, j - 1)
                ringA.freed(nc.scalar.activation(QKf[:, j % 2, :], ringA.bank(use)[:], ACT.Identity,
                                                 bias=bias, scale=scale), use)

            for step in PHASE_A:
                what, i, half = step
                if what == "w":
                    act.wait_ge(*((wkv_loaded, 32) if i == 4 else (wq_loaded, 16)))
                    nc.scalar.activation(w_split(W0h, i), w_raw(i), ACT.Copy).then_inc(w0h_ready, 1)
                elif what == "scores":
                    for bank in range(3 if i == 0 else 1):
                        softmax_exp(act, A0, 0, i, bank, Sb0, 1.0)
                if step not in A_USE:
                    continue
                use = A_USE[step]
                if what != "vt":
                    ringA.wait_full(act, use)
                if what == "x":
                    nc.scalar.activation(XTh[:, :, i * P:(i + 1) * P],
                                         ringA.bank(use)[:].rearrange("p (c t) -> p c t", c=KC),
                                         ACT.Copy).then_inc(xh_ready, 1)
                elif what == "k":
                    if half == 0:
                        act.wait_ge(biases_loaded, 32)
                    biased(use, PIECES.index(step), bk_t[:, 0:1], 1.0)
                elif what == "q":
                    if i == 0 and half == 0:
                        act.wait_ge(bqs_ready, 1)
                    biased(use, PIECES.index(step), bq_s[:, i:i + 1], SCALE0)
                elif what == "v":
                    ringA.freed(nc.scalar.activation(VTf[:, half * HALF:(half + 1) * HALF], ringA.bank(use)[:],
                                                     ACT.Identity, bias=bv_t[:, 0:1]), use)
                elif what == "wf":
                    nc.scalar.activation(WFh[:, :, i * P:(i + 1) * P],
                                         ringA.bank(use)[:].rearrange("p (c t) -> p c t", c=KC),
                                         ACT.Copy).then_inc(wfh_ready, 1)

            def attention_pair(pair, last):
                n = UNITS * pair
                for k in range(UNITS):
                    act.wait_ge(A0["pt_full"], 3 * (n + k) + 1)
                    nc.scalar.activation(PT0[:, 0, :], turn_bank(A0, k, 0)[:], ACT.Copy).then_inc(pt0_act, 1)
                    if k + 1 < UNITS or not last:
                        softmax_exp(act, A0, n, k + 1, 1, Sb0, 1.0)
                        softmax_exp(act, A0, n, k + 1, 2, Sb0, 1.0)
                    if k + 2 < UNITS or not last:
                        softmax_exp(act, A0, n, k + 2, 0, Sb0, 1.0)
                    wait_moved(act, n, k)
                    read_out(act, n, k, 0, lambda dst, src: nc.scalar.activation(dst, src, ACT.Copy))

            attention_pair(0, False)
            with act.Fori(1, GP - 1) as pair:
                attention_pair(pair, False)
            attention_pair(GP - 1, True)

            act.wait_ge(eps_ready, 1)

            def std_of(i):
                act.wait_ge(ln_dve, 2 * i + 2)
                nc.scalar.activation(std[:, i % 4:i % 4 + 1], moments[:, i % 4, 1:2], ACT.Sqrt,
                                     bias=eps[:, 0:1]).then_inc(std_ready, 1)

            def scale_of(what, i, t, y):
                act.wait_ge(rec_ready, SCALED[what, t])
                nc.scalar.activation(X[:, t, :], y, ACT.Identity, bias=shift[:, i % 4:i % 4 + 1],
                                     scale=rstd[:, i % 4:i % 4 + 1]).then_inc(xn_ready, 1)

            def hi_of(use, dst, done):
                ringC.wait_full(act, use)
                nc.scalar.activation(dst, ringC.bank(use)[:].rearrange("p (c t) -> p c t", c=KC),
                                     ACT.Copy).then_inc(done, 1)

            proj_use = {t: use for what, t, use, _, _ in POST if what == "proj"}
            for what, t, use, i, before in POST:
                if what == "attn":
                    if t % (TILES // 2) == 0:
                        act.wait_ge(out_moved[t // (TILES // 2)], 16 * NKV)
                    if t >= 2:
                        ringC.wait_full(act, proj_use[t - 2])
                    nc.scalar.activation(ATh[:, t % 2], attn[:, :, t * P:(t + 1) * P], ACT.Copy)\
                      .then_inc(ath_ready, 1)
                elif what in ("norm1", "norm2"):
                    std_of(i)
                elif what in ("scale1", "scale2"):
                    scale_of(what, i, t, Y[:, i % 2, :])
                elif what == "turn1":
                    hi_of(use, X1h[:, t % 2], x1h_ready)
                elif what == "turn2":
                    hi_of(use, XTh[:, :, t * P:(t + 1) * P], x2h_ready)

            def table(g):
                for h in range(GRP):
                    last = nc.scalar.activation(tab[:, h, :], dist[:], ACT.Copy,
                                                scale=slopes[:, bass.ds(g * GRP + h, 1)])
                last.then_inc(tab_ready, 1)

            def q_out1(g, j):
                use = RQ + j
                ringL.wait_full(act, use, g * TURNS)
                nc.scalar.activation(q_half(QA, j), tiles_of(ringL.bank(use), 0), ACT.Copy)
                nc.scalar.activation(q_half(QBh, j), tiles_of(ringL.bank(use), 1), ACT.Copy).then_inc(qt_ready, 1)

            def group(g, last):
                n = B * g
                for j in range(2):
                    use = RVK + 2 * j
                    ringL.wait_full(act, use, g * TURNS)
                    nc.scalar.activation(KA[:, j * HALF // 2:(j + 1) * HALF // 2].rearrange("p (b q) -> p b q", q=P),
                                         tiles_of(ringL.bank(use), 0), ACT.Copy)
                    nc.scalar.activation(KBh[:, j * HALF:(j + 1) * HALF], ringL.bank(use)[:], ACT.Copy)\
                      .then_inc(kh_ready, 1)
                for j in range(2):
                    ringL.wait_full(act, RVT + j, g * TURNS)
                    nc.scalar.activation(Vh[:, 4 * j:4 * j + 4, :],
                                         ringL.bank(RVT + j)[:].rearrange("p (t d) -> p t d", t=4),
                                         ACT.Copy).then_inc(vh_ready, 1)

                def exps(b, bank):
                    softmax_exp(act, A1, n, b, bank, Sb1, SCALE1)

                def out_hi(b, qt):
                    use = RPV[b][qt]
                    ringL.wait_full(act, use, g * TURNS)
                    nc.scalar.activation(OTh[:, qt], ringL.bank(use)[:].rearrange("p (h q) -> p h q", h=GRP),
                                         ACT.Copy).then_inc(oth_ready, 1)

                for j in range(5):
                    q_out1(g, j)
                for bank in range(3):
                    exps(0, bank)
                q_out1(g, 5)
                q_out1(g, 6)
                exps(1, 0)
                split_hi(act, A1, n, 0, 0, PTh1)
                exps(1, 1)
                split_hi(act, A1, n, 0, 1, PTh1)
                q_out1(g, 7)
                exps(1, 2)
                split_hi(act, A1, n, 0, 2, PTh1)
                out_hi(0, 0)
                exps(2, 0)
                exps(2, 1)
                out_hi(0, 1)
                for b in range(1, B):
                    split_hi(act, A1, n, b, 0, PTh1)
                    if b == 1:
                        exps(2, 2)
                    if b == 2:
                        exps(3, 1)
                        exps(3, 2)
                        if last:
                            tail(0)
                    split_hi(act, A1, n, b, 1, PTh1)
                    if last and b >= 2:
                        tail(2 * b - 3)
                    split_hi(act, A1, n, b, 2, PTh1)
                    out_hi(b, 0)
                    if last and b >= 2:
                        tail(2 * b - 2)
                    out_hi(b, 1)
                    if b == 1:
                        exps(3, 0)
                if last:
                    tail(*range(5, TAIL_SLOTS))
                else:
                    act.wait_ge(A1["scores_read"], 3 * (n + B))
                    table(g + 1)

            def tail(*slots):
                for what, t, use, i, before in tail_steps(slots):
                    if what in ("norm3", "norm4"):
                        std_of(NORMS + i)
                    elif what in ("scale3", "scale4"):
                        scale_of(what, NORMS + i, t, X[:, t, :])
                    elif what == "turn":
                        ringF.wait_full(act, use)
                        nc.scalar.activation(FTh[:, t % 2, :], ringF.bank(use)[:, 0:P], ACT.Copy)\
                          .then_inc(fh_ready, 1)

            ringC.wait_done(act, POST_USES)
            table(0)
            group(0, False)
            with act.Fori(1, NKV - 1) as g:
                group(g, False)
            group(NKV - 1, True)

        @block.vector
        def _(v):
            def mask_of(h, qt):
                return mask[:, 0:P] if qt == 0 else mask[:, P:3 * P]


            def split_qk(step):
                what, m, half = step
                j = PIECES.index(step)
                hi, lo = (Kh, Kl) if what == "k" else (Qh[:, m], Ql[:, m])
                cols = slice(half * HALF, (half + 1) * HALF)
                ringA.wait_read(v, A_USE[step])
                nc.vector.tensor_copy(hi[:, cols], QKf[:, j % 2, :]).then_inc(qkh_ready, 1)
                v.wait_ge(qkh_ready, j + 1)
                nc.vector.tensor_tensor(lo[:, cols], QKf[:, j % 2, :], hi[:, cols].bitcast(F32),
                                        ALU.subtract).then_inc(qkl_ready, 1)

            weights = 0
            for step in PHASE_A:
                what, i, half = step
                use = A_USE.get(step)
                if what == "w":
                    weights += 1
                    if weights == 2:
                        v.wait_ge(bq_loaded, 16 * NKV)
                        nc.vector.tensor_scalar(bq_s[:], bq_t[:], SCALE0, None, ALU.mult).then_inc(bqs_ready, 1)
                    v.wait_ge(w0h_ready, weights)
                    nc.vector.tensor_tensor(w_split(W0l, i), w_raw(i), w_split(W0h, i).bitcast(F32),
                                            ALU.subtract).then_inc(w0l_ready, 1)
                elif what == "x":
                    v.wait_ge(xh_ready, i + 1)
                    ringA.freed(nc.vector.tensor_tensor(XTl[:, :, i * P:(i + 1) * P],
                                                        ringA.bank(use)[:].rearrange("p (c t) -> p c t", c=KC),
                                                        XTh[:, :, i * P:(i + 1) * P].bitcast(F32), ALU.subtract), use)
                elif what in ("k", "q"):
                    split_qk(step)
                elif what == "deq":
                    v.wait_ge(q_loaded, 32)
                    nc.vector.tensor_scalar(qw[:], qv[:], -128.0, None, ALU.add).then_inc(deq_step, 1)
                    v.wait_ge(deq_step, 1)
                    for c in range(KC):
                        w = qw[:, c, :].rearrange("p (b k) -> p b k", k=32)
                        nc.vector.tensor_tensor(w, w, qs[:, c, :].unsqueeze(2).broadcast_to([P, 16, 32]),
                                                ALU.mult).then_inc(deq_step, 1)
                elif what == "vt":
                    ringA.wait_full(v, use)
                    ringA.freed(nc.vector.tensor_copy(Vf[:, 4 * half:4 * half + 4, :],
                                                      ringA.bank(use)[:].rearrange("p (t d) -> p t d", t=4)), use)
                elif what == "wf":
                    v.wait_ge(wfh_ready, i + 1)
                    ringA.freed(nc.vector.tensor_tensor(WFl[:, :, i * P:(i + 1) * P],
                                                        ringA.bank(use)[:].rearrange("p (c t) -> p c t", c=KC),
                                                        WFh[:, :, i * P:(i + 1) * P].bitcast(F32), ALU.subtract), use)
                elif what == "scores":
                    if i == 0:
                        v.wait_ge(consts_loaded, 48)
                    else:
                        for bank in range(3):
                            softmax_rec(v, A0, 0, 0, bank)
                    softmax_max(v, A0, 0, i, Sb0, mask_of, 1.0)

            def attention_pair(pair, last):
                n = UNITS * pair
                for k in range(UNITS):
                    ahead = k + 2 < UNITS or not last
                    if k + 1 < UNITS or not last:
                        softmax_rec(v, A0, n, k + 1, 0)
                    if k or not at_start(n):
                        outs0(n, k - 1)
                    if ahead:
                        hold(v, A0["pt_full"], 3 * (n + k) + 1)
                        softmax_max(v, A0, n, k + 2, Sb0, mask_of, 1.0, [0])
                    for part in (1, 2):
                        v.wait_ge(A0["pt_full"], 3 * (n + k) + part + 1)
                        nc.vector.tensor_copy(PT0[:, part, :], turn_bank(A0, k, part)[:])\
                          .then_inc(pt0_dve, 1)
                    if k + 1 < UNITS or not last:
                        softmax_rec(v, A0, n, k + 1, 1)
                        softmax_rec(v, A0, n, k + 1, 2)
                    if ahead:
                        softmax_max(v, A0, n, k + 2, Sb0, mask_of, 1.0, [1, 2])

            def outs0(n, k):
                wait_moved(v, n, k)
                read_out(v, n, k, 1, lambda dst, src: nc.vector.tensor_copy(dst, src))

            attention_pair(0, False)
            with v.Fori(1, GP - 1) as pair:
                attention_pair(pair, False)
            attention_pair(GP - 1, True)
            outs0(UNITS * (GP - 1), UNITS - 1)

            def norm(i, t, y):
                k = i % 4
                nc.vector.bn_stats(stats[:, k, :], y).then_inc(ln_dve, 1)
                v.wait_ge(ln_dve, 2 * i + 1)
                nc.vector.bn_aggr(moments[:, k, :], stats[:, k, :]).then_inc(ln_dve, 1)

            def normalize(what, i, t):
                k, done = i % 4, SCALED[what, t]
                v.wait_ge(std_ready, i + 1)
                nc.vector.reciprocal(rstd[:, k:k + 1], std[:, k:k + 1]).then_inc(rstd_ready, 1)
                v.wait_ge(rstd_ready, done)
                nc.vector.scalar_tensor_tensor(shift[:, k:k + 1], moments[:, k, 0:1], -1.0, rstd[:, k:k + 1],
                                               ALU.mult, ALU.mult).then_inc(rec_ready, 1)

            for what, t, use, i, before in POST:
                if what == "attn":
                    v.wait_ge(ath_ready, t + 1)
                    nc.vector.tensor_tensor(ATl[:, t % 2], attn[:, :, t * P:(t + 1) * P], ATh[:, t % 2].bitcast(F32),
                                            ALU.subtract).then_inc(atl_ready, 1)
                elif what in ("norm1", "norm2"):
                    y = Y[:, i % 2, :]
                    if what == "norm1":
                        v.wait_ge(bias_added, t + 1)
                    else:
                        v.wait_ge(z_ready, t + 1)
                    if i >= 2:
                        v.wait_ge(xn_ready, SCALED[NAMES[i - 2]])
                    ringC.wait_full(v, before)
                    ringC.freed(nc.vector.tensor_tensor(y, ringC.bank(before)[:],
                                                        (X if what == "norm1" else Z)[:, t, :], ALU.add), before)
                    ringC.wait_read(v, before)
                    norm(i, t, y)
                elif what in ("scale1", "scale2"):
                    normalize(what, i, t)
                elif what == "turn1":
                    v.wait_ge(x1h_ready, t + 1)
                    ringC.freed(nc.vector.tensor_tensor(
                        X1l[:, t % 2], ringC.bank(use)[:].rearrange("p (c t) -> p c t", c=KC),
                        X1h[:, t % 2].bitcast(F32), ALU.subtract), use)
                elif what == "turn2":
                    v.wait_ge(x2h_ready, t + 1)
                    ringC.freed(nc.vector.tensor_tensor(
                        XTl[:, :, t * P:(t + 1) * P], ringC.bank(use)[:].rearrange("p (c t) -> p c t", c=KC),
                        XTh[:, :, t * P:(t + 1) * P].bitcast(F32), ALU.subtract), use)

            def tab_of(h, qt):
                return tab[:, h, 0:P] if qt == 0 else tab[:, h, P:3 * P]

            def add_out(g, b, qt):
                use = ROP[b][qt]
                ringL.wait_full(v, use, g * TURNS)
                t = 2 * b + qt
                nc.vector.tensor_tensor(X[:, t, :], ringL.bank(use)[:], X[:, t, :], ALU.add).then_inc(x_added, 1)

            def out_lo(g, b, qt):
                use = RPV[b][qt]
                v.wait_ge(oth_ready, 2 * (B * g + b) + qt + 1)
                nc.vector.tensor_tensor(
                    OTl[:, qt], ringL.bank(use)[:].rearrange("p (h q) -> p h q", h=GRP),
                    OTh[:, qt].bitcast(F32), ALU.subtract).then_inc(otl_ready, 1)

            def group(g, last):
                n = B * g

                def maxes(b, only=range(3)):
                    softmax_max(v, A1, n, b, Sb1, tab_of, SCALE1, only)

                def recs(b):
                    for bank in range(3):
                        softmax_rec(v, A1, n, b, bank)

                for j in range(2):
                    cols = slice(j * HALF, (j + 1) * HALF)
                    use = RVK + 2 * j
                    v.wait_ge(kh_ready, 2 * g + j + 1)
                    nc.vector.tensor_tensor(KBl[:, cols], ringL.bank(use)[:], KBh[:, cols].bitcast(F32),
                                            ALU.subtract).then_inc(kt_ready, 1)
                    ringL.wait_full(v, use + 1, g * TURNS)
                    nc.vector.tensor_copy(VT[:, cols], ringL.bank(use + 1)[:]).then_inc(vt1_ready, 1)
                for j in range(2):
                    v.wait_ge(vh_ready, 2 * g + j + 1)
                    nc.vector.tensor_tensor(
                        Vl[:, 4 * j:4 * j + 4, :], ringL.bank(RVT + j)[:].rearrange("p (t d) -> p t d", t=4),
                        Vh[:, 4 * j:4 * j + 4, :].bitcast(F32), ALU.subtract).then_inc(vl_ready, 1)

                def q_lo(*pieces):
                    for j in pieces:
                        v.wait_ge(qt_ready, 8 * g + j + 1)
                        nc.vector.tensor_tensor(q_half(QBl, j), tiles_of(ringL.bank(RQ + j), 1),
                                                q_half(QBh, j).bitcast(F32), ALU.subtract).then_inc(ql_ready, 1)

                q_lo(0, 1, 2, 3, 4)
                v.wait_ge(tab_ready, g + 1)
                maxes(0)
                recs(0)
                q_lo(5, 6)
                maxes(1)
                softmax_rec(v, A1, n, 1, 0)
                split_lo(v, A1, n, 0, 0, PTh1, PTl1)
                softmax_rec(v, A1, n, 1, 1)
                split_lo(v, A1, n, 0, 1, PTh1, PTl1)
                q_lo(7)
                softmax_rec(v, A1, n, 1, 2)
                split_lo(v, A1, n, 0, 2, PTh1, PTl1)
                maxes(2, [0])
                out_lo(g, 0, 0)
                maxes(2, [1, 2])
                softmax_rec(v, A1, n, 2, 0)
                softmax_rec(v, A1, n, 2, 1)
                out_lo(g, 0, 1)
                for b in range(1, B):
                    split_lo(v, A1, n, b, 0, PTh1, PTl1)
                    if b == 1:
                        softmax_rec(v, A1, n, 2, 2)
                    if b == 2:
                        softmax_rec(v, A1, n, 3, 1)
                    split_lo(v, A1, n, b, 1, PTh1, PTl1)
                    if b == 2:
                        softmax_rec(v, A1, n, 3, 2)
                    if last and b >= 2:
                        tail(2 * b - 3)
                    add_out(g, b - 1, 0)
                    split_lo(v, A1, n, b, 2, PTh1, PTl1)
                    out_lo(g, b, 0)
                    if last and b >= 2:
                        tail(2 * b - 2)
                    add_out(g, b - 1, 1)
                    out_lo(g, b, 1)
                    if b == 1:
                        maxes(3)
                        softmax_rec(v, A1, n, 3, 0)
                        if last:
                            tail(0)
                if last:
                    tail(5)
                add_out(g, B - 1, 0)
                if last:
                    tail(6)
                add_out(g, B - 1, 1)
                if last:
                    tail(*range(7, TAIL_SLOTS))

            def tail(*slots):
                for what, t, use, i, before in tail_steps(slots):
                    if what == "norm3":
                        v.wait_ge(x_added, 2 * B * (NKV - 1) + t + 1)
                        norm(NORMS + i, t, X[:, t, :])
                    elif what in ("scale3", "scale4"):
                        normalize(what, NORMS + i, t)
                    elif what == "turn":
                        v.wait_ge(fh_ready, t + 1)
                        ringF.freed(nc.vector.tensor_tensor(
                            FTl[:, t % 2, :], ringF.bank(use)[:, 0:P], FTh[:, t % 2, :].bitcast(F32),
                            ALU.subtract), use)
                    elif what == "norm4":
                        ringF.wait_full(v, before)
                        v.wait_ge(xn_ready, SCALED["scale3", t])
                        ringF.freed(nc.vector.tensor_tensor(X[:, t, :], ringF.bank(before)[:], X[:, t, :], ALU.add),
                                    before)
                        ringF.wait_read(v, before)
                        norm(NORMS + i, t, X[:, t, :])

            group(0, False)
            with v.Fori(1, NKV - 1) as g:
                group(g, False)
            group(NKV - 1, True)

        @block.tensor
        def _(pe):
            def three(out_ap, lh, ll, rh, rl, first, last):
                nc.tensor.matmul(out_ap, lh, rh, start=first, stop=False)
                nc.tensor.matmul(out_ap, lh, rl, start=False, stop=False)
                return nc.tensor.matmul(out_ap, ll, rh, start=False, stop=last)

            def scores0(n, k, pair):
                b, par = k % B, (k // B) % 2
                rows_ = slice(64 * par, 64 * par + 64)
                if b % 2 == 0:
                    pe.wait_ge(qs_loaded[par][b // 2], (pair + 1) * 16 * 8)
                for bank in range(3):
                    if not at_start(n) or k:
                        pe.wait_ge(A0["scores_read"], 3 * (n + k) + bank - 2)
                    heads = range(GRP) if bank == 0 else range(2 * bank - 2, 2 * bank)
                    for h in heads:
                        qt = 0 if bank == 0 else 1
                        _, c0, _, w = score_slices(h)[qt]
                        last = nc.tensor.matmul(banks[bank][:, c0:c0 + w],
                                                QS[rows_, h, b * S + qt * P:b * S + (qt + 1) * P],
                                                KS[rows_, b * S:b * S + w], start=True, stop=True)
                    last.then_inc(A0["scores_ready"], 1)

            def turn(use, source):
                ringA.wait_free(pe, use)
                for c in range(KC):
                    last = nc.tensor.transpose(ringA.bank(use)[:, c * P:(c + 1) * P], source(c), ident[:])
                ringA.filled(last, use)

            def project0(use, m, half):
                ringA.wait_free(pe, use)
                cols = slice(half * HALF, (half + 1) * HALF)
                for c in range(KC):
                    last = three(ringA.bank(use)[:], W0h[:, c, m * P:(m + 1) * P], W0l[:, c, m * P:(m + 1) * P],
                                 XTh[:, c, cols], XTl[:, c, cols], c == 0, c == KC - 1)
                ringA.filled(last, use)

            pe.wait_ge(ident_loaded, 16)
            for step in PHASE_A:
                what, i, half = step
                use = A_USE.get(step)
                if what == "x":
                    pe.wait_ge(x_loaded[i // 2], 16)
                    turn(use, lambda c: X[:, i, c * P:(c + 1) * P])
                elif what == "k":
                    pe.wait_ge(w0l_ready, 1)
                    for t in range(TILES // 2 * half, TILES // 2 * (half + 1)):
                        ringA.wait_read(pe, A_USE["x", t, half])
                    project0(use, 4, half)
                elif what == "v":
                    project0(use, 5, half)
                elif what == "q":
                    pe.wait_ge(w0l_ready, i + 2)
                    project0(use, i, half)
                elif what == "vt":
                    ringA.wait_read(pe, A_USE["v", 0, half])
                    turn(use, lambda c: VTf[:, (4 * half + c) * P:(4 * half + c + 1) * P])
                elif what == "wf":
                    pe.wait_ge(deq_step, 1 + KC)
                    turn(use, lambda c: qw[:, i, c * P:(c + 1) * P])
                elif what == "scores":
                    scores0(0, i, 0)

            def values0(n, k, pair, qt):
                b, par = k % B, (k // B) % 2
                if b == 0 and qt == 0:
                    pe.wait_ge(vs_ready, 2 * pair + par + 1)
                u = 2 * k + qt
                ringO0.wait_free(pe, u, n)
                if qt == 0:
                    pe.wait_ge(pt0_act, n + k + 1)
                else:
                    pe.wait_ge(pt0_dve, 2 * (n + k) + 2)
                parts = [(0, 0)] if qt == 0 else [(1, 0), (2, 1)]
                for j, (part, kt) in enumerate(parts):
                    last = nc.tensor.matmul(ringO0.bank(u)[0:HD0, :], VS[:, par, 2 * b + kt, :],
                                            PT0[:, part, :], start=(j == 0), stop=(j == len(parts) - 1))
                ringO0.filled(last, u)

            def attention_pair(pair, last):
                n = UNITS * pair
                for k in range(UNITS):
                    transpose_probs(pe, A0, n, k, 0, Sb0)
                    if k or not at_start(n):
                        values0(n, k - 1, pair, 1)
                    if k + 2 < UNITS or not last:
                        scores0(n, k + 2, pair + (k + 2) // UNITS)
                    transpose_probs(pe, A0, n, k, 1, Sb0)
                    transpose_probs(pe, A0, n, k, 2, Sb0)
                    values0(n, k, pair, 0)

            ringA.wait_done(pe, len(A_STEPS))
            attention_pair(0, False)
            with pe.Fori(1, GP - 1) as pair:
                attention_pair(pair, False)
            attention_pair(GP - 1, True)
            values0(UNITS * (GP - 1), UNITS - 1, GP - 1, 1)

            def lwait(g, use):
                prev = use - len(ringL.banks)
                if prev < 0 and at_start(g):
                    return
                if prev < 0:
                    pe.wait_ge(*((otl_ready, 2 * B * g) if prev == -3 else (x_added, 2 * B * g + prev + 1)))
                elif prev < RVT:
                    pe.wait_ge((kt_ready, vt1_ready)[prev % 2], 2 * g + prev // 2 + 1)
                elif prev < RQ:
                    pe.wait_ge(vl_ready, 2 * g + prev - RVT + 1)
                elif prev < RP:
                    pe.wait_ge(ql_ready, 8 * g + prev - RQ + 1)
                else:
                    for b in range(B):
                        for qt in range(2):
                            if prev == RPV[b][qt]:
                                pe.wait_ge(otl_ready, 2 * (B * g + b) + qt + 1)
                            if prev == ROP[b][qt]:
                                pe.wait_ge(x_added, 2 * (B * g + b) + qt + 1)

            def project1(g, use, m, half):
                lwait(g, use)
                cols = slice(half * HALF, (half + 1) * HALF)
                for c in range(KC):
                    last = three(ringL.bank(use)[:], W1h[:, c, m * P:(m + 1) * P], W1l[:, c, m * P:(m + 1) * P],
                                 XTh[:, c, cols], XTl[:, c, cols], c == 0, c == KC - 1)
                ringL.filled(last, use)

            def project_vk(g, half, which=(0, 1)):
                for vk in which:
                    project1(g, RVK + 2 * half + vk, 4 + vk, half)

            pe.wait_ge(wo0_ready, UNITS)
            turned = {t: use for what, t, use, _, _ in POST if what == "turn2"}
            for what, t, i, _, before in POST:
                if what == "turn1" and t == TILES - 1:
                    pe.wait_ge(w1_split, 1)
                    for done in range(TILES // 2):
                        ringC.wait_read(pe, turned[done])
                    project_vk(0, 0, [0])
                if what == "turn2" and t == TILES - 1:
                    project_vk(0, 0, [1])
                if what == "proj":
                    pe.wait_ge(atl_ready, t + 1)
                    ringC.wait_free(pe, i)
                    for c in range(KC):
                        last = three(ringC.bank(i)[:], ATh[:, t % 2, c, :], ATl[:, t % 2, c, :],
                                     Wo0h[:, c, :], Wo0l[:, c, :], c == 0, c == KC - 1)
                    ringC.filled(last, i)
                elif what == "linear":
                    ringC.wait_read(pe, before)
                    ringC.wait_free(pe, i)
                    for c in range(KC):
                        last = three(ringC.bank(i)[:], X1h[:, t % 2, c, :], X1l[:, t % 2, c, :],
                                     WFh[:, c, :], WFl[:, c, :], c == 0, c == KC - 1)
                    ringC.filled(last, i)
                elif what in ("turn1", "turn2"):
                    pe.wait_ge(xn_ready, SCALED["scale" + what[-1], t])
                    ringC.wait_free(pe, i)
                    for c in range(KC):
                        last = nc.tensor.transpose(ringC.bank(i)[:, c * P:(c + 1) * P],
                                                   X[:, t, c * P:(c + 1) * P], ident[:])
                    ringC.filled(last, i)

            def scores1(g, b):
                n = B * g
                for bank in range(3):
                    if not at_start(n) or b:
                        pe.wait_ge(A1["scores_read"], 3 * (n + b) + bank - 2)
                    heads = range(GRP) if bank == 0 else range(2 * bank - 2, 2 * bank)
                    for h in heads:
                        qt = 0 if bank == 0 else 1
                        _, c0, _, w = score_slices(h)[qt]
                        scores, tile = banks[bank][:, c0:c0 + w], slice(b * P, (b + 1) * P)
                        if qt == 0:
                            last = nc.tensor.matmul(scores, QA[:, h, tile], KA[:, tile], start=True, stop=True)
                        else:
                            keys = slice(b * S, (b + 1) * S)
                            last = three(scores, QBh[:, h, tile], QBl[:, h, tile], KBh[:, keys], KBl[:, keys],
                                         True, True)
                    last.then_inc(A1["scores_ready"], 1)

            def values1(g, b, qt):
                n = B * g
                use = RPV[b][qt]
                lwait(g, use)
                pe.wait_ge(ptl_ready, 3 * (n + b) + (1 if qt == 0 else 3))
                parts = [(0, 0)] if qt == 0 else [(1, 0), (2, 1)]
                for j, (part, kt) in enumerate(parts):
                    last = three(ringL.bank(use)[:], Vh[:, 2 * b + kt, :], Vl[:, 2 * b + kt, :],
                                 PTh1[:, part, :], PTl1[:, part, :], j == 0, j == len(parts) - 1)
                ringL.filled(last, use)

            def output1(g, b, qt):
                use = ROP[b][qt]
                lwait(g, use)
                if b == 0 and qt == 0:
                    pe.wait_ge(wo1_split, g + 1)
                pe.wait_ge(otl_ready, 2 * (B * g + b) + qt + 1)
                for h in range(GRP):
                    last = three(ringL.bank(use)[:], OTh[:, qt, h, :], OTl[:, qt, h, :],
                                 Woh[:, h, :], Wol[:, h, :], h == 0, h == GRP - 1)
                ringL.filled(last, use)

            def group(g, last):
                n = B * g
                if at_start(g):
                    project_vk(g, 1)
                else:
                    pe.wait_ge(w1_split, g + 1)
                    project_vk(g, 0)
                    project_vk(g, 1)
                for j in range(2):
                    lwait(g, RVT + j)
                    pe.wait_ge(vt1_ready, 2 * g + j + 1)
                    for t in range(4):
                        ins = nc.tensor.transpose(ringL.bank(RVT + j)[:, t * P:(t + 1) * P],
                                                  VT[:, (4 * j + t) * P:(4 * j + t + 1) * P], ident[:])
                    ringL.filled(ins, RVT + j)
                for j in range(5):
                    project1(g, RQ + j, j % GRP, j // GRP)
                pe.wait_ge(ql_ready, 8 * g + 4)
                scores1(g, 0)
                project1(g, RQ + 5, 1, 1)
                project1(g, RQ + 6, 2, 1)
                scores1(g, 1)
                transpose_probs(pe, A1, n, 0, 0, Sb1)
                transpose_probs(pe, A1, n, 0, 1, Sb1)
                project1(g, RQ + 7, 3, 1)
                transpose_probs(pe, A1, n, 0, 2, Sb1)
                values1(g, 0, 0)
                pe.wait_ge(ql_ready, 8 * g + 8)
                scores1(g, 2)
                values1(g, 0, 1)
                for b in range(1, B):
                    transpose_probs(pe, A1, n, b, 0, Sb1)
                    transpose_probs(pe, A1, n, b, 1, Sb1)
                    if last and b >= 2:
                        tail(2 * b - 3)
                    output1(g, b - 1, 0)
                    transpose_probs(pe, A1, n, b, 2, Sb1)
                    values1(g, b, 0)
                    output1(g, b - 1, 1)
                    if last and b >= 2:
                        tail(2 * b - 2)
                    values1(g, b, 1)
                    if b == 1:
                        scores1(g, 3)
                        if last:
                            tail(0)
                if last:
                    tail(5)
                output1(g, B - 1, 0)
                if last:
                    tail(6)
                output1(g, B - 1, 1)
                if last:
                    tail(*range(7, TAIL_SLOTS))

            def tail(*slots):
                for what, t, i, _, before in tail_steps(slots):
                    if what == "turn":
                        pe.wait_ge(xn_ready, SCALED["scale3", t])
                        pe.wait_ge(A1["scores_read"], 3 * B * NKV)
                        ringF.wait_free(pe, i)
                        for c in range(KC):
                            last_ = nc.tensor.matmul(ringF.bank(i)[:, 0:P], X[:, t, c * P:(c + 1) * P], ident[:],
                                                     start=(c == 0), stop=(c == KC - 1))
                        ringF.filled(last_, i)
                    elif what == "codes":
                        pe.wait_ge(codes_ready, 1)
                        ringF.wait_read(pe, before)
                        ringF.wait_free(pe, i)
                        nc.tensor.matmul(ringF.bank(i)[:], FTh[:, t % 2, :], codes_f[:], start=True, stop=False)
                        ringF.filled(nc.tensor.matmul(ringF.bank(i)[:], FTl[:, t % 2, :], codes_f[:],
                                                      start=False, stop=True), i)

            ringC.wait_done(pe, POST_USES)
            group(0, False)
            with pe.Fori(1, NKV - 1) as g:
                group(g, False)
            group(NKV - 1, True)


_INS = ["L0_attn_x", "L0_attn_Wq", "L0_attn_bq", "L0_attn_Wk", "L0_attn_bk", "L0_attn_Wv", "L0_attn_bv",
        "L0_attn_Wo", "L0_attn_bo", "L0_ffn_q_scales", "L0_ffn_q_vals", "L0_ffn_bias", "L1_attn_w_qkv",
        "L1_attn_w_o", "L1_ffn_kernel"]


def kernel(**inputs):
    import numpy as _np
    import concourse.bacc as _bacc
    from concourse import mybir as _mybir
    from concourse.bass_utils import run_bass_kernel_spmd as _run

    nc = _bacc.Bacc("TRN2", target_bir_lowering=False, num_devices=1)
    arrays, args = {}, []

    def feed(name, a):
        arrays[name] = a
        args.append(nc.dram_tensor(name, a.shape, _mybir.dt.from_np(a.dtype), kind="ExternalInput").ap())

    for name in _INS:
        a = _np.ascontiguousarray(inputs[name])
        feed(f"in_{name}_dram", a.view(_np.int32) if a.dtype == _np.int8 else a)
    q = _np.arange(P)[:, None]
    rel = _np.concatenate([q - _np.arange(P)[None, :], q + P - _np.arange(S)[None, :]], axis=1)
    feed("identity", _np.eye(P, dtype=_np.float32))
    feed("mask_const", _np.where(rel >= 0, 0.0, -1e30).astype(_np.float32))
    feed("dist_const", _np.where(rel >= 0, -_np.sqrt(_np.maximum(rel, 0)) / SCALE1, -1e30).astype(_np.float32))
    slopes = (2.0 ** (-8.0 / (NKV * GRP))) ** _np.arange(1, NKV * GRP + 1, dtype=_np.float32)
    feed("slopes_const", _np.ascontiguousarray(_np.broadcast_to(slopes.astype(_np.float32), (P, NKV * GRP))))
    args.append(nc.dram_tensor("out_0_dram", (B, S, DM), _mybir.dt.float32, kind="ExternalOutput").ap())
    two_layers(nc, *args)
    r = _run(nc, [arrays], core_ids=[0])
    return r.results[0]["out_0_dram"]
```
